# Optimizing a Trainium2 kernel written in Bass

```python
import numpy as np
import jax
import jax.numpy as jnp

def _softmax(x, axis=-1):
    return jax.nn.softmax(x, axis=axis)

def _gelu(x):
    return jax.nn.gelu(x, approximate=True)

def _silu(x):
    return jax.nn.silu(x)

def _sigmoid(x):
    return jax.nn.sigmoid(x)

def _layernorm(x, axis=-1, eps=1e-05):
    m = jnp.mean(x, axis=axis, keepdims=True)
    v = jnp.var(x, axis=axis, keepdims=True)
    return (x - m) / jnp.sqrt(v + eps)

def _scatter_add(tgt, idx, src, axis=0):
    return tgt.at[idx].add(src)

def _segment_sum(src, seg, n):
    return jax.ops.segment_sum(src, seg, n)
kernel_name = 'mk_gps_d1_gnn_r8_7016b1'

def setup_inputs(seed: int=0):
    np.random.seed(seed)
    _w = jnp.asarray

    def _rec_inputs():
        import jax
        import jax.numpy as jnp
        _gk = jax.random.key(seed)
        x = -0.0003713 + 1 * jax.random.normal(jax.random.fold_in(_gk, 1), (6250, 256), jnp.float32)
        src = jax.random.randint(jax.random.fold_in(_gk, 2), (200000,), 0, 6250, jnp.int32)
        dst = jnp.minimum((6250 * jax.random.uniform(jax.random.fold_in(_gk, 3), (200000,)) ** 2.0).astype(jnp.int32), 49999)
        _o = jnp.argsort(dst, stable=True)
        src = src[_o]
        dst = dst[_o]
        return (x, src, dst)
    x, src, dst = _rec_inputs()

    def _L0_gnn_setup():
        import jax, jax.numpy as jnp
        import numpy as np
        N, E, D, L = (6250, 200000, 256, 3)
        EPS = 1e-05
        key = jax.random.key(seed)
        ks = jax.random.split(key, 10)
        x = jax.random.normal(ks[0], (N, D), dtype=jnp.float32)
        edge_index = jax.random.randint(ks[1], (2, E), 0, N, dtype=jnp.int32)
        mask_embed = jax.random.normal(ks[2], (D,), dtype=jnp.float32)
        s = 1.0 / np.sqrt(D)
        Wl = jax.random.normal(ks[3], (L, D, D), dtype=jnp.float32) * s
        Wr = jax.random.normal(ks[4], (L, D, D), dtype=jnp.float32) * s
        b = jax.random.normal(ks[5], (L, D), dtype=jnp.float32) * 0.01
        gamma = 1.0 + 0.1 * jax.random.normal(ks[6], (L, D), dtype=jnp.float32)
        beta = 0.1 * jax.random.normal(ks[7], (L, D), dtype=jnp.float32)
        rmean = 0.1 * jax.random.normal(ks[8], (L, D), dtype=jnp.float32)
        rvar = 0.5 + jax.random.uniform(ks[9], (L, D), dtype=jnp.float32)
        return {'x': x, 'edge_index': edge_index, 'mask_embed': mask_embed, 'Wl': Wl, 'Wr': Wr, 'b': b, 'gamma': gamma, 'beta': beta, 'rmean': rmean, 'rvar': rvar}
    _L0_gnn_all = _L0_gnn_setup()
    _L0_gnn_in = {k: v for k, v in _L0_gnn_all.items() if k in ('mask_embed', 'Wl', 'Wr', 'b', 'gamma', 'beta', 'rmean', 'rvar')}
    del _L0_gnn_all

    def _L0_mix_setup():
        import jax, jax.numpy as jnp
        import numpy as np
        import math
        EMBED = 256
        HEADS = 4
        HEAD_DIM = EMBED // HEADS
        OUT_DIM = 256
        LN_EPS = 1e-05

        def _qkv_init(key):
            spread = math.sqrt(3.0 / EMBED)
            gain, delta = (0.01, 0.01)
            w = jax.random.uniform(key, (EMBED, EMBED), minval=-spread, maxval=spread) * gain
            return w + delta * jnp.eye(EMBED, dtype=w.dtype)

        def _layer_norm(x, g, b):
            mu = jnp.mean(x, axis=-1, keepdims=True)
            var = jnp.mean(jnp.square(x - mu), axis=-1, keepdims=True)
            return (x - mu) * jax.lax.rsqrt(var + LN_EPS) * g + b

        def _split_heads(x, B, S):
            return x.reshape(B, S, HEADS, HEAD_DIM).transpose(0, 2, 1, 3)
        key = jax.random.key(seed)
        ks = jax.random.split(key, 6)
        seq = jax.random.normal(ks[0], (4, 1024, EMBED), dtype=jnp.float32)
        wq = _qkv_init(ks[1])
        wk = _qkv_init(ks[2])
        wv = _qkv_init(ks[3])
        bound = 1.0 / math.sqrt(EMBED)
        wo = jax.random.uniform(ks[4], (OUT_DIM, EMBED), minval=-bound, maxval=bound)
        bo = jax.random.uniform(ks[5], (OUT_DIM,), minval=-bound, maxval=bound)
        ln_k_g = jnp.ones((HEAD_DIM,), jnp.float32)
        ln_k_b = jnp.zeros((HEAD_DIM,), jnp.float32)
        ln_v_g = jnp.ones((HEAD_DIM,), jnp.float32)
        ln_v_b = jnp.zeros((HEAD_DIM,), jnp.float32)
        return {'seq': seq, 'wq': wq, 'wk': wk, 'wv': wv, 'wo': wo, 'bo': bo, 'ln_k_g': ln_k_g, 'ln_k_b': ln_k_b, 'ln_v_g': ln_v_g, 'ln_v_b': ln_v_b}
    _L0_mix_all = _L0_mix_setup()
    _L0_mix_in = {k: v for k, v in _L0_mix_all.items() if k in ('wq', 'wk', 'wv', 'wo', 'bo', 'ln_k_g', 'ln_k_b', 'ln_v_g', 'ln_v_b')}
    del _L0_mix_all

    def _L0_ffn_setup():
        import jax, jax.numpy as jnp
        import numpy as np
        B, S, H, F, E, K = (8, 512, 256, 512, 16, 2)
        EPS = 1e-05
        key = jax.random.key(seed)
        ks = jax.random.split(key, 9)
        sc = 0.02
        return {'x': jax.random.normal(ks[0], (B, S, H), dtype=jnp.float32), 'gate_w': jax.random.normal(ks[1], (H, E), dtype=jnp.float32) * sc, 'gate_b': jnp.zeros((E,), dtype=jnp.float32), 'w1': jax.random.normal(ks[2], (E, H, F), dtype=jnp.float32) * sc, 'b1': jnp.zeros((E, F), dtype=jnp.float32), 'w2': jax.random.normal(ks[3], (E, F, H), dtype=jnp.float32) * sc, 'b2': jnp.zeros((E, H), dtype=jnp.float32), 'gamma': jnp.ones((H,), dtype=jnp.float32), 'beta': jnp.zeros((H,), dtype=jnp.float32)}
    _L0_ffn_all = _L0_ffn_setup()
    _L0_ffn_in = {k: v for k, v in _L0_ffn_all.items() if k in ('gate_w', 'gate_b', 'w1', 'b1', 'w2', 'b2', 'gamma', 'beta')}
    del _L0_ffn_all
    return {'x': x, 'src': src, 'dst': dst, 'L0_gnn_mask_embed': _L0_gnn_in['mask_embed'], 'L0_gnn_Wl': _L0_gnn_in['Wl'], 'L0_gnn_Wr': _L0_gnn_in['Wr'], 'L0_gnn_b': _L0_gnn_in['b'], 'L0_gnn_gamma': _L0_gnn_in['gamma'], 'L0_gnn_beta': _L0_gnn_in['beta'], 'L0_gnn_rmean': _L0_gnn_in['rmean'], 'L0_gnn_rvar': _L0_gnn_in['rvar'], 'L0_mix_wq': _L0_mix_in['wq'], 'L0_mix_wk': _L0_mix_in['wk'], 'L0_mix_wv': _L0_mix_in['wv'], 'L0_mix_wo': _L0_mix_in['wo'], 'L0_mix_bo': _L0_mix_in['bo'], 'L0_mix_ln_k_g': _L0_mix_in['ln_k_g'], 'L0_mix_ln_k_b': _L0_mix_in['ln_k_b'], 'L0_mix_ln_v_g': _L0_mix_in['ln_v_g'], 'L0_mix_ln_v_b': _L0_mix_in['ln_v_b'], 'L0_ffn_gate_w': _L0_ffn_in['gate_w'], 'L0_ffn_gate_b': _L0_ffn_in['gate_b'], 'L0_ffn_w1': _L0_ffn_in['w1'], 'L0_ffn_b1': _L0_ffn_in['b1'], 'L0_ffn_w2': _L0_ffn_in['w2'], 'L0_ffn_b2': _L0_ffn_in['b2'], 'L0_ffn_gamma': _L0_ffn_in['gamma'], 'L0_ffn_beta': _L0_ffn_in['beta']}

def reference(x, src, dst, L0_gnn_mask_embed, L0_gnn_Wl, L0_gnn_Wr, L0_gnn_b, L0_gnn_gamma, L0_gnn_beta, L0_gnn_rmean, L0_gnn_rvar, L0_mix_wq, L0_mix_wk, L0_mix_wv, L0_mix_wo, L0_mix_bo, L0_mix_ln_k_g, L0_mix_ln_k_b, L0_mix_ln_v_g, L0_mix_ln_v_b, L0_ffn_gate_w, L0_ffn_gate_b, L0_ffn_w1, L0_ffn_b1, L0_ffn_w2, L0_ffn_b2, L0_ffn_gamma, L0_ffn_beta):
    import jax
    import jax.numpy as jnp

    def _L0_gnn_ref(x, edge_index, mask_embed, Wl, Wr, b, gamma, beta, rmean, rvar):
        import jax, jax.numpy as jnp
        import numpy as np
        N, E, D, L = (6250, 200000, 256, 3)
        EPS = 1e-05
        src, dst = (edge_index[0], edge_index[1])
        h = x.at[0].set(mask_embed)
        deg = jax.ops.segment_sum(jnp.ones((src.shape[0],), h.dtype), dst, num_segments=N)
        deg = jnp.maximum(deg, 1.0)[:, None]
        for i in range(L):
            agg = jax.ops.segment_sum(h[src], dst, num_segments=N) / deg
            z = agg @ Wl[i] + b[i] + h @ Wr[i]
            z = (z - rmean[i]) * jax.lax.rsqrt(rvar[i] + EPS) * gamma[i] + beta[i]
            if i != L - 1:
                z = jax.nn.relu(z)
            z = z + h
            h = z
        return h

    def _L0_mix_ref(seq, wq, wk, wv, wo, bo, ln_k_g, ln_k_b, ln_v_g, ln_v_b):
        import jax, jax.numpy as jnp
        import numpy as np
        import math
        EMBED = 256
        HEADS = 4
        HEAD_DIM = EMBED // HEADS
        OUT_DIM = 256
        LN_EPS = 1e-05

        def _qkv_init(key):
            spread = math.sqrt(3.0 / EMBED)
            gain, delta = (0.01, 0.01)
            w = jax.random.uniform(key, (EMBED, EMBED), minval=-spread, maxval=spread) * gain
            return w + delta * jnp.eye(EMBED, dtype=w.dtype)

        def _layer_norm(x, g, b):
            mu = jnp.mean(x, axis=-1, keepdims=True)
            var = jnp.mean(jnp.square(x - mu), axis=-1, keepdims=True)
            return (x - mu) * jax.lax.rsqrt(var + LN_EPS) * g + b

        def _split_heads(x, B, S):
            return x.reshape(B, S, HEADS, HEAD_DIM).transpose(0, 2, 1, 3)
        B, S, _ = seq.shape
        q = _split_heads(seq @ wq.T, B, S)
        k = _split_heads(seq @ wk.T, B, S)
        v = _split_heads(seq @ wv.T, B, S)
        k = _layer_norm(k, ln_k_g, ln_k_b)
        v = _layer_norm(v, ln_v_g, ln_v_b)
        kv = jnp.einsum('bhsd,bhse->bhde', k, v) / S
        ga = jnp.einsum('bhsd,bhde->bhse', q, kv)
        ga = ga.transpose(0, 2, 1, 3).reshape(B, S, EMBED)
        return ga @ wo.T + bo

    def _L0_ffn_ref(x, gate_w, gate_b, w1, b1, w2, b2, gamma, beta):
        import jax, jax.numpy as jnp
        import numpy as np
        B, S, H, F, E, K = (8, 512, 256, 512, 16, 2)
        EPS = 1e-05
        gate_logits = x @ gate_w + gate_b
        topk_vals, topk_idx = jax.lax.top_k(gate_logits, K)
        topk_w = jax.nn.softmax(topk_vals, axis=-1)
        h = jax.nn.relu(jnp.einsum('bsh,ehf->bsef', x, w1) + b1)
        expert_out = jnp.einsum('bsef,efh->bseh', h, w2) + b2
        sel = jnp.take_along_axis(expert_out, topk_idx[:, :, :, None], axis=2)
        moe = jnp.sum(topk_w[..., None] * sel, axis=2)
        y = x + moe
        mu = jnp.mean(y, axis=-1, keepdims=True)
        var = jnp.var(y, axis=-1, keepdims=True)
        return (y - mu) / jnp.sqrt(var + EPS) * gamma + beta
    edge_index = jnp.stack([src, dst])
    xn = _layernorm(x, axis=-1)
    x = x + _L0_gnn_ref(xn, edge_index, L0_gnn_mask_embed, L0_gnn_Wl, L0_gnn_Wr, L0_gnn_b, L0_gnn_gamma, L0_gnn_beta, L0_gnn_rmean, L0_gnn_rvar) + _L0_mix_ref(xn[None], L0_mix_wq, L0_mix_wk, L0_mix_wv, L0_mix_wo, L0_mix_bo, L0_mix_ln_k_g, L0_mix_ln_k_b, L0_mix_ln_v_g, L0_mix_ln_v_b)[0]
    x = x + _L0_ffn_ref(_layernorm(x, axis=-1)[None], L0_ffn_gate_w, L0_ffn_gate_b, L0_ffn_w1, L0_ffn_b1, L0_ffn_w2, L0_ffn_b2, L0_ffn_gamma, L0_ffn_beta)[0]
    return x

_drawn_inputs = setup_inputs


def setup_inputs(seed=0):
    import zlib

    import numpy as np

    out = dict(_drawn_inputs(seed))
    spreads = {'L0_mix_ln_k_g': (1.0, 0.6),
     'L0_mix_ln_k_b': (0.0, 0.8),
     'L0_mix_ln_v_g': (1.0, 0.6),
     'L0_mix_ln_v_b': (0.0, 0.8),
     'L0_ffn_gate_b': (0.0, 0.477),
     'L0_ffn_b1': (0.0, 0.8),
     'L0_ffn_b2': (0.0, 0.473),
     'L0_ffn_gamma': (1.0, 0.2),
     'L0_ffn_beta': (0.0, 0.349)}
    factors = {'L0_gnn_mask_embed': 6.112,
     'L0_gnn_b': 8.0,
     'L0_mix_wq': 8.0,
     'L0_mix_wk': 8.0,
     'L0_mix_wv': 8.0,
     'L0_mix_wo': 8.0,
     'L0_mix_bo': 4.791,
     'L0_ffn_w1': 3.937,
     'L0_ffn_w2': 3.128}
    for name, (base, spread) in spreads.items():
        noise = np.random.default_rng([zlib.crc32(name.encode()), seed]).standard_normal(out[name].shape)
        drawn = base * np.exp(spread * noise) if base else spread * noise
        out[name] = jnp.asarray(drawn.astype(out[name].dtype))
    for name, factor in factors.items():
        out[name] = (out[name] * factor).astype(out[name].dtype)
    return out
```

```python
from contextlib import ExitStack, contextmanager

import concourse.bass as bass
from concourse import mybir

F32, F32R, BF16 = mybir.dt.float32, mybir.dt.float32r, mybir.dt.bfloat16
I32 = mybir.dt.int32
U32 = mybir.dt.uint32
ALU = mybir.AluOpType
ACT = mybir.ActivationFunctionType
X_AXIS = mybir.AxisListType.X

P = 128
N, D, EDGES, LAYERS = 6250, 256, 200000, 3
HALVES = D // P
TILES = -(-N // P)
FULL = TILES - 1
TAIL = N - FULL * P
EPS = 1e-5

CHUNK = 512
CHUNKS = N // CHUNK
PART_BITS, TILE_BITS, COL_BITS = 7, 6, 9
CELL_CHUNK = 1 << (PART_BITS + TILE_BITS + COL_BITS)
GROUP = 8
QUADS = 4
ECHUNKS = -(-EDGES // P)
ITERS = -(-ECHUNKS // (GROUP * QUADS))
ECOLS = ITERS * GROUP * QUADS
ETILES = -(-ECOLS // P)
DUMMY = (CHUNKS + 1) * CELL_CHUNK
CELLS = DUMMY + 2 * GROUP * P
TAG = 0x20000000
CREDIT = 1
EXACT = 4096

BATCHES = 12
SLOTS = 4
HEADS, HEAD = 4, 64
E, FF = 16, 512
XT = (2 * N + E * (P - 1)) // P


def batch_tiles(b):
    return (4 * b, 4 if b < BATCHES - 1 else TILES - 4 * (BATCHES - 1))


@contextmanager
def stage_semaphores(nc):
    taken = []

    def sem(name):
        taken.append(nc.alloc_semaphore(name))
        return taken[-1]

    yield sem
    nc.clear_and_free_semaphores(taken)
    nc.all_engine_barrier()


class Steps:

    def __init__(self, eng, sem):
        self.eng, self.sem, self.base, self.k, self.at = eng, sem, 0, 0, 0

    def loop(self, n, per):
        self.base, self.at, self.k = self.base + self.k, n * per, 0

    def end(self, per, times):
        assert self.k == per, (self.k, per)
        self.base, self.at, self.k = self.base + per * times, 0, 0

    def __call__(self, ins):
        self.k += 1
        ins.then_inc(self.sem, 1)
        self.eng.wait_ge(self.sem, self.at + (self.base + self.k))


def rows(ap):
    return ap[0:FULL * P, :].rearrange("(t p) w -> p t w", p=P)


def index_stage(nc, mem, src, dst):
    with ExitStack() as ctx:
        sb = lambda n, s, d: ctx.enter_context(nc.sbuf_tensor(n, s, d))
        sem = ctx.enter_context(stage_semaphores(nc))
        s_sb, d_sb = sb("src_rows", [P, ETILES, P], I32), sb("dst_rows", [P, ETILES, P], I32)
        a2, a3 = sb("cell_tile", [P, ETILES, P], I32), sb("cell_chunk", [P, ETILES, P], I32)
        cleared, loaded, own, cells_ready = sem("edges_cleared"), sem("edges_loaded"), sem("index_own"), sem("cells_ready")
        stored, flipped, const_in, zeroed = sem("cells_stored"), sem("cells_flipped"), sem("const_in"), sem("zero_tile_set")
        x_in, moved, pool_set = sem("x_in"), sem("x_pad_set"), sem("pool_set")
        full = EDGES // (P * P)
        rest = EDGES - full * P * P
        rrows, rcols = rest // P, rest % P
        with nc.Block() as block:
            @block.sync
            def _(sp):
                sp.dma_start(mem.cf[:], mem.cf_dram).then_inc(const_in, 16)
                sp.dma_start(mem.ci[:], mem.ci_dram).then_inc(const_in, 16)
                sp.wait_ge(cleared, 2)
                for t, a in ((s_sb, src), (d_sb, dst)):
                    sp.dma_start(t[:, 0:full, :], a[0:full * P * P].rearrange("(i q p) -> q i p", q=P, p=P)).then_inc(loaded, 16)
                    sp.dma_start(t[0:rrows, full, :], a[full * P * P:full * P * P + rrows * P].rearrange("(q p) -> q p", p=P)).then_inc(loaded, 16)
                    sp.dma_start(t[rrows:rrows + 1, full, 0:rcols], a[EDGES - rcols:EDGES].rearrange("(q p) -> q p", q=1)).then_inc(loaded, 16)
                sp.wait_ge(moved, 1)
                for k in range(4):
                    m = FULL // 4
                    sp.dma_start(mem.xk[:, k * m:(k + 1) * m, :], rows(mem.x)[:, k * m:(k + 1) * m, :]).then_inc(x_in, 16)
                sp.dma_start(mem.xk[0:TAIL, FULL, :], mem.x[FULL * P:N, :]).then_inc(x_in, 16)
                sp.wait_ge(cells_ready, 1)
                store = mem.cells_dram.rearrange("(i q p) -> q i p", q=P, p=P)
                sp.dma_start(store, s_sb[:]).then_inc(stored, 16)
                sp.wait_ge(stored, 16)
                sp.wait_ge(x_in, 80)

            @block.scalar
            def _(act):
                act.wait_ge(zeroed, 1)
                for c in range(CHUNKS):
                    dest = mem.counts[c * CELL_CHUNK:(c + 1) * CELL_CHUNK].rearrange("(p s) -> p s", p=P)
                    act.dma_start(dest[:, 0:TILES * CHUNK].rearrange("p (r m) -> p r m", r=7),
                                  mem.zeros[:].rearrange("p (r m) -> p r m", r=1).to_broadcast([P, 7, 7 * CHUNK])).then_inc(mem.counts_zeroed, 16)
                dest = mem.counts[CHUNKS * CELL_CHUNK:(CHUNKS + 1) * CELL_CHUNK].rearrange("(p s j) -> p s j", p=P, j=CHUNK)
                act.dma_start(dest[:, 0:28, 0:P], mem.zeros[:].rearrange("p (s j) -> p s j", j=P)).then_inc(mem.counts_zeroed, 16)
                act.dma_start(dest[:, 28:TILES, 0:P], mem.zeros[:, 0:21 * P].rearrange("p (s j) -> p s j", j=P)).then_inc(mem.counts_zeroed, 16)
                act.dma_start(mem.counts[DUMMY:DUMMY + 2 * GROUP * P].rearrange("(p s) -> p s", p=P), mem.zeros[:, 0:2 * GROUP]).then_inc(mem.counts_zeroed, 16)

            @block.gpsimd
            def _(pool):
                nc.gpsimd.memset(mem.zeros[:], 0.0).then_inc(zeroed, 1)
                nc.gpsimd.memset(mem.minus_half[:], -0.5)
                nc.gpsimd.memset(mem.xk[:, FULL, :], 0.0).then_inc(moved, 1)

            @block.vector
            def _(dve):
                step = Steps(dve, own)
                nc.vector.memset(s_sb[:, full, :], 0).then_inc(cleared, 1)
                nc.vector.memset(d_sb[:, full, :], 0).then_inc(cleared, 1)
                dve.wait_ge(const_in, 32)
                dve.wait_ge(loaded, 96)
                nc.vector.tensor_scalar(a2[:], s_sb[:], PART_BITS, COL_BITS, ALU.logical_shift_right, ALU.logical_shift_left)
                nc.vector.tensor_scalar(a3[:], d_sb[:], COL_BITS, PART_BITS + TILE_BITS + COL_BITS, ALU.logical_shift_right, ALU.logical_shift_left)
                nc.vector.tensor_scalar(d_sb[:], d_sb[:], CHUNK - 1, TAG, ALU.bitwise_and, ALU.bitwise_or)
                step(nc.vector.tensor_scalar(s_sb[:], s_sb[:], P - 1, TILE_BITS + COL_BITS, ALU.bitwise_and, ALU.logical_shift_left))
                step(nc.vector.tensor_tensor(a2[:], a2[:], a3[:], ALU.bitwise_or))
                step(nc.vector.tensor_tensor(a2[:], a2[:], d_sb[:], ALU.bitwise_or))
                step(nc.vector.tensor_tensor(s_sb[:], s_sb[:], a2[:], ALU.bitwise_or))
                step(nc.vector.tensor_tensor(s_sb[:, full, :], s_sb[:, full, :], mem.pad_and, ALU.bitwise_and))
                nc.vector.tensor_tensor(s_sb[:, full, :], s_sb[:, full, :], mem.pad_or, ALU.bitwise_or).then_inc(cells_ready, 1)
                for i in range(ETILES):
                    if i % 4 == 0:
                        dve.wait_ge(flipped, i // 4 + 1)
                    nc.vector.tensor_scalar(mem.cell_col[:, i * P:(i + 1) * P], mem.bank[i // 4][:, (i % 4) * P:(i % 4 + 1) * P].bitcast(I32),
                                            TAG, None, ALU.bitwise_xor)

            @block.tensor
            def _(pe):
                pe.wait_ge(cells_ready, 1)
                for i in range(ETILES):
                    last = nc.tensor.transpose(mem.bank[i // 4][:, (i % 4) * P:(i % 4 + 1) * P], s_sb[:, i, :].bitcast(F32), mem.ident)
                    if i % 4 == 3 or i == ETILES - 1:
                        last.then_inc(flipped, 1)


def mix_stage(nc, mem, w):
    with ExitStack() as ctx:
        sb = lambda n, s, d: ctx.enter_context(nc.sbuf_tensor(n, s, d))
        sem = ctx.enter_context(stage_semaphores(nc))
        bank, h, xk, ident = mem.bank, mem.h, mem.xk, mem.ident
        raw = [sb(f"raw_{n}", [P, HALVES, D], F32) for n in ("wk", "wv", "wo")]
        wq = sb("wq_sb", [P, HALVES, D], F32)
        wkv, woT = sb("wkv", [P, HALVES, 2 * D], F32), sb("woT", [P, HALVES, D], F32)
        gain, shift = sb("kv_gain", [P, 2, HEADS, HEAD], F32), sb("kv_shift", [P, 2, HEADS, HEAD], F32)
        bo_b = sb("bo_b", [P, D], F32)
        stats = sb("ln_stats", [P, TILES, 6], F32)
        mean, rstd, tmp = sb("ln_mean", [P, TILES], F32), sb("ln_rstd", [P, TILES], F32), sb("ln_tmp", [P, TILES], F32)
        xs_out = sb("xs_out", [P, 2, D], F32)
        xs, xT = sb("xs", [P, 2, D], F32), sb("xT", [P, 2, HALVES, P], F32)
        cen, sq, kvn = sb("cen", [P, 2, 2 * D], F32), sb("sq", [P, 2, 2 * D], F32), sb("kvn", [P, 2, 2 * D], F32)
        hs = sb("head_stats", [P, 2, 3, 2 * HEADS], F32)
        kvb, tq, m_sb = sb("kv_blocks", [P, HALVES, P], F32), sb("kv_wo", [P, HALVES, D], F32), sb("mix_w", [P, HALVES, D], F32)
        w_in, b_in, own, wT, wTd = sem("mixw_in"), sem("mixb_in"), sem("mix_own"), sem("mixw_T"), sem("mixw_Td")
        xs_ready, xs_flipped, xT_ready, kv_ps, cen_ready, sq_ready = (sem(n) for n in ("xs_ready", "xs_flipped", "xT_ready", "kv_ps", "cen_ready", "sq_ready"))
        scaled, kvn_ready, kv_added, pool_own, zero_kv = (sem(n) for n in ("kv_scaled", "kvn_ready", "kv_added", "pool_own1", "zero_kv"))
        kvb_ready, tq_ps, tq_ready, m_ps, m_ready, act_h = (sem(n) for n in ("kvb_ready", "tq_ps", "tq_ready", "m_ps", "m_ready", "act_h"))
        stats_done = sem("stats_done")
        var_ready, rstd_ready, head_var, head_rstd = (sem(n) for n in ("var_ready", "rstd_ready", "head_var", "head_rstd"))
        mixed, mix_read, xs2, fl2, xt2 = (sem(n) for n in ("mixed", "mix_read", "xs_again", "xs_flipped_again", "xT_again"))

        with nc.Block() as block:
            @block.sync
            def _(sp):
                for t, n in zip(raw + [wq], ("wk", "wv", "wo", "wq")):
                    sp.dma_start(t[:], w[n].rearrange("(a p) d -> p a d", p=P)).then_inc(w_in, 16)
                for side, n in enumerate(("k", "v")):
                    for hd in range(HEADS):
                        sp.dma_start(gain[:, side, hd, :], w[f"ln_{n}_g"].partition_broadcast(P)).then_inc(b_in, 16)
                        sp.dma_start(shift[:, side, hd, :], w[f"ln_{n}_b"].partition_broadcast(P)).then_inc(b_in, 16)
                sp.dma_start(bo_b[:], w["bo"].partition_broadcast(P)).then_inc(b_in, 16)
                sp.wait_ge(b_in, 16 * 17)

            @block.tensor
            def _(pe):
                for s in (fl2, kv_added, xs_flipped):
                    pe.sem_inc(s, CREDIT)
                pe.wait_ge(w_in, 64)
                for i, t in enumerate(raw):
                    for a in range(HALVES):
                        for b in range(HALVES):
                            last = nc.tensor.transpose(bank[i][:, (b * HALVES + a) * P:(b * HALVES + a + 1) * P], t[:, a, b * P:(b + 1) * P], ident)
                    last.then_inc(wT, 1)

                def kv_tile(j, n):
                    pe.wait_ge(xs_ready, 2 * n + j + 1)
                    for a in range(HALVES):
                        last = nc.tensor.transpose(bank[3 + j][:, a * P:(a + 1) * P], xs[:, j, a * P:(a + 1) * P], ident)
                    last.then_inc(xs_flipped, 1)
                    pe.wait_ge(xT_ready, 2 * n + j + 1)
                    for a in range(HALVES):
                        last = nc.tensor.matmul(bank[5 + j][:, :], xT[:, j, a, :], wkv[:, a, :], start=(a == 0), stop=(a == HALVES - 1))
                    last.then_inc(kv_ps, 1)

                def kv_add(j, n, r=P, stop=False):
                    pe.wait_ge(kvn_ready, 2 * n + j + 1 + CREDIT)
                    for a in range(HALVES):
                        last = nc.tensor.matmul(bank[7][:, a * P:(a + 1) * P], kvn[0:r, j, D + a * P:D + (a + 1) * P],
                                                kvn[0:r, j, a * P:(a + 1) * P], start=False, stop=stop, skip_group_check=True)
                    last.then_inc(kv_added, 1)

                pe.wait_ge(zero_kv, 1)
                pe.wait_ge(wTd, 3)
                nc.tensor.matmul(bank[7][:, 0:D], kvn[:, 0, 0:P], kvn[:, 0, 0:D], start=True, stop=False, skip_group_check=True)
                with pe.Fori(0, FULL // 2) as n:
                    for j in range(2):
                        kv_tile(j, n)
                    for j in range(2):
                        kv_add(j, n)
                kv_tile(0, FULL // 2)
                kv_add(0, FULL // 2, r=TAIL, stop=True)
                pe.wait_ge(kvb_ready, 1)
                for a in range(HALVES):
                    last = nc.tensor.matmul(bank[a][:, 0:D], kvb[:, a, :], woT[:, a, :], start=True, stop=True)
                last.then_inc(tq_ps, 1)
                pe.wait_ge(tq_ready, 1)
                for i in range(HALVES):
                    for a in range(HALVES):
                        last = nc.tensor.matmul(bank[3 + i][:, 0:D], wq[:, a, i * P:(i + 1) * P], tq[:, a, :], start=(a == 0), stop=(a == HALVES - 1))
                last.then_inc(m_ps, 1)
                pe.wait_ge(m_ready, 1)

                def apply(j, n):
                    pe.wait_ge(xs2, 2 * n + j + 1)
                    for a in range(HALVES):
                        last = nc.tensor.transpose(bank[3 + j][:, a * P:(a + 1) * P], xs[:, j, a * P:(a + 1) * P], ident)
                    last.then_inc(fl2, 1)
                    pe.wait_ge(xt2, 2 * n + j + 1)
                    pe.wait_ge(mix_read, 2 * n + CREDIT)
                    for a in range(HALVES):
                        last = nc.tensor.matmul(bank[5 + j][:, 0:D], xT[:, j, a, :], m_sb[:, a, :], start=(a == 0), stop=(a == HALVES - 1))
                    last.then_inc(mixed, 1)

                with pe.Fori(0, FULL // 2) as n:
                    for j in range(2):
                        apply(j, n)
                apply(0, FULL // 2)

            @block.scalar
            def _(act):
                act.sem_inc(act_h, CREDIT)
                def flip_out(j, n):
                    act.wait_ge(xs_flipped, 2 * n + j + 1 + CREDIT)
                    nc.scalar.copy(xT[:, j, :, :].rearrange("p a b -> p (a b)"), bank[3 + j][:, 0:D]).then_inc(xT_ready, 1)

                def square(j, n):
                    act.wait_ge(cen_ready, 2 * n + j + 1)
                    nc.scalar.activation(sq[:, j, :], cen[:, j, :], ACT.Square).then_inc(sq_ready, 1)

                def keep(j, n, t):
                    act.wait_ge(xs_ready, 2 * n + j + 1)
                    nc.scalar.copy(h[:, t, :], xs[:, j, :]).then_inc(act_h, 1)

                with act.Fori(0, FULL // 2) as n:
                    for j in range(2):
                        keep(j, n, 2 * n + j)
                        flip_out(j, n)
                    for j in range(2):
                        square(j, n)
                keep(0, FULL // 2, FULL)
                flip_out(0, FULL // 2)
                square(0, FULL // 2)
                act.wait_ge(act_h, TILES + CREDIT)

                def again(j, n, t):
                    act.wait_ge(fl2, 2 * n + CREDIT)
                    nc.scalar.copy(xs[:, j, :], h[:, t, :]).then_inc(xs2, 1)

                def out(j, n):
                    act.wait_ge(fl2, 2 * n + j + 1 + CREDIT)
                    nc.scalar.copy(xT[:, j, :, :].rearrange("p a b -> p (a b)"), bank[3 + j][:, 0:D]).then_inc(xt2, 1)

                act.wait_ge(m_ready, 1)
                with act.Fori(0, FULL // 2) as n:
                    for j in range(2):
                        again(j, n, 2 * n + j)
                    for j in range(2):
                        out(j, n)
                again(0, FULL // 2, FULL)
                out(0, FULL // 2)

            @block.gpsimd
            def _(pool):
                pool.sem_inc(kvn_ready, CREDIT)
                nc.gpsimd.memset(kvn[:, 0, :], 0.0).then_inc(zero_kv, 1)
                nc.gpsimd.memset(kvb[:], 0.0).then_inc(zero_kv, 1)
                pool.wait_ge(b_in, 16 * 17)
                step = Steps(pool, pool_own)

                pool.wait_ge(var_ready, 1)
                power(nc, mem, rstd[:], TILES).then_inc(rstd_ready, 1)

                def head_power(j, n):
                    pool.wait_ge(head_var, 2 * n + j + 1)
                    power(nc, mem, hs[:, j, 1, :], 2 * HEADS).then_inc(head_rstd, 1)

                def affine(j, n):
                    pool.wait_ge(scaled, 2 * n + j + 1)
                    pool.wait_ge(kv_added, 2 * n + CREDIT)
                    step(nc.gpsimd.tensor_tensor(cen[:, j, :], cen[:, j, :], gain[:].rearrange("p s h d -> p (s h d)"), ALU.mult))
                    nc.gpsimd.tensor_tensor(kvn[:, j, :], cen[:, j, :], shift[:].rearrange("p s h d -> p (s h d)"), ALU.add).then_inc(kvn_ready, 1)

                with pool.Fori(0, FULL // 2) as n:
                    step.loop(n, 2)
                    for j in range(2):
                        head_power(j, n)
                    for j in range(2):
                        affine(j, n)
                step.end(2, FULL // 2)
                head_power(0, FULL // 2)
                affine(0, FULL // 2)

            @block.vector
            def _(dve):
                dve.sem_inc(mix_read, CREDIT)
                step = Steps(dve, own)
                with dve.Fori(0, TILES) as n:
                    nc.vector.bn_stats(stats[:, n, :], xk[:, n, :]).then_inc(stats_done, 1)
                dve.wait_ge(stats_done, TILES)
                ln_rows(nc, dve, step, stats, mean, rstd, tmp, var_ready, rstd_ready)
                for i in range(3):
                    dve.wait_ge(wT, i + 1)
                    dest = woT[:] if i == 2 else wkv[:, :, i * D:(i + 1) * D]
                    nc.vector.tensor_copy(dest, bank[i][:].rearrange("p (b c) -> p b c", b=HALVES)).then_inc(wTd, 1)

                def normalise(j, n, t):
                    dve.wait_ge(xs_flipped, 2 * n + CREDIT)
                    dve.wait_ge(act_h, 2 * n + CREDIT)
                    nc.vector.tensor_scalar(xs[:, j, :], xk[:, t, :], mean[:, bass.ds(t, 1)], rstd[:, bass.ds(t, 1)], ALU.subtract, ALU.mult).then_inc(xs_ready, 1)

                def heads(j, n):
                    dve.wait_ge(kv_ps, 2 * n + j + 1)
                    dve.wait_ge(kvn_ready, 2 * n + CREDIT)
                    k3 = bank[5 + j][:].rearrange("p (g d) -> p g d", d=HEAD)
                    c3, q3 = (t[:, j, :].rearrange("p (g d) -> p g d", d=HEAD) for t in (cen, sq))
                    wide = lambda v: v.rearrange("p (g o) -> p g o", o=1).to_broadcast([P, 2 * HEADS, HEAD])
                    step(nc.vector.tensor_reduce(hs[:, j, 0, :], k3, X_AXIS, ALU.add))
                    step(nc.vector.tensor_scalar(hs[:, j, 0, :], hs[:, j, 0, :], 1.0 / HEAD, None, ALU.mult))
                    nc.vector.tensor_tensor(c3, k3, wide(hs[:, j, 0, :]), ALU.subtract).then_inc(cen_ready, 1)

                def heads2(j, n):
                    c3, q3 = (t[:, j, :].rearrange("p (g d) -> p g d", d=HEAD) for t in (cen, sq))
                    wide = lambda v: v.rearrange("p (g o) -> p g o", o=1).to_broadcast([P, 2 * HEADS, HEAD])
                    dve.wait_ge(sq_ready, 2 * n + j + 1)
                    step(nc.vector.tensor_reduce(hs[:, j, 1, :], q3, X_AXIS, ALU.add))
                    nc.vector.tensor_scalar(hs[:, j, 1, :], hs[:, j, 1, :], 1.0 / HEAD, EPS, ALU.mult, ALU.add).then_inc(head_var, 1)

                def heads3(j, n):
                    c3 = cen[:, j, :].rearrange("p (g d) -> p g d", d=HEAD)
                    wide = lambda v: v.rearrange("p (g o) -> p g o", o=1).to_broadcast([P, 2 * HEADS, HEAD])
                    dve.wait_ge(head_rstd, 2 * n + j + 1)
                    nc.vector.tensor_tensor(c3, c3, wide(hs[:, j, 1, :]), ALU.mult).then_inc(scaled, 1)

                with dve.Fori(0, FULL // 2) as n:
                    step.loop(n, 6)
                    for j in range(2):
                        normalise(j, n, 2 * n + j)
                    for j in range(2):
                        heads(j, n)
                    for j in range(2):
                        heads2(j, n)
                    for j in range(2):
                        heads3(j, n)
                step.end(6, FULL // 2)
                normalise(0, FULL // 2, FULL)
                heads(0, FULL // 2)
                heads2(0, FULL // 2)
                heads3(0, FULL // 2)
                dve.wait_ge(kv_added, TILES + CREDIT)
                dve.wait_ge(zero_kv, 2)
                for a in range(HALVES):
                    for b in range(2):
                        r = slice(b * HEAD, (b + 1) * HEAD)
                        last = nc.vector.tensor_scalar(kvb[r, a, r], bank[7][r, a * P + b * HEAD:a * P + (b + 1) * HEAD], 1.0 / N, None, ALU.mult)
                last.then_inc(kvb_ready, 1)
                dve.wait_ge(tq_ps, 1)
                for a in range(HALVES):
                    last = nc.vector.tensor_copy(tq[:, a, :], bank[a][:, 0:D])
                last.then_inc(tq_ready, 1)
                dve.wait_ge(m_ps, 1)
                for a in range(HALVES):
                    last = nc.vector.tensor_copy(m_sb[:, a, :], bank[3 + a][:, 0:D])
                last.then_inc(m_ready, 1)
                dve.wait_ge(b_in, 16 * 17)

                def finish(j, n, t):
                    dve.wait_ge(mixed, 2 * n + j + 1)
                    nc.vector.tensor_tensor(xs_out[:, j, :], bank[5 + j][:, 0:D], bo_b[:], ALU.add).then_inc(mix_read, 1)
                    dve.wait_ge(mix_read, 2 * n + j + 1 + CREDIT)
                    nc.vector.tensor_tensor(xk[:, t, :], xs_out[:, j, :], xk[:, t, :], ALU.add)

                with dve.Fori(0, FULL // 2) as n:
                    for j in range(2):
                        finish(j, n, 2 * n + j)
                finish(0, FULL // 2, FULL)


def ln_rows(nc, dve, step, stats, mean, rstd, tmp, var_ready, rstd_ready, width=D):
    m_e, m_o, v_e, v_o = (stats[:, :, k] for k in (1, 4, 2, 5))
    step(nc.vector.tensor_tensor(mean[:], m_e, m_o, ALU.add))
    step(nc.vector.tensor_tensor(tmp[:], m_e, m_o, ALU.subtract))
    step(nc.vector.tensor_scalar(mean[:], mean[:], 0.5, None, ALU.mult))
    step(nc.vector.tensor_tensor(tmp[:], tmp[:], tmp[:], ALU.mult))
    step(nc.vector.tensor_tensor(rstd[:], v_e, v_o, ALU.add))
    step(nc.vector.tensor_scalar(tmp[:], tmp[:], 0.25, EPS, ALU.mult, ALU.add))
    nc.vector.scalar_tensor_tensor(out=rstd[:], in0=rstd[:], scalar=1.0 / width, in1=tmp[:], op0=ALU.mult, op1=ALU.add).then_inc(var_ready, 1)
    dve.wait_ge(rstd_ready, 1)


def power(nc, mem, ap, width):
    return nc.gpsimd.tensor_tensor(ap, ap, mem.minus_half[:].to_broadcast([P, width]), ALU.pow)


def scatter_stage(nc, mem):
    with ExitStack() as ctx:
        sb = lambda n, s, d: ctx.enter_context(nc.sbuf_tensor(n, s, d))
        sem = ctx.enter_context(stage_semaphores(nc))
        bank = mem.bank
        key_rows, key_bits = sb("key_rows", [P, GROUP * P], I32), sb("key_bits", [P, GROUP * P], BF16)
        masked = sb("key_masked", [P, GROUP * P], I32)
        dup_f, dup_in = sb("dup_mask_f", [P, GROUP * P], F32), sem("dup_mask_in")
        dup_mask = sb("dup_mask", [P, GROUP * P], BF16)
        equal = sb("equal", [P, 4, GROUP * P], BF16)
        value = sb("cell_value", [P, QUADS, GROUP], F32)
        earlier, is_dup = sb("earlier", [P, QUADS, GROUP], F32), sb("is_dup", [P, QUADS, GROUP], I32)
        cell = sb("cell_slot", [P, QUADS, GROUP], I32)
        lane, tile_no, bits_a, bits_b = (sb(n, [P, ETILES * P], F32 if n[:1] == "d" else I32) for n in ("dst_lane", "dst_tile", "bits_a", "bits_b"))
        iota = sb("iota_f", [P, P], F32)
        hot_lane, hot_tile = sb("hot_lane", [P, QUADS, GROUP, P], BF16), sb("hot_tile", [P, QUADS, GROUP, TILES], BF16)
        bias15 = sb("bias15", [P, 1], F32)
        keys_in, bits_ready, own, cleared = sem("keys_in"), sem("bits_ready"), sem("scatter_own"), sem("hot_cleared")
        dots, equals, dups, cells_set, retired, hots, hots_used = (
            sem(n) for n in ("dots", "equals", "dups", "cells_set", "groups_retired", "hots", "hots_used"))
        own_turns, own_turns_pool = sem("own_turns"), sem("own_turns_pool")
        scattered, deg_done, masked_done, xm_out = sem("scattered"), sem("deg_done"), sem("masked_done"), sem("xm_out")
        GQ = GROUP * QUADS
        pair = lambda k: mem.psum[:, 2 * (k % 2) * 512:(2 * (k % 2) + 2) * 512]
        deg_ps = bank[4][:, 0:TILES]

        with nc.Block() as block:
            @block.sync
            def _(sp):
                rows4 = mem.cells_dram[0:ITERS * GQ * P].rearrange("(n q m) -> n q m", q=QUADS, m=GROUP * P)
                sp.dma_start(dup_f[:], mem.dup_mask_dram).then_inc(dup_in, 16)
                sp.dma_start(rows(mem.xm_dram), mem.xk[:, 0:FULL, :]).then_inc(xm_out, 16)
                sp.dma_start(mem.xm_dram[FULL * P:N, :], mem.xk[0:TAIL, FULL, :]).then_inc(xm_out, 16)
                sp.dma_start(mem.h[0:1, 0, :], mem.mask_embed.rearrange("(o d) -> o d", o=1)).then_inc(xm_out, 16)
                slots = mem.slot_rows.rearrange("(p t) d -> p (t d)", p=P)
                whole = XT * D // (7 * CHUNK)
                sp.dma_start(slots[:, 0:whole * 7 * CHUNK].rearrange("p (r m) -> p r m", r=whole),
                             mem.zeros[:].rearrange("p (r m) -> p r m", r=1).to_broadcast([P, whole, 7 * CHUNK])).then_inc(xm_out, 16)
                sp.dma_start(slots[:, whole * 7 * CHUNK:], mem.zeros[:, 0:XT * D - whole * 7 * CHUNK]).then_inc(xm_out, 16)
                with sp.Fori(0, ITERS) as n:
                    sp.wait_ge(masked_done, n + CREDIT)
                    for q in range(QUADS):
                        sp.dma_start(key_rows[32 * q:32 * q + 32, :], rows4[n][q].partition_broadcast(32)).then_inc(keys_in, 16)
                sp.wait_ge(xm_out, 16 * 5)

            @block.gpsimd
            def _(pool):
                pool.wait_ge(mem.counts_zeroed, 16 * (CHUNKS + 3))
                with pool.Fori(0, ITERS) as n:
                    for q in range(QUADS):
                        pool.wait_ge(cells_set, QUADS * n + q + 1)
                        pool.sem_inc(own_turns_pool, 1)
                        for i in range(GROUP):
                            pool.indirect_dma_start(out=mem.counts_2d, out_offset=bass.IndirectOffsetOnAxis(ap=cell[:, q, i:i + 1], axis=0),
                                                    in_=value[:, q, i:i + 1], in_offset=None, compute_op=ALU.add).then_inc(scattered, 16)
                        pool.wait_ge(scattered, 16 * GROUP * (QUADS * n + q + 1))
                        pool.sem_inc(retired, 1)

            @block.tensor
            def _(pe):
                pe.sem_inc(dots, CREDIT)
                pe.sem_inc(hots_used, CREDIT)
                pe.wait_ge(cleared, 5)
                nc.tensor.matmul(deg_ps, hot_lane[:, 2, 0, :], hot_tile[:, 2, 0, :], start=True, stop=False, skip_group_check=True)

                def degrees(q):
                    for i in range(GROUP):
                        last = nc.tensor.matmul(deg_ps, hot_lane[:, q, i, :], hot_tile[:, q, i, :], start=False, stop=False, skip_group_check=True)
                    last.then_inc(hots_used, 1)

                with pe.Fori(0, ITERS) as n:
                    pe.wait_ge(bits_ready, n + 1)
                    for q in range(QUADS):
                        for i in range(GROUP):
                            k = GROUP * q + i
                            pe.wait_ge(equals, GQ * n + k + 1)
                            qs = slice(32 * q, 32 * q + 32)
                            for b in range(2):
                                last = nc.tensor.matmul(pair(k)[:, b * 512:(b + 1) * 512], key_bits[qs, i * P:(i + 1) * P],
                                                        key_bits[qs, b * 512:(b + 1) * 512], start=True, stop=True)
                            last.then_inc(dots, 1)
                        pe.wait_ge(hots, QUADS * n + q + 1)
                        degrees((q + 2) % QUADS)
                pe.wait_ge(hots, QUADS * ITERS + 1)
                degrees(2)
                pe.wait_ge(hots, QUADS * ITERS + 2)
                degrees(3)
                nc.tensor.matmul(deg_ps, hot_lane[:, 3, 0, :], mem.zero_bf[:, 0:TILES], start=False, stop=True, skip_group_check=True).then_inc(deg_done, 1)

            @block.scalar
            def _(act):
                act.sem_inc(equals, 2)
                act.wait_ge(cleared, 5)
                with act.Fori(0, ITERS) as n:
                    for q in range(QUADS):
                        act.wait_ge(retired, QUADS * n + q + 1)
                        for i in range(GROUP):
                            k = GROUP * q + i
                            act.wait_ge(dots, GQ * n + k + 1 + CREDIT)
                            act.wait_ge(dups, GQ * n + k + 1)
                            nc.scalar.activation(equal[:, k % 4, :], pair(k), ACT.Relu, bias=bias15[:], scale=2.0,
                                                 accum_out=value[:, q, i:i + 1]).then_inc(equals, 1)

            @block.vector
            def _(dve):
                step = Steps(dve, own)
                dve.sem_inc(dups, 4)
                dve.sem_inc(retired, 4)
                dve.sem_inc(masked_done, CREDIT)
                dve.sem_inc(hots, 2)
                nc.vector.memset(hot_lane[:, 2:4], 0.0).then_inc(cleared, 1)
                nc.vector.memset(hot_tile[:, 2:4], 0.0).then_inc(cleared, 1)
                nc.vector.memset(mem.zero_bf[:], 0.0).then_inc(cleared, 1)
                nc.vector.memset(bias15[:], -15.0).then_inc(cleared, 1)
                step(nc.vector.tensor_copy(iota[:], mem.iota))
                dve.wait_ge(dup_in, 16)
                nc.vector.tensor_copy(dup_mask[:], dup_f[:]).then_inc(cleared, 1)
                cc = mem.cell_col
                nc.vector.tensor_scalar(bits_b[:], cc[:], PART_BITS, 3, ALU.logical_shift_right, ALU.bitwise_and)
                step(nc.vector.tensor_scalar(bits_a[:], cc[:], PART_BITS + TILE_BITS + COL_BITS, 2, ALU.logical_shift_right, ALU.logical_shift_left))
                step(nc.vector.tensor_tensor(bits_a[:], bits_a[:], bits_b[:], ALU.bitwise_or))
                step(nc.vector.tensor_copy(tile_no[:], bits_a[:]))
                step(nc.vector.tensor_scalar(bits_b[:], cc[:], P - 1, None, ALU.bitwise_and))
                step(nc.vector.tensor_copy(lane[:], bits_b[:]))
                with dve.Fori(0, ITERS) as n:
                    step.loop(n, QUADS)
                    dve.wait_ge(keys_in, 64 * n + 64)
                    nc.vector.tensor_tensor(masked[:], key_rows[:], mem.bit_mask.to_broadcast([P, GROUP * P]), ALU.bitwise_and).then_inc(masked_done, 1)
                    dve.wait_ge(masked_done, n + 1 + CREDIT)
                    dve.wait_ge(dots, GQ * n + CREDIT)
                    nc.vector.tensor_scalar(key_bits[:], masked[:], 0.0, 0.5, ALU.not_equal, ALU.subtract).then_inc(bits_ready, 1)
                    for q in range(QUADS):
                        for i in range(GROUP):
                            k = GROUP * q + i
                            dve.wait_ge(equals, GQ * n + k + 3)
                            nc.vector.scalar_tensor_tensor(out=equal[:, k % 4, 0:(i + 1) * P], in0=equal[:, k % 4, 0:(i + 1) * P], scalar=1.0,
                                                           in1=dup_mask[:, (GROUP - 1 - i) * P:], op0=ALU.mult, op1=ALU.mult,
                                                           accum_out=earlier[:, q, i:i + 1]).then_inc(dups, 1)
                        cols = bass.ds(n * GQ + q * GROUP, GROUP)
                        dve.wait_ge(hots_used, QUADS * n + q + CREDIT)
                        flat = lambda t, m: t[:, cols].rearrange("p (g o) -> p g o", o=1).to_broadcast([P, GROUP, m])
                        row = lambda m: iota[:, 0:m].rearrange("p (o j) -> p o j", o=1).to_broadcast([P, GROUP, m])
                        nc.vector.tensor_tensor(hot_lane[:, q], flat(lane, P), row(P), ALU.is_equal)
                        nc.vector.tensor_tensor(hot_tile[:, q], flat(tile_no, TILES), row(TILES), ALU.is_equal).then_inc(hots, 1)
                        dve.wait_ge(dups, GQ * n + GROUP * q + GROUP + 4)
                        dve.wait_ge(retired, QUADS * n + q + 1)
                        nc.vector.tensor_copy(cell[:, q, :], cc[:, cols])
                        step(nc.vector.tensor_scalar(is_dup[:, q, :], earlier[:, q, :], 0.0, None, ALU.is_gt))
                        dve.sem_inc(own_turns, 1)
                        nc.vector.copy_predicated(cell[:, q, :], is_dup[:, q, :], mem.dummy).then_inc(cells_set, 1)
                step.end(QUADS, ITERS)
                dve.wait_ge(deg_done, 1)
                step(nc.vector.tensor_scalar(mem.rdeg[:], deg_ps, 1.0, None, ALU.max))
                step(nc.vector.reduce_max(mem.top[:, 0:1], mem.rdeg[:], X_AXIS))
                nc.vector.reciprocal(mem.rdeg[:], mem.rdeg[:])


def largest_degree(nc, mem):
    with ExitStack() as ctx:
        flipped, topped = (ctx.enter_context(nc.semaphore(n)) for n in ("top_flipped", "topped"))
        with nc.Block() as block:
            @block.tensor
            def _(pe):
                nc.tensor.transpose(mem.bank[0][0:1, 0:P], mem.top[:, 0:1], mem.ident).then_inc(flipped, 1)

            @block.vector
            def _(dve):
                dve.wait_ge(flipped, 1)
                nc.vector.reduce_max(mem.top[0:1, 1:2], mem.bank[0][0:1, 0:P], X_AXIS).then_inc(topped, 1)
                dve.wait_ge(topped, 1)
                nc.vector.tensor_copy(mem.top_int[0:1, 0:1], mem.top[0:1, 1:2])


def gnn_layer(nc, mem, layer, g):
    with ExitStack() as ctx:
        sb = lambda n, s, d: ctx.enter_context(nc.sbuf_tensor(f"{n}_{layer}", s, d))
        new_sem = ctx.enter_context(stage_semaphores(nc))
        sem = lambda n: new_sem(f"{n}_{layer}")
        bank, h, hi, lo = mem.bank, mem.h, mem.h_hi, mem.h_lo
        wl, wr = sb("wl", [P, HALVES, D], F32), sb("wr", [P, HALVES, D], F32)
        bn = sb("bn_rows", [P, 5, D], F32)
        agg, own_rows, hT = sb("agg", [P, HALVES, CHUNK], F32), sb("own_rows", [P, 2, D], F32), sb("hT", [P, 2, HALVES, P], F32)
        z1s = sb("z1", [P, 2, D], F32)
        landed = [sem(f"counts_in{k}") for k in range(SLOTS)]
        split, batch_done, agg_out, copied, flipped, hT_ready = (sem(n) for n in ("h_split", "batch_done", "agg_out", "rows_copied", "rows_flipped", "hT_ready"))
        own, z_ps, z_read, w_in, w_ready, hi_done, z_own = (sem(n) for n in ("bn_own", "z_ps", "z_read", "w_in", "w_ready", "hi_done", "z_own"))

        var_ready, rstd_ready = sem("bn_var_ready"), sem("bn_rstd_ready")
        with nc.Block() as block:
            @block.sync
            def _(sp):
                def load(n, b):
                    s0, m = batch_tiles(b)
                    k = b % SLOTS
                    if isinstance(n, int) and n == CHUNKS:
                        cells = mem.counts[CHUNKS * CELL_CHUNK:(CHUNKS + 1) * CELL_CHUNK].rearrange("(p s j) -> p s j", p=P, j=CHUNK)[:, s0:s0 + m, 0:P]
                        dest = mem.slot[k][:, 0:m * P].rearrange("p (s j) -> p s j", j=P)
                    else:
                        cells = mem.counts[0:CHUNKS * CELL_CHUNK].rearrange("(n p s) -> n p s", n=CHUNKS, p=P)[n][:, s0 * CHUNK:(s0 + m) * CHUNK]
                        dest = mem.slot[k][:, 0:m * CHUNK]
                    sp.dma_start(dest.bitcast(F32), cells).then_inc(landed[k], 16)

                for b in range(SLOTS):
                    load(0, b)
                sp.dma_start(wl[:], g["Wl"][layer].rearrange("(a p) d -> p a d", p=P)).then_inc(w_in, 16)
                sp.dma_start(wr[:], g["Wr"][layer].rearrange("(a p) d -> p a d", p=P)).then_inc(w_in, 16)
                for i, name in enumerate(("rvar", "gamma", "b", "rmean", "beta")):
                    sp.dma_start(bn[:, i, :], g[name][layer].partition_broadcast(P)).then_inc(w_in, 16)

                def chunk_loads(n, following):
                    for b in range(BATCHES):
                        nxt = (n, b + SLOTS) if b + SLOTS < BATCHES else (following, b + SLOTS - BATCHES)
                        if nxt[0] is None:
                            continue
                        sp.wait_ge(batch_done, BATCHES * n + b + 1)
                        load(*nxt)

                with sp.Fori(0, CHUNKS - 1) as n:
                    chunk_loads(n, n + 1)
                chunk_loads(CHUNKS - 1, CHUNKS)
                chunk_loads(CHUNKS, None)

            @block.tensor
            def _(pe):
                pe.sem_inc(z_ps, CREDIT)
                def products(b, width, ty):
                    s0, m = batch_tiles(b)
                    for i in range(m):
                        s = s0 + i
                        right = mem.slot[b % SLOTS][:, i * width:(i + 1) * width]
                        for a in range(HALVES):
                            for part, left in enumerate((hi, lo)):
                                l = left[:, s, a * P:(a + 1) * P]
                                last = nc.tensor.matmul(bank[a][:, 0:width], l if ty is F32R else l.bitcast(F32), right if ty is F32R else right.bitcast(F32),
                                                        start=(s == 0 and part == 0), stop=(s == TILES - 1 and part == 1))
                    last.then_inc(batch_done, 1)

                def flip(n, i, per=4):
                    pe.wait_ge(copied, 4 * n + i + 1)
                    for a in range(HALVES):
                        last = nc.tensor.transpose(bank[2 + i % 2][:, a * P:(a + 1) * P], own_rows[:, i % 2, a * P:(a + 1) * P], mem.ident)
                    last.then_inc(flipped, 1)

                def project(n, i):
                    out = bank[4 + i % 2]
                    pe.wait_ge(hT_ready, 4 * n + i + 1)
                    pe.wait_ge(z_read, 4 * n + i + 1)
                    for a in range(HALVES):
                        nc.tensor.matmul(out[:, 0:D], hT[:, i % 2, a, :], wr[:, a, :], start=(a == 0), stop=(a == HALVES - 1))
                    pe.wait_ge(agg_out, HALVES * n + HALVES + CREDIT)
                    for a in range(HALVES):
                        last = nc.tensor.matmul(out[:, D:2 * D], agg[:, a, i * P:(i + 1) * P], wl[:, a, :], start=(a == 0), stop=(a == HALVES - 1))
                    last.then_inc(z_ps, 1)

                def chunk(n, width, ty):
                    tiles = width // P
                    pe.wait_ge(agg_out, HALVES * n + CREDIT)
                    for b in range(BATCHES):
                        s0, m = batch_tiles(b)
                        pe.wait_ge(split, (s0 + m - 1) // 7 + 1)
                        pe.wait_ge(landed[b % SLOTS], 16 * (BATCHES // SLOTS) * n + 16 * (b // SLOTS + 1))
                        if b == BATCHES - 1:
                            for i in range(min(2, tiles)):
                                flip(n, i)
                        products(b, width, ty)
                    pe.wait_ge(w_ready, 1)
                    for i in range(tiles):
                        project(n, i)
                        if i + 2 < tiles:
                            flip(n, i + 2)

                def everything(ty):
                    with pe.Fori(0, CHUNKS) as n:
                        chunk(n, CHUNK, ty)
                    chunk(CHUNKS, P, ty)

                with pe.register(f"top_{layer}") as top:
                    pe.reg_load(top, mem.top_int[0:1, 0:1])
                    with pe.If_lt(top, EXACT):
                        everything(F32R)
                    with pe.Else():
                        everything(F32)

            @block.gpsimd
            def _(pool):
                pool.wait_ge(var_ready, 1)
                power(nc, mem, bn[:, 0, :], D).then_inc(rstd_ready, 1)

            @block.scalar
            def _(act):
                def copy_rows(n, i, t):
                    nc.scalar.copy(own_rows[:, i % 2, :], h[:, t, :]).then_inc(copied, 1)

                def take(n, i):
                    act.wait_ge(flipped, 4 * n + i + 1)
                    nc.scalar.copy(hT[:, i % 2, :, :].rearrange("p a b -> p (a b)"), bank[2 + i % 2][:, 0:D]).then_inc(hT_ready, 1)

                def sums(n, width):
                    act.wait_ge(batch_done, BATCHES * n + BATCHES)
                    nc.scalar.copy(agg[:, 1, 0:width], bank[1][:, 0:width]).then_inc(agg_out, 1)

                with act.Fori(0, CHUNKS) as n:
                    for i in range(2):
                        act.wait_ge(z_ps, 4 * n + CREDIT)
                        copy_rows(n, i, 4 * n + i)
                    for i in range(2):
                        take(n, i)
                    sums(n, CHUNK)
                    for i in range(2, 4):
                        copy_rows(n, i, 4 * n + i)
                    for i in range(2, 4):
                        act.wait_ge(z_ps, 4 * n + i - 1 + CREDIT)
                        take(n, i)
                act.wait_ge(z_ps, 4 * CHUNKS + CREDIT)
                copy_rows(CHUNKS, 0, FULL)
                take(CHUNKS, 0)
                sums(CHUNKS, P)

            @block.vector
            def _(dve):
                step = Steps(dve, own)
                dve.sem_inc(z_read, 2)
                dve.sem_inc(agg_out, CREDIT)
                for k in range(7):
                    part = slice(7 * k, 7 * k + 7)
                    nc.vector.tensor_copy(hi[:, part, :], h[:, part, :]).then_inc(hi_done, 1)
                    dve.wait_ge(hi_done, k + 1)
                    nc.vector.tensor_tensor(lo[:, part, :], h[:, part, :], hi[:, part, :].bitcast(F32), ALU.subtract).then_inc(split, 1)
                dve.wait_ge(w_in, 16 * 7)
                rvar, gamma, b, rmean, beta = (bn[:, i, :] for i in range(5))
                nc.vector.tensor_scalar(rvar, rvar, EPS, None, ALU.add).then_inc(var_ready, 1)
                dve.wait_ge(rstd_ready, 1)
                step(nc.vector.tensor_tensor(gamma, gamma, rvar, ALU.mult))
                step(nc.vector.tensor_tensor(b, b, rmean, ALU.subtract))
                step(nc.vector.tensor_tensor(b, b, gamma, ALU.mult))
                step(nc.vector.tensor_tensor(b, b, beta, ALU.add))
                for w in (wl, wr):
                    for a in range(HALVES):
                        last = nc.vector.tensor_tensor(w[:, a, :], w[:, a, :], gamma, ALU.mult)
                last.then_inc(w_ready, 1)

                def sums(n, width):
                    dve.wait_ge(batch_done, BATCHES * n + BATCHES)
                    nc.vector.tensor_copy(agg[:, 0, 0:width], bank[0][:, 0:width]).then_inc(agg_out, 1)

                def finish(n, i, t):
                    z, z1 = bank[4 + i % 2], z1s[:, i % 2, :]
                    dve.wait_ge(z_ps, 4 * n + i + 1 + CREDIT)
                    step(nc.vector.tensor_tensor(z1, z[:, 0:D], b, ALU.add))
                    nc.vector.scalar_tensor_tensor(out=z1, in0=z[:, D:2 * D], scalar=mem.rdeg[:, bass.ds(t, 1)], in1=z1,
                                                   op0=ALU.mult, op1=ALU.add).then_inc(z_read, 1)
                    dve.wait_ge(z_read, 4 * n + i + 3)
                    if layer < LAYERS - 1:
                        nc.vector.scalar_tensor_tensor(out=h[:, t, :], in0=z1, scalar=0.0, in1=h[:, t, :], op0=ALU.max, op1=ALU.add)
                    else:
                        nc.vector.tensor_tensor(h[:, t, :], z1, h[:, t, :], ALU.add)

                with dve.Fori(0, CHUNKS) as n:
                    step.loop(n, 4)
                    sums(n, CHUNK)
                    for i in range(4):
                        finish(n, i, 4 * n + i)
                step.end(4, CHUNKS)
                sums(CHUNKS, P)
                finish(CHUNKS, 0, FULL)


def router_stage(nc, mem, f):
    with ExitStack() as ctx:
        sb = lambda n, s, d: ctx.enter_context(nc.sbuf_tensor(n, s, d))
        sem = ctx.enter_context(stage_semaphores(nc))
        bank, h = mem.bank, mem.h
        xm, stats, tmp = sb("xm_rows", [P, TILES, D], F32), sb("ffn_stats", [P, TILES, 6], F32), sb("ffn_tmp", [P, TILES], F32)
        gate_w, gate_b = sb("gate_w", [P, HALVES, E], F32), sb("gate_b", [P, E], F32)
        xs, xT = sb("router_rows", [P, 2, D], F32), sb("router_xT", [P, 2, HALVES, P], F32)
        logits, score, onehot = (sb(n, [P, TILES, E], F32) for n in ("logits", "score", "onehot"))
        best = sb("best", [P, 3, TILES], F32)
        chosen = sb("chosen", [P, E, TILES, 2], BF16)
        tri, ones = sb("tri_bf", [P, P], BF16), sb("ones_bf", [P, P], BF16)
        rank = sb("rank_e", [P, E], F32)
        counts, counts_i, ends = sb("e_counts", [P, E], F32), sb("e_counts_i", [P, E], I32), sb("e_ends", [P, E], F32)
        room, w_e = xm[:].rearrange("p t d -> p (t d)"), E * 2 * TILES
        before, place, keep = (room[:, k * w_e:(k + 1) * w_e].rearrange("p (e m) -> p e m", e=E) for k in range(3))
        tile_e = room[0:1, 3 * w_e:3 * w_e + XT * E].rearrange("p (j e) -> p j e", e=E)
        one = sb("ones_e", [P, E], F32)
        slot_f, tile_f = sb("slot_f", [P, TILES, 2], F32), sb("tile_f", [1, XT], F32)
        loaded, gate_in, added, own, stats_done = (sem(n) for n in ("xm_in", "gate_in", "x2_done", "router_own", "ffn_stats_done"))
        var_ready, rstd_ready, xs_ready, flipped, xT_ready, logit_ps, logit_read = (
            sem(n) for n in ("ffn_var", "ffn_rstd", "router_xs", "router_flip", "router_xT_ready", "logit_ps", "logit_read"))
        cleared, chosen_ready, ranked, exp_in, exp_out = (sem(n) for n in ("router_cleared", "chosen_ready", "ranked", "exp_in", "exp_out"))
        parts = [(12 * k, 12) for k in range(4)] + [(FULL, 1)]

        with nc.Block() as block:
            @block.sync
            def _(sp):
                sp.wait_ge(cleared, 1)
                for k, (t, m) in enumerate(parts):
                    if t < FULL:
                        sp.dma_start(xm[:, t:t + m, :], rows(mem.xm_dram)[:, t:t + m, :]).then_inc(mem.part_in[k], 16)
                    else:
                        sp.dma_start(xm[0:TAIL, t, :], mem.xm_dram[FULL * P:N, :]).then_inc(mem.part_in[k], 16)
                sp.dma_start(gate_w[:], f["gate_w"].rearrange("(a p) e -> p a e", p=P)).then_inc(gate_in, 16)
                sp.dma_start(gate_b[:], f["gate_b"].partition_broadcast(P)).then_inc(gate_in, 16)
                for e in range(E):
                    sp.dma_start(mem.w1[:, e, :, :], f["w1"][e].rearrange("(a p) f -> p a f", p=P)).then_inc(mem.w1_in, 16)

            @block.tensor
            def _(pe):
                pe.sem_inc(flipped, CREDIT)
                pe.wait_ge(gate_in, 32)

                def tile(j, n):
                    pe.wait_ge(xs_ready, 2 * n + j + 1)
                    for a in range(HALVES):
                        last = nc.tensor.transpose(bank[j][:, a * P:(a + 1) * P], xs[:, j, a * P:(a + 1) * P], mem.ident)
                    last.then_inc(flipped, 1)
                    pe.wait_ge(xT_ready, 2 * n + j + 1)
                    pe.wait_ge(logit_read, 2 * n + CREDIT)
                    for a in range(HALVES):
                        last = nc.tensor.matmul(bank[2 + j][:, 0:E], xT[:, j, a, :], gate_w[:, a, :], start=(a == 0), stop=(a == HALVES - 1))
                    last.then_inc(logit_ps, 1)

                with pe.Fori(0, FULL // 2) as n:
                    for j in range(2):
                        tile(j, n)
                tile(0, FULL // 2)
                pe.wait_ge(chosen_ready, 1)
                flat = chosen[:].rearrange("p e t k -> p (e t k)")
                w = E // 4 * 2 * TILES
                for c in range(4):
                    nc.tensor.matmul(bank[c][:, 0:w], tri[:], flat[:, c * w:(c + 1) * w], start=True, stop=True)
                    last = nc.tensor.matmul(bank[4 + c][:, 0:w], ones[:], flat[:, c * w:(c + 1) * w], start=True, stop=True)
                last.then_inc(ranked, 1)

            @block.scalar
            def _(act):
                def take(j, n):
                    act.wait_ge(flipped, 2 * n + j + 1 + CREDIT)
                    nc.scalar.copy(xT[:, j, :, :].rearrange("p a b -> p (a b)"), bank[j][:, 0:D]).then_inc(xT_ready, 1)

                with act.Fori(0, FULL // 2) as n:
                    for j in range(2):
                        take(j, n)
                take(0, FULL // 2)
                act.wait_ge(exp_in, 1)
                nc.scalar.activation(mem.gates[:, 1, :], mem.gates[:, 1, :], ACT.Exp).then_inc(exp_out, 1)

            @block.gpsimd
            def _(pool):
                nc.gpsimd.memset(xm[:, FULL, :], 0.0).then_inc(cleared, 1)
                nc.gpsimd.iota(mem.rank_i[:], pattern=[[-1, E]], base=E, channel_multiplier=0).then_inc(cleared, 1)
                pool.wait_ge(var_ready, 1)
                power(nc, mem, mem.rstd[:], TILES).then_inc(rstd_ready, 1)

            @block.vector
            def _(dve):
                step = Steps(dve, own)
                dve.sem_inc(logit_read, CREDIT)
                for k, (t, m) in enumerate(parts):
                    dve.wait_ge(mem.part_in[k], 16)
                    nc.vector.tensor_tensor(h[:, t:t + m, :], h[:, t:t + m, :], xm[:, t:t + m, :], ALU.add).then_inc(added, 1)
                dve.wait_ge(added, len(parts))
                with dve.Fori(0, TILES) as n:
                    nc.vector.bn_stats(stats[:, n, :], h[:, n, :]).then_inc(stats_done, 1)
                dve.wait_ge(stats_done, TILES)
                ln_rows(nc, dve, step, stats, mem.mean, mem.rstd, tmp, var_ready, rstd_ready)

                def normalise(j, n, t):
                    dve.wait_ge(flipped, 2 * n + CREDIT)
                    nc.vector.tensor_scalar(xs[:, j, :], h[:, t, :], mem.mean[:, bass.ds(t, 1)], mem.rstd[:, bass.ds(t, 1)], ALU.subtract, ALU.mult).then_inc(xs_ready, 1)

                def read(j, n, t):
                    dve.wait_ge(logit_ps, 2 * n + j + 1)
                    nc.vector.tensor_tensor(logits[:, t, :], bank[2 + j][:, 0:E], gate_b[:], ALU.add).then_inc(logit_read, 1)

                dve.wait_ge(gate_in, 32)
                with dve.Fori(0, FULL // 2) as n:
                    for j in range(2):
                        normalise(j, n, 2 * n + j)
                    for j in range(2):
                        read(j, n, 2 * n + j)
                normalise(0, FULL // 2, FULL)
                read(0, FULL // 2, FULL)
                dve.wait_ge(logit_read, TILES + CREDIT)
                dve.wait_ge(cleared, 2)
                step(nc.vector.tensor_copy(rank[:], mem.rank_i[:]))
                wide = lambda v: v.rearrange("p (t o) -> p t o", o=1).to_broadcast([P, TILES, E])
                each = rank[:].rearrange("p (o e) -> p o e", o=1).to_broadcast([P, TILES, E])
                for k in range(2):
                    step(nc.vector.reduce_max(best[:, k, :], logits[:], X_AXIS))
                    step(nc.vector.tensor_tensor(score[:], logits[:], wide(best[:, k, :]), ALU.is_equal))
                    step(nc.vector.tensor_tensor(score[:], score[:], each, ALU.mult))
                    step(nc.vector.reduce_max(best[:, 2, :], score[:], X_AXIS))
                    step(nc.vector.tensor_tensor(onehot[:], score[:], wide(best[:, 2, :]), ALU.is_equal))
                    step(nc.vector.tensor_scalar(onehot[:, FULL, :], onehot[:, FULL, :], mem.valid, None, ALU.mult))
                    step(nc.vector.tensor_copy(chosen[:, :, :, k], onehot[:].rearrange("p t e -> p e t")))
                    if k == 0:
                        step(nc.vector.scalar_tensor_tensor(out=logits[:], in0=onehot[:], scalar=-3e38, in1=logits[:], op0=ALU.mult, op1=ALU.add))
                        step(nc.vector.tensor_copy(mem.weigh[:], onehot[:]))
                nc.vector.tensor_copy(tri[:], mem.tri)
                nc.vector.memset(ones[:], 1.0).then_inc(chosen_ready, 1)
                nc.vector.tensor_tensor(mem.gates[:, 1, :], best[:, 1, :], best[:, 0, :], ALU.subtract).then_inc(exp_in, 1)
                dve.wait_ge(exp_out, 1)
                step(nc.vector.tensor_scalar(mem.gates[:, 0, :], mem.gates[:, 1, :], 1.0, None, ALU.add))
                step(nc.vector.reciprocal(mem.gates[:, 0, :], mem.gates[:, 0, :]))
                step(nc.vector.tensor_tensor(mem.gates[:, 1, :], mem.gates[:, 0, :], mem.gates[:, 1, :], ALU.mult))
                step(nc.vector.tensor_tensor(mem.weigh[:], mem.weigh[:], wide(mem.gates[:, 0, :]), ALU.mult))
                step(nc.vector.tensor_tensor(onehot[:], onehot[:], wide(mem.gates[:, 1, :]), ALU.mult))
                step(nc.vector.tensor_tensor(mem.weigh[:], mem.weigh[:], onehot[:], ALU.add))
                step(nc.vector.memset(keep, 1.0))
                step(nc.vector.memset(keep[:, :, 0:1], 0.0))
                step(nc.vector.memset(one[:], 1.0))
                dve.wait_ge(ranked, 1)
                w = E // 4 * 2 * TILES
                per = lambda c: mem.bank[c][:, 0:w].rearrange("p (e m) -> p e m", e=E // 4)
                for c in range(4):
                    nc.vector.tensor_reduce(counts[:, 4 * c:4 * c + 4], per(4 + c), X_AXIS, ALU.add)
                    last = nc.vector.tensor_copy(before[:, 4 * c:4 * c + 4, 1:], per(4 + c)[:, :, 0:2 * TILES - 1])
                step(last)
                step(nc.vector.tensor_scalar(counts_i[:], counts[:], float(P - 1), None, ALU.add))
                step(nc.vector.tensor_scalar(counts_i[:], counts_i[:], 7, 7, ALU.logical_shift_right, ALU.logical_shift_left))
                step(nc.vector.tensor_copy(counts[:], counts_i[:]))
                step(nc.vector.tensor_tensor_scan(ends[:], one[:], counts[:], 0.0, ALU.mult, ALU.add))
                step(nc.vector.tensor_tensor(before[:, :, 0], ends[:], counts[:], ALU.subtract))
                flat = lambda t: t.rearrange("p e m -> p (e m)")
                step(nc.vector.tensor_tensor_scan(flat(place), flat(keep), flat(before), 0.0, ALU.mult, ALU.add))
                for c in range(4):
                    last = nc.vector.tensor_tensor(place[:, 4 * c:4 * c + 4, :], place[:, 4 * c:4 * c + 4, :], per(c), ALU.add)
                step(last)
                step(nc.vector.tensor_tensor(place, place, chosen[:].rearrange("p e t k -> p e (t k)"), ALU.mult))
                step(nc.vector.tensor_reduce(slot_f[:].rearrange("p t k -> p (t k)"), place.rearrange("p e m -> p m e"), X_AXIS, ALU.add))
                step(nc.vector.tensor_copy(mem.slots[:], slot_f[:]))
                step(nc.vector.tensor_scalar(tile_f[:], mem.iota[0:1, 0:XT], float(P), None, ALU.mult))
                first = tile_f[:].rearrange("p (j o) -> p j o", o=1).to_broadcast([1, XT, E])
                last_of = ends[0:1, :].rearrange("p (o e) -> p o e", o=1).to_broadcast([1, XT, E])
                step(nc.vector.tensor_tensor(tile_e, first, last_of, ALU.is_ge))
                step(nc.vector.tensor_reduce(tile_f[:], tile_e, X_AXIS, ALU.add))
                step(nc.vector.tensor_scalar(mem.tile_expert[:], tile_f[:], float(E - 1), None, ALU.min))


def dispatch_stage(nc, mem, f):
    with ExitStack() as ctx:
        sb = lambda n, s, d: ctx.enter_context(nc.sbuf_tensor(n, s, d))
        sem = ctx.enter_context(stage_semaphores(nc))
        xs, where = sb("dispatch_rows", [P, 2, D], F32), sb("dispatch_slot", [P, 2, 2], I32)
        ready, free, turn = sem("dispatch_ready"), sem("dispatch_free"), sem("dispatch_turn")
        sent = [sem(f"dispatch_sent{j}") for j in range(2)]
        with nc.Block() as block:
            @block.sync
            def _(sp):
                for e in range(E):
                    sp.dma_start(mem.w2[:, e, :, :], f["w2"][e].rearrange("(a p) f -> p a f", p=P)).then_inc(mem.w2_in, 16)
                sp.dma_start(mem.b1_rows[:], f["b1"].rearrange("e (a p) -> (e a) p", p=P)).then_inc(mem.b1_in, 16)

            @block.vector
            def _(dve):
                def prepare(j, n, t):
                    dve.wait_ge(free, 2 * n + j + 1)
                    nc.vector.tensor_scalar(xs[:, j, :], mem.h[:, t, :], mem.mean[:, bass.ds(t, 1)], mem.rstd[:, bass.ds(t, 1)], ALU.subtract, ALU.mult)
                    nc.vector.tensor_copy(where[:, j, :], mem.slots[:, t, :]).then_inc(ready, 1)

                dve.sem_inc(free, 2)
                with dve.Fori(0, FULL // 2) as n:
                    for j in range(2):
                        prepare(j, n, 2 * n + j)
                prepare(0, FULL // 2, FULL)

            @block.gpsimd
            def _(pool):
                def send(j, r):
                    for k in range(2):
                        pool.indirect_dma_start(out=mem.slot_rows, out_offset=bass.IndirectOffsetOnAxis(ap=where[0:r, j, k:k + 1], axis=0),
                                                in_=xs[0:r, j, :], in_offset=None).then_inc(sent[j], 16)

                with pool.Fori(0, FULL // 2) as n:
                    for j in range(2):
                        pool.wait_ge(ready, 2 * n + j + 1)
                        pool.sem_inc(turn, 1)
                        send(j, P)
                    for j in range(2):
                        pool.wait_ge(sent[j], 32 * n + 32)
                        pool.sem_inc(free, 1)
                pool.wait_ge(ready, TILES)
                pool.sem_inc(turn, 1)
                send(0, TAIL)
                pool.wait_ge(sent[0], 32 * (FULL // 2) + 32)


def expert_stage(nc, mem):
    with ExitStack() as ctx:
        sb = lambda n, s, d: ctx.enter_context(nc.sbuf_tensor(n, s, d))
        sem = ctx.enter_context(stage_semaphores(nc))
        bank = mem.bank
        FT = FF // P
        xs, xT = sb("slot_x", [P, 2, D], F32), sb("slot_xT", [P, HALVES, P], F32)
        hid, hT, y = sb("hidden", [P, FF], F32), sb("hidden_T", [P, FT, P], F32), sb("slot_y", [P, 2, D], F32)
        x_in = [sem(f"slot_in{j}") for j in range(2)]
        y_out = [sem(f"slot_out{j}") for j in range(2)]
        y_free = sem("y_free")
        flipped, xT_ready, hid_ps, hid_ready, hid_flipped, hT_ready, y_ps, y_ready = (
            sem(n) for n in ("slot_flipped", "slot_xT_ready", "hid_ps", "hid_ready", "hid_flipped", "hT_ready_e", "y_ps", "y_ready"))
        b1_flipped, b1_ready, hid_last = sem("b1_flipped"), sem("b1_ready"), sem("hT_dve")
        PAIRS = XT // 2
        load_v = mem.slot_rows.rearrange("(t p) d -> t p d", p=P)
        store_v = mem.slot_out.rearrange("(t p) d -> t p d", p=P)

        with nc.Block() as block:
            @block.sync
            def _(sp):
                def load(t, j):
                    sp.dma_start(xs[:, j, :], load_v[t]).then_inc(x_in[j], 16)

                def store(n, t, j):
                    sp.wait_ge(y_ready, 2 * n + j + 1)
                    sp.dma_start(store_v[t], y[:, j, :]).then_inc(y_out[j], 16)

                for j in range(2):
                    load(j, j)
                with sp.Fori(0, PAIRS - 1) as n:
                    for j in range(2):
                        sp.wait_ge(flipped, 2 * n + j + 1)
                        load(2 * n + j + 2, j)
                        store(n, 2 * n + j, j)
                n = PAIRS - 1
                sp.wait_ge(flipped, 2 * n + 1)
                load(2 * n + 2, 0)
                for j in range(2):
                    store(n, 2 * n + j, j)
                store(PAIRS, 2 * PAIRS, 0)
                sp.wait_ge(y_out[0], 16 * (PAIRS + 1))
                sp.wait_ge(y_out[1], 16 * PAIRS)

            @block.tensor
            def _(pe):
                pe.wait_ge(mem.b1_in, 16)
                nc.tensor.transpose(bank[7][:, 0:E * FT], mem.b1_rows[:], mem.ident[0:E * FT, 0:E * FT]).then_inc(b1_flipped, 1)
                pe.wait_ge(mem.w1_in, 16 * E)
                pe.wait_ge(mem.w2_in, 16 * E)
                w1 = mem.w1[:].rearrange("p e a f -> p e (a f)")
                w2 = mem.w2[:].rearrange("p e a f -> p e (a f)")

                def tile(n, t, j):
                    e = pe.value_load(mem.tile_expert[0:1, bass.ds(t, 1)], min_val=0, max_val=E - 1)
                    pe.wait_ge(x_in[j], 16 * n + 16)
                    for a in range(HALVES):
                        last = nc.tensor.transpose(bank[0][:, a * P:(a + 1) * P], xs[:, j, a * P:(a + 1) * P], mem.ident)
                    last.then_inc(flipped, 1)
                    pe.wait_ge(xT_ready, 2 * n + j + 1)
                    for a in range(HALVES):
                        last = nc.tensor.matmul(bank[1][:, :], xT[:, a, :], w1[:, e, a * FF:(a + 1) * FF], start=(a == 0), stop=(a == HALVES - 1))
                    last.then_inc(hid_ps, 1)
                    pe.wait_ge(hid_ready, 2 * n + j + 1)
                    for k in range(FT):
                        last = nc.tensor.transpose(bank[2 + k // 2][:, (k % 2) * P:(k % 2 + 1) * P], hid[:, k * P:(k + 1) * P], mem.ident)
                        if k % 2:
                            last.then_inc(hid_flipped, 1)
                    pe.wait_ge(hT_ready, 2 * n + j + 1)
                    pe.wait_ge(hid_last, 2 * n + j + 1)
                    for k in range(FT):
                        last = nc.tensor.matmul(bank[4 + j][:, 0:D], hT[:, k, :], w2[:, e, k * D:(k + 1) * D], start=(k == 0), stop=(k == FT - 1))
                    last.then_inc(y_ps, 1)

                with pe.Fori(0, PAIRS) as n:
                    for j in range(2):
                        tile(n, 2 * n + j, j)
                tile(PAIRS, 2 * PAIRS, 0)

            @block.scalar
            def _(act):
                act.wait_ge(b1_ready, 1)

                def tile(n, t, j):
                    e = act.value_load(mem.tile_expert[0:1, bass.ds(t, 1)], min_val=0, max_val=E - 1)
                    act.wait_ge(flipped, 2 * n + j + 1)
                    nc.scalar.copy(xT[:].rearrange("p a b -> p (a b)"), bank[0][:, 0:D]).then_inc(xT_ready, 1)
                    act.wait_ge(hid_flipped, 4 * n + 2 * j + 1)
                    for k in range(FT // 2):
                        last = nc.scalar.activation(hT[:, k, :], bank[2][:, k * P:(k + 1) * P], ACT.Relu, bias=mem.b1T[:, bass.ds(e * FT + k, 1)])
                    last.then_inc(hT_ready, 1)
                    act.wait_ge(y_ps, 2 * n + j + 1)
                    act.wait_ge(y_free, 2 * n + j + 1)
                    nc.scalar.copy(y[:, j, :], bank[4 + j][:, 0:D]).then_inc(y_ready, 1)

                with act.Fori(0, PAIRS) as n:
                    for j in range(2):
                        tile(n, 2 * n + j, j)
                tile(PAIRS, 2 * PAIRS, 0)

            @block.gpsimd
            def _(pool):
                pool.sem_inc(y_free, 2)
                with pool.Fori(0, PAIRS) as n:
                    for j in range(2):
                        pool.wait_ge(y_out[j], 16 * n + 16)
                        pool.sem_inc(y_free, 1)

            @block.vector
            def _(dve):
                dve.wait_ge(b1_flipped, 1)
                nc.vector.tensor_copy(mem.b1T[:], bank[7][:, 0:E * FT]).then_inc(b1_ready, 1)
                dve.wait_ge(b1_ready, 1)

                def tile(n, t, j):
                    e = dve.value_load(mem.tile_expert[0:1, bass.ds(t, 1)], min_val=0, max_val=E - 1)
                    dve.wait_ge(hid_ps, 2 * n + j + 1)
                    nc.vector.tensor_copy(hid[:], bank[1][:, :]).then_inc(hid_ready, 1)
                    dve.wait_ge(hid_flipped, 4 * n + 2 * j + 2)
                    for k in range(FT // 2, FT):
                        last = nc.vector.tensor_scalar(hT[:, k, :], bank[3][:, (k % 2) * P:(k % 2 + 1) * P], mem.b1T[:, bass.ds(e * FT + k, 1)], 0.0, ALU.add, ALU.max)
                    last.then_inc(hid_last, 1)

                with dve.Fori(0, PAIRS) as n:
                    for j in range(2):
                        tile(n, 2 * n + j, j)
                tile(PAIRS, 2 * PAIRS, 0)


def combine_stage(nc, mem, f, out):
    with ExitStack() as ctx:
        sb = lambda n, s, d: ctx.enter_context(nc.sbuf_tensor(n, s, d))
        sem = ctx.enter_context(stage_semaphores(nc))
        bank, h = mem.bank, mem.h
        gamma, beta, b2 = sb("ffn_gamma", [P, D], F32), sb("ffn_beta", [P, D], F32), sb("ffn_b2", [E, D], F32)
        rows_in, where, wrow, wT = sb("gathered", [P, 2, 2, D], F32), sb("gather_slot", [P, 2, 2], I32), sb("weigh_rows", [P, 2, E], F32), sb("weigh_T", [E, 2, P], F32)
        acc, st, mv, norm, res = sb("acc", [P, 2, D], F32), sb("acc_stats", [P, 2, 6], F32), sb("acc_mv", [P, 2, 2], F32), sb("acc_norm", [P, 2, D], F32), sb("res", [P, 2, D], F32)
        in_b, where_ready, turn, weigh_ready, w_flipped, wT_ready, bias_ps = (
            sem(n) for n in ("ffn_rows_in", "where_ready", "gather_turn", "weigh_ready", "w_flipped", "wT_ready_c", "bias_ps"))
        own, acc_done, var_ready, rstd_ready, res_ready, res_free, rows_done = (
            sem(n) for n in ("combine_own", "acc_done", "acc_var", "acc_rstd", "res_ready", "res_free", "rows_done"))
        aggr_turn = sem("aggr_turn")
        gathered = [sem(f"gathered{j}") for j in range(2)]
        stored = [sem(f"stored{j}") for j in range(2)]
        HALF = FULL // 2

        with nc.Block() as block:
            @block.sync
            def _(sp):
                sp.dma_start(gamma[:], f["gamma"].partition_broadcast(P)).then_inc(in_b, 16)
                sp.dma_start(beta[:], f["beta"].partition_broadcast(P)).then_inc(in_b, 16)
                sp.dma_start(b2[:], f["b2"]).then_inc(in_b, 16)
                out_v = out[0:FULL * P, :].rearrange("(t p) d -> t p d", p=P)
                sp.sem_inc(res_free, 2)
                with sp.Fori(0, HALF) as n:
                    for j in range(2):
                        sp.wait_ge(res_ready, 2 * n + j + 1)
                        sp.dma_start(out_v[2 * n + j], res[:, j, :]).then_inc(stored[j], 16)
                    for j in range(2):
                        sp.wait_ge(stored[j], 16 * n + 16)
                        sp.sem_inc(res_free, 1)
                sp.wait_ge(res_ready, TILES)
                sp.dma_start(out[FULL * P:N, :], res[0:TAIL, 0, :]).then_inc(stored[0], 16)
                sp.wait_ge(stored[0], 16 * HALF + 16)
                sp.wait_ge(stored[1], 16 * HALF)

            @block.gpsimd
            def _(pool):
                def gather(j, r):
                    for k in range(2):
                        pool.indirect_dma_start(out=rows_in[0:r, j, k, :], out_offset=None, in_=mem.slot_out,
                                                in_offset=bass.IndirectOffsetOnAxis(ap=where[0:r, j, k:k + 1], axis=0)).then_inc(gathered[j], 16)

                def root(j, n):
                    pool.wait_ge(var_ready, 2 * n + j + 1)
                    power(nc, mem, mv[:, j, 1:2], 1).then_inc(rstd_ready, 1)

                nc.gpsimd.memset(rows_in[:, 0, :, :], 0.0).then_inc(turn, 1)
                pool.wait_ge(turn, 1)
                with pool.Fori(0, HALF) as n:
                    for j in range(2):
                        pool.wait_ge(where_ready, 2 * n + j + 1)
                        pool.sem_inc(turn, 1)
                        gather(j, P)
                    for j in range(2):
                        root(j, n)
                pool.wait_ge(where_ready, TILES)
                pool.sem_inc(turn, 1)
                gather(0, TAIL)
                root(0, HALF)

            @block.tensor
            def _(pe):
                pe.sem_inc(w_flipped, CREDIT)
                pe.wait_ge(in_b, 48)

                def tile(j, n):
                    pe.wait_ge(weigh_ready, 2 * n + j + 1)
                    nc.tensor.transpose(bank[j][0:E, 0:P], wrow[:, j, :], mem.ident).then_inc(w_flipped, 1)
                    pe.wait_ge(wT_ready, 2 * n + j + 1)
                    pe.wait_ge(rows_done, 2 * n + CREDIT)
                    nc.tensor.matmul(bank[2 + j][:, 0:D], wT[:, j, :], b2[:], start=True, stop=True).then_inc(bias_ps, 1)

                with pe.Fori(0, HALF) as n:
                    for j in range(2):
                        tile(j, n)
                tile(0, HALF)

            @block.scalar
            def _(act):
                def flip_out(j, n):
                    act.wait_ge(w_flipped, 2 * n + j + 1 + CREDIT)
                    nc.scalar.copy(wT[:, j, :], bank[j][0:E, 0:P]).then_inc(wT_ready, 1)

                with act.Fori(0, HALF) as n:
                    for j in range(2):
                        flip_out(j, n)
                flip_out(0, HALF)

            @block.vector
            def _(dve):
                step = Steps(dve, own)
                dve.sem_inc(rows_done, CREDIT)
                dve.wait_ge(in_b, 48)

                def ask(j, n, t):
                    dve.wait_ge(rows_done, 2 * n + CREDIT)
                    dve.wait_ge(w_flipped, 2 * n + CREDIT)
                    nc.vector.tensor_copy(wrow[:, j, :], mem.weigh[:, t, :]).then_inc(weigh_ready, 1)
                    nc.vector.tensor_copy(where[:, j, :], mem.slots[:, t, :]).then_inc(where_ready, 1)
                    step(nc.vector.tensor_scalar(acc[:, j, :], h[:, t, :], mem.mean[:, bass.ds(t, 1)], mem.rstd[:, bass.ds(t, 1)], ALU.subtract, ALU.mult))

                def add(j, n, t):
                    dve.wait_ge(gathered[j], 32 * n + 32)
                    a = acc[:, j, :]
                    for k in range(2):
                        step(nc.vector.scalar_tensor_tensor(out=a, in0=rows_in[:, j, k, :], scalar=mem.gates[:, k, bass.ds(t, 1)], in1=a, op0=ALU.mult, op1=ALU.add))
                    dve.wait_ge(bias_ps, 2 * n + j + 1)
                    nc.vector.tensor_tensor(a, a, bank[2 + j][:, 0:D], ALU.add).then_inc(rows_done, 1)
                    dve.wait_ge(rows_done, 2 * n + j + 1 + CREDIT)
                    step(nc.vector.bn_stats(st[:, j, :], a))
                    dve.sem_inc(aggr_turn, 1)
                    step(nc.vector.bn_aggr(mv[:, j, :], st[:, j, :]))
                    nc.vector.tensor_scalar(mv[:, j, 1:2], mv[:, j, 1:2], EPS, None, ALU.add).then_inc(var_ready, 1)

                def end(j, n, t):
                    dve.wait_ge(rstd_ready, 2 * n + j + 1)
                    dve.wait_ge(res_free, 2 * n + j + 1)
                    a, b = norm[:, j, :], res[:, j, :]
                    step(nc.vector.tensor_scalar(a, acc[:, j, :], mv[:, j, 0:1], mv[:, j, 1:2], ALU.subtract, ALU.mult))
                    step(nc.vector.tensor_tensor(a, a, gamma[:], ALU.mult))
                    step(nc.vector.tensor_tensor(a, a, beta[:], ALU.add))
                    nc.vector.tensor_tensor(b, a, h[:, t, :], ALU.add).then_inc(res_ready, 1)

                with dve.Fori(0, HALF) as n:
                    step.loop(n, 16)
                    for j in range(2):
                        ask(j, n, 2 * n + j)
                    for j in range(2):
                        add(j, n, 2 * n + j)
                    for j in range(2):
                        end(j, n, 2 * n + j)
                step.end(16, HALF)
                ask(0, HALF, FULL)
                add(0, HALF, FULL)
                end(0, HALF, FULL)


class Memory:
    pass


def program(nc, a, out):
    mem = Memory()
    with ExitStack() as ctx:
        sb = lambda n, s, d: ctx.enter_context(nc.sbuf_tensor(n, s, d))
        mem.psum = ctx.enter_context(nc.psum_tensor("psum", [P, 8 * 512], F32))
        mem.bank = [mem.psum[:, k * 512:(k + 1) * 512] for k in range(8)]
        mem.h = sb("h", [P, TILES, D], F32)
        mem.cf = sb("const_f", [P, 3 * P + 1], F32)
        mem.ident, mem.iota, mem.tri = (mem.cf[:, k * P:(k + 1) * P] for k in range(3))
        mem.minus_half = sb("minus_half", [P, 1], F32)
        mem.valid = mem.cf[:, 3 * P:3 * P + 1]
        mem.rdeg, mem.top, mem.top_int = sb("rdeg", [P, TILES], F32), sb("top", [P, 2], F32), sb("top_int", [P, 1], I32)
        mem.x, mem.mask_embed, mem.cf_dram, mem.ci_dram = a["x"], a["L0_gnn_mask_embed"], a["const_f"][:, 0:3 * P + 1], a["const_i"]
        mem.counts_2d = nc.dram_tensor("counts", [CELLS, 1], F32).ap()
        mem.counts = mem.counts_2d.rearrange("n o -> (n o)")
        mem.cells_dram = nc.dram_tensor("cells", [ETILES * P * P], I32).ap()
        mem.slot_rows = nc.dram_tensor("slot_rows", [XT * P, D], F32).ap()
        mem.slot_out = nc.dram_tensor("slot_out", [XT * P, D], F32).ap()
        mem.xm_dram = nc.dram_tensor("x_mix", [N, D], F32).ap()
        mem.counts_zeroed = ctx.enter_context(nc.semaphore("counts_zeroed"))

        with ExitStack() as early:
            sbe = lambda n, s, d: early.enter_context(nc.sbuf_tensor(n, s, d))
            mem.xk = sbe("x_keep", [P, TILES, D], F32)
            mem.ci = sbe("const_i", [P, 1 + GROUP + 2 * P], I32)
            mem.bit_mask, mem.dummy = mem.ci[:, 0:1], mem.ci[:, 1:1 + GROUP]
            mem.pad_and, mem.pad_or = (mem.ci[:, 1 + GROUP + k * P:1 + GROUP + (k + 1) * P] for k in range(2))
            mem.zeros = sbe("zeros", [P, 7 * CHUNK], F32)
            mem.zero_bf = sbe("zero_bf", [P, P], BF16)
            mem.cell_col = sbe("cell_col", [P, ETILES * P], I32)
            mem.dup_mask_dram = a["const_f"][:, 3 * P + 1:]
            index_stage(nc, mem, a["src"], a["dst"])
            mix_stage(nc, mem, {k: a["L0_mix_" + k] for k in ("wq", "wk", "wv", "wo", "bo", "ln_k_g", "ln_k_b", "ln_v_g", "ln_v_b")})
            scatter_stage(nc, mem)
        largest_degree(nc, mem)
        with ExitStack() as mid:
            sbm = lambda n, s, d: mid.enter_context(nc.sbuf_tensor(n, s, d))
            mem.h_hi, mem.h_lo = (sbm(n, [P, TILES, D], F32R) for n in ("h_hi", "h_lo"))
            mem.slot = [sbm(f"counts_slot{k}", [P, 5 * CHUNK], F32R) for k in range(SLOTS)]
            for layer in range(LAYERS):
                gnn_layer(nc, mem, layer, {k: a["L0_gnn_" + k] for k in ("Wl", "Wr", "rvar", "gamma", "b", "rmean", "beta")})
        with ExitStack() as late:
            sbl = lambda n, s, d: late.enter_context(nc.sbuf_tensor(n, s, d))
            seml = lambda n: late.enter_context(nc.semaphore(n))
            mem.w1 = sbl("w1", [P, E, HALVES, FF], F32)
            mem.mean, mem.rstd = sbl("ffn_mean", [P, TILES], F32), sbl("ffn_rstd", [P, TILES], F32)
            mem.gates, mem.weigh, mem.slots = sbl("gates", [P, 2, TILES], F32), sbl("weigh", [P, TILES, E], F32), sbl("slots", [P, TILES, 2], I32)
            mem.tile_expert, mem.rank_i = sbl("tile_expert", [1, XT], I32), sbl("rank_i", [P, E], I32)
            mem.part_in = [seml(f"xm_in{k}") for k in range(5)]
            mem.w1_in, mem.w2_in, mem.b1_in = seml("w1_in"), seml("w2_in"), seml("b1_in")
            f = {k: a["L0_ffn_" + k] for k in ("gate_w", "gate_b", "w1", "b1", "w2", "b2", "gamma", "beta")}
            router_stage(nc, mem, f)
            with ExitStack() as experts:
                sbx = lambda n, s, d: experts.enter_context(nc.sbuf_tensor(n, s, d))
                mem.w2 = sbx("w2", [P, E, FF // P, D], F32)
                mem.b1_rows, mem.b1T = sbx("b1_rows", [E * FF // P, P], F32), sbx("b1T", [P, E * FF // P], F32)
                dispatch_stage(nc, mem, f)
                expert_stage(nc, mem)
            combine_stage(nc, mem, f, out)


INPUTS = ["x", "src", "dst"] + ["L0_gnn_" + k for k in ("mask_embed", "Wl", "Wr", "b", "gamma", "beta", "rmean", "rvar")] \
    + ["L0_mix_" + k for k in ("wq", "wk", "wv", "wo", "bo", "ln_k_g", "ln_k_b", "ln_v_g", "ln_v_b")] \
    + ["L0_ffn_" + k for k in ("gate_w", "gate_b", "w1", "b1", "w2", "b2", "gamma", "beta")]


def constants(np):
    p = np.arange(P)
    ident = np.eye(P, dtype=np.float32)
    iota = np.broadcast_to(p.astype(np.float32), (P, P))
    tri = (p[:, None] < p[None, :]).astype(np.float32)
    dup = np.concatenate([np.ones((P, (GROUP - 1) * P), np.float32), tri.T], axis=1)
    const_f = np.ascontiguousarray(np.concatenate([ident, iota, tri, (p < TAIL)[:, None], dup], axis=1), dtype=np.float32)
    bit = (np.uint32(1) << (p % 32).astype(np.uint32)).view(np.int32)[:, None]
    dummy = DUMMY + np.arange(GROUP)[None, :] * P + p[:, None]
    edge = (ETILES - 1) * P * P + np.arange(P * P).reshape(P, P)
    pad = edge >= EDGES
    pad_and = np.where(pad, 0, -1)
    pad_or = np.where(pad, (DUMMY + GROUP * P + (edge - EDGES) % (GROUP * P)) | TAG, 0)
    const_i = np.ascontiguousarray(np.concatenate([bit, dummy, pad_and, pad_or], axis=1).astype(np.int32))
    return {"const_f": const_f, "const_i": const_i}


def kernel(**inputs):
    import numpy as np
    import concourse.bacc as bacc
    from concourse.bass_utils import run_bass_kernel_spmd

    nc = bacc.Bacc("TRN2", target_bir_lowering=False, num_devices=1)
    arrays, a = {}, {}
    for name, value in list({k: inputs[k] for k in INPUTS}.items()) + list(constants(np).items()):
        value = np.ascontiguousarray(value)
        arrays[f"in_{name}"] = value
        a[name] = nc.dram_tensor(f"in_{name}", value.shape, mybir.dt.from_np(value.dtype), kind="ExternalInput").ap()
    out = nc.dram_tensor("out_rows", (N, D), F32, kind="ExternalOutput").ap()
    program(nc, a, out)
    return run_bass_kernel_spmd(nc, [arrays], core_ids=[0]).results[0]["out_rows"]
```

```python
from contextlib import ExitStack, contextmanager

import concourse.bass as bass
from concourse import mybir

F32, F32R, BF16 = mybir.dt.float32, mybir.dt.float32r, mybir.dt.bfloat16
I32 = mybir.dt.int32
U32 = mybir.dt.uint32
ALU = mybir.AluOpType
ACT = mybir.ActivationFunctionType
X_AXIS = mybir.AxisListType.X

P = 128
N, D, EDGES, LAYERS = 6250, 256, 200000, 3
HALVES = D // P
TILES = -(-N // P)
FULL = TILES - 1
TAIL = N - FULL * P
EPS = 1e-5

CHUNK = 512
CHUNKS = N // CHUNK
PART_BITS, TILE_BITS, COL_BITS = 7, 6, 9
CELL_CHUNK = 1 << (PART_BITS + TILE_BITS + COL_BITS)
GROUP = 8
QUADS = 4
ECHUNKS = -(-EDGES // P)
ITERS = -(-ECHUNKS // (GROUP * QUADS))
ECOLS = ITERS * GROUP * QUADS
ETILES = -(-ECOLS // P)
DUMMY = (CHUNKS + 1) * CELL_CHUNK
CELLS = DUMMY + 2 * GROUP * P
TAG = 0x20000000
CREDIT = 1
EXACT = 4096

BATCHES = 12
SLOTS = 4
HEADS, HEAD = 4, 64
E, FF = 16, 512
XT = (2 * N + E * (P - 1)) // P


def batch_tiles(b):
    return (4 * b, 4 if b < BATCHES - 1 else TILES - 4 * (BATCHES - 1))


@contextmanager
def stage_semaphores(nc):
    taken = []

    def sem(name):
        taken.append(nc.alloc_semaphore(name))
        return taken[-1]

    yield sem
    nc.clear_and_free_semaphores(taken)
    nc.all_engine_barrier()


class Steps:

    def __init__(self, eng, sem):
        self.eng, self.sem, self.base, self.k, self.at = eng, sem, 0, 0, 0

    def loop(self, n, per):
        self.base, self.at, self.k = self.base + self.k, n * per, 0

    def end(self, per, times):
        assert self.k == per, (self.k, per)
        self.base, self.at, self.k = self.base + per * times, 0, 0

    def __call__(self, ins):
        self.k += 1
        ins.then_inc(self.sem, 1)
        self.eng.wait_ge(self.sem, self.at + (self.base + self.k))


class Count:

    def __init__(self, n, c):
        self.n, self.c = n, c

    def __add__(self, k):
        return Count(self.n, self.c + k)

    def value(self, times=1, over=1):
        c = times * (self.c // over)
        return c if self.n is None else self.n * (4 // over * times) + c

    def slot(self, k):
        return self.c % k

    def exists(self, last):
        return self.n is not None or 0 <= self.c < last


def after(eng, sem, count, times=1, over=1):
    v = count.value(times, over)
    if count.n is not None or v > 0:
        eng.wait_ge(sem, v)


def four_steps(eng, first, last, peel, body):
    n_loop = (last - first + 1 - 2 * peel) // 4
    for t in range(first, first + peel):
        body(Count(None, t))
    with eng.Fori(0, n_loop) as n:
        for j in range(4):
            body(Count(n, first + peel + j))
    for t in range(first + peel + 4 * n_loop, last + 1):
        body(Count(None, t))


class StepCount:

    def __init__(self, eng, sem, per, first):
        self.eng, self.sem, self.per, self.first = eng, sem, per, first

    def begin(self, t):
        self.at, self.k = (t + -self.first).value(times=self.per), 0

    def issue(self, ins):
        self.k += 1
        ins.then_inc(self.sem, 1)

    def __call__(self, ins):
        self.issue(ins)
        self.eng.wait_ge(self.sem, self.at + self.k)

    def finish(self):
        if self.k < self.per:
            self.eng.sem_inc(self.sem, self.per - self.k)


def rows(ap):
    return ap[0:FULL * P, :].rearrange("(t p) w -> p t w", p=P)


def index_stage(nc, mem, src, dst):
    with ExitStack() as ctx:
        sb = lambda n, s, d: ctx.enter_context(nc.sbuf_tensor(n, s, d))
        sem = ctx.enter_context(stage_semaphores(nc))
        s_sb, d_sb = sb("src_rows", [P, ETILES, P], I32), sb("dst_rows", [P, ETILES, P], I32)
        a2, a3 = sb("cell_tile", [P, ETILES, P], I32), sb("cell_chunk", [P, ETILES, P], I32)
        cleared, loaded, own, cells_ready = sem("edges_cleared"), sem("edges_loaded"), sem("index_own"), sem("cells_ready")
        stored, flipped, const_in = sem("cells_stored"), sem("cells_flipped"), sem("const_in")
        x_in, moved, pool_set = sem("x_in"), sem("x_pad_set"), sem("pool_set")
        full = EDGES // (P * P)
        rest = EDGES - full * P * P
        rrows, rcols = rest // P, rest % P
        with nc.Block() as block:
            @block.sync
            def _(sp):
                sp.dma_start(mem.cf[:], mem.cf_dram).then_inc(const_in, 16)
                sp.dma_start(mem.ci[:], mem.ci_dram).then_inc(const_in, 16)
                sp.wait_ge(cleared, 2)
                for t, a in ((s_sb, src), (d_sb, dst)):
                    sp.dma_start(t[:, 0:full, :], a[0:full * P * P].rearrange("(i q p) -> q i p", q=P, p=P)).then_inc(loaded, 16)
                    sp.dma_start(t[0:rrows, full, :], a[full * P * P:full * P * P + rrows * P].rearrange("(q p) -> q p", p=P)).then_inc(loaded, 16)
                    sp.dma_start(t[rrows:rrows + 1, full, 0:rcols], a[EDGES - rcols:EDGES].rearrange("(q p) -> q p", q=1)).then_inc(loaded, 16)
                sp.wait_ge(moved, 1)
                for k in range(4):
                    m = FULL // 4
                    sp.dma_start(mem.xk[:, k * m:(k + 1) * m, :], rows(mem.x)[:, k * m:(k + 1) * m, :]).then_inc(x_in, 16)
                sp.dma_start(mem.xk[0:TAIL, FULL, :], mem.x[FULL * P:N, :]).then_inc(x_in, 16)
                sp.wait_ge(cells_ready, 1)
                store = mem.cells_dram.rearrange("(i q p) -> q i p", q=P, p=P)
                sp.dma_start(store, s_sb[:]).then_inc(stored, 16)
                sp.wait_ge(stored, 16)
                sp.wait_ge(x_in, 80)

            @block.gpsimd
            def _(pool):
                nc.gpsimd.memset(mem.zeros[:], 0.0)
                nc.gpsimd.memset(mem.minus_half[:], -0.5)
                nc.gpsimd.memset(mem.xk[:, FULL, :], 0.0).then_inc(moved, 1)

            @block.vector
            def _(dve):
                step = Steps(dve, own)
                nc.vector.memset(s_sb[:, full, :], 0).then_inc(cleared, 1)
                nc.vector.memset(d_sb[:, full, :], 0).then_inc(cleared, 1)
                dve.wait_ge(const_in, 32)
                dve.wait_ge(loaded, 96)
                nc.vector.tensor_scalar(a2[:], s_sb[:], PART_BITS, COL_BITS, ALU.logical_shift_right, ALU.logical_shift_left)
                nc.vector.tensor_scalar(a3[:], d_sb[:], COL_BITS, PART_BITS + TILE_BITS + COL_BITS, ALU.logical_shift_right, ALU.logical_shift_left)
                nc.vector.tensor_scalar(d_sb[:], d_sb[:], CHUNK - 1, TAG, ALU.bitwise_and, ALU.bitwise_or)
                step(nc.vector.tensor_scalar(s_sb[:], s_sb[:], P - 1, TILE_BITS + COL_BITS, ALU.bitwise_and, ALU.logical_shift_left))
                step(nc.vector.tensor_tensor(a2[:], a2[:], a3[:], ALU.bitwise_or))
                step(nc.vector.tensor_tensor(a2[:], a2[:], d_sb[:], ALU.bitwise_or))
                step(nc.vector.tensor_tensor(s_sb[:], s_sb[:], a2[:], ALU.bitwise_or))
                step(nc.vector.tensor_tensor(s_sb[:, full, :], s_sb[:, full, :], mem.pad_and, ALU.bitwise_and))
                nc.vector.tensor_tensor(s_sb[:, full, :], s_sb[:, full, :], mem.pad_or, ALU.bitwise_or).then_inc(cells_ready, 1)
                for i in range(ETILES):
                    if i % 4 == 0:
                        dve.wait_ge(flipped, i // 4 + 1)
                    nc.vector.tensor_scalar(mem.cell_col[:, i * P:(i + 1) * P], mem.bank[i // 4][:, (i % 4) * P:(i % 4 + 1) * P].bitcast(I32),
                                            TAG, None, ALU.bitwise_xor)

            @block.tensor
            def _(pe):
                pe.wait_ge(cells_ready, 1)
                for i in range(ETILES):
                    last = nc.tensor.transpose(mem.bank[i // 4][:, (i % 4) * P:(i % 4 + 1) * P], s_sb[:, i, :].bitcast(F32), mem.ident)
                    if i % 4 == 3 or i == ETILES - 1:
                        last.then_inc(flipped, 1)


def mix_stage(nc, mem, w):
    with ExitStack() as ctx:
        sb = lambda n, s, d: ctx.enter_context(nc.sbuf_tensor(n, s, d))
        sem = ctx.enter_context(stage_semaphores(nc))
        bank, h, xk, ident = mem.bank, mem.h, mem.xk, mem.ident
        raw = [sb(f"raw_{n}", [P, HALVES, D], F32) for n in ("wk", "wv", "wo")]
        wq = sb("wq_sb", [P, HALVES, D], F32)
        wkv, woT = sb("wkv", [P, HALVES, 2 * D], F32), sb("woT", [P, HALVES, D], F32)
        w_mean = sb("w_mean", [P, HALVES, 2 * HEADS], F32)
        k_gain, k_shift = sb("k_gain", [P, HEAD], F32), sb("k_shift", [P, HEAD], F32)
        v_col = sb("v_gain_shift", [P, 2], F32)
        bo_row, ones_row = sb("bo_row", [1, D], F32), sb("ones_row", [1, P], F32)
        stats = sb("ln_stats", [P, TILES, 6], F32)
        mean, rstd, tmp = sb("ln_mean", [P, TILES], F32), sb("ln_rstd", [P, TILES], F32), sb("ln_tmp", [P, TILES], F32)
        xs, xT = sb("xs", [P, 4, D], F32), sb("xT", [P, 2, D], F32)
        sq, kvn = sb("sq", [P, 2, 2 * D], F32), sb("kvn", [P, 2, 2 * HALVES, P + 1], F32)
        hs = sb("head_var_rstd", [P, 4, 2 * HEADS], F32)
        V, K_COL = 200, 400
        sums, k_sum, k_row = sb("kv_sums", [P, K_COL + HALVES], F32), sb("k_sum_wide", [P, HALVES, P], F32), sb("k_part", [P, HALVES, P], F32)
        v_part = sb("v_part", [P, HALVES], F32)
        kvb, tq, m_sb = sb("kv_blocks", [P, HALVES, P], F32), sb("kv_wo", [P, HALVES, D], F32), sb("mix_w", [P, HALVES, D], F32)
        w_in, b_in, own, wT, wTd = sem("mixw_in"), sem("mixb_in"), sem("mix_own"), sem("mixw_T"), sem("mixw_Td")
        xs_ready, xs_flipped, xT_ready, kv_ps, sq_ready, own_tiles = (sem(n) for n in ("xs_ready", "xs_flipped", "xT_ready", "kv_ps", "sq_ready", "own_tiles"))
        kvn_ready, kv_added, zero_kv, k_sum_ready, k_sum_flipped = (sem(n) for n in ("kvn_ready", "kv_added", "zero_kv", "k_sum_ready", "k_sum_flipped"))
        kvb_ready, tq_ps, tq_ready, m_ps, m_ready, act_h = (sem(n) for n in ("kvb_ready", "tq_ps", "tq_ready", "m_ps", "m_ready", "act_h"))
        stats_done = sem("stats_done")
        var_ready, rstd_ready, head_var, head_rstd = (sem(n) for n in ("var_ready", "rstd_ready", "head_var", "head_rstd"))
        mixed, mix_read, xs2, fl2, xt2 = (sem(n) for n in ("mixed", "mix_read", "xs_again", "xs_flipped_again", "xT_again"))
        kv_bank = [bank[k] for k in (0, 1, 5, 6)]
        B_LOADS = 7

        def first_pass(eng, body):
            four_steps(eng, -3, TILES + 1, 6, body)

        def second_pass(eng, body):
            four_steps(eng, -2, TILES - 1, 4, body)

        with nc.Block() as block:
            @block.sync
            def _(sp):
                for t, n in zip(raw + [wq], ("wk", "wv", "wo", "wq")):
                    sp.dma_start(t[:], w[n].rearrange("(a p) d -> p a d", p=P)).then_inc(w_in, 16)
                sp.dma_start(k_gain[:], w["ln_k_g"].partition_broadcast(P)).then_inc(b_in, 16)
                sp.dma_start(k_shift[:], w["ln_k_b"].partition_broadcast(P)).then_inc(b_in, 16)
                for b in range(P // HEAD):
                    for k, n in enumerate(("ln_v_g", "ln_v_b")):
                        sp.dma_start(v_col[b * HEAD:(b + 1) * HEAD, k:k + 1], w[n].rearrange("(p o) -> p o", o=1)).then_inc(b_in, 16)
                sp.dma_start(bo_row[:], w["bo"].rearrange("(o d) -> o d", o=1)).then_inc(b_in, 16)
                sp.wait_ge(b_in, 16 * B_LOADS)

            @block.tensor
            def _(pe):
                pe.wait_ge(w_in, 64)
                for i, t in enumerate(raw):
                    for a in range(HALVES):
                        for b in range(HALVES):
                            last = nc.tensor.transpose(bank[i][:, (b * HALVES + a) * P:(b * HALVES + a + 1) * P], t[:, a, b * P:(b + 1) * P], ident)
                    last.then_inc(wT, 1)
                nc.tensor.matmul(bank[7][:, 0:K_COL + HALVES], mem.zeros[:, 0:P], mem.zeros[:, 0:K_COL + HALVES], start=True, stop=False, skip_group_check=True)
                pe.wait_ge(wTd, 4)

                def flip(u):
                    after(pe, xs_ready, u + 1)
                    after(pe, xT_ready, u + -1)
                    for a in range(HALVES):
                        last = nc.tensor.transpose(bank[3 + u.slot(2)][:, a * P:(a + 1) * P], xs[:, u.slot(4), a * P:(a + 1) * P], ident)
                    last.then_inc(xs_flipped, 1)

                def product(u):
                    after(pe, xT_ready, u + 1)
                    after(pe, kvn_ready, u + -3)
                    for a in range(HALVES):
                        last = nc.tensor.matmul(kv_bank[u.slot(4)][:, :], xT[:, u.slot(2), a * P:(a + 1) * P], wkv[:, a, :], start=(a == 0), stop=(a == HALVES - 1))
                    last.then_inc(kv_ps, 1)

                def add(u):
                    tail = u.n is None and u.c == FULL
                    r, j = TAIL if tail else P, u.slot(2)
                    after(pe, kvn_ready, u + 1)
                    for a in range(HALVES):
                        nc.tensor.matmul(bank[7][:, a * V:a * V + P + 1], kvn[0:r, j, HALVES + a, 0:P], kvn[0:r, j, a, :],
                                         start=False, stop=tail, skip_group_check=True)
                        last = nc.tensor.matmul(bank[7][:, K_COL + a:K_COL + a + 1], kvn[0:r, j, a, 0:P], kvn[0:r, j, a, P:P + 1],
                                                start=False, stop=tail, skip_group_check=True)
                    last.then_inc(kv_added, 1)

                pe.wait_ge(zero_kv, 3)

                def step(t):
                    if (t + 2).exists(TILES):
                        flip(t + 2)
                    if (t + 1).exists(TILES):
                        product(t + 1)
                    if (t + -2).exists(TILES):
                        add(t + -2)

                first_pass(pe, step)
                pe.wait_ge(k_sum_ready, 1)
                for a in range(HALVES):
                    last = nc.tensor.matmul(bank[2][:, a * P:(a + 1) * P], k_sum[:, a, :], ident, start=True, stop=True)
                last.then_inc(k_sum_flipped, 1)
                pe.wait_ge(kvb_ready, 1)
                for a in range(HALVES):
                    last = nc.tensor.matmul(bank[a][:, 0:D], kvb[:, a, :], woT[:, a, :], start=True, stop=True)
                last.then_inc(tq_ps, 1)
                pe.wait_ge(tq_ready, 1)
                for i in range(HALVES):
                    for a in range(HALVES):
                        last = nc.tensor.matmul(bank[3 + i][:, 0:D], wq[:, a, i * P:(i + 1) * P], tq[:, a, :], start=(a == 0), stop=(a == HALVES - 1))
                last.then_inc(m_ps, 1)
                pe.wait_ge(m_ready, 1)

                def flip_again(u):
                    after(pe, xs2, u + 1)
                    after(pe, xt2, u + -1)
                    for a in range(HALVES):
                        last = nc.tensor.transpose(bank[3 + u.slot(2)][:, a * P:(a + 1) * P], xs[:, u.slot(4), a * P:(a + 1) * P], ident)
                    last.then_inc(fl2, 1)

                def mix(u):
                    after(pe, xt2, u + 1)
                    after(pe, mix_read, u + -1)
                    to = bank[5 + u.slot(2)][:, 0:D]
                    nc.tensor.matmul(to, ones_row[:], bo_row[:], start=True, stop=False)
                    for a in range(HALVES):
                        last = nc.tensor.matmul(to, xT[:, u.slot(2), a * P:(a + 1) * P], m_sb[:, a, :], start=False, stop=(a == HALVES - 1))
                    last.then_inc(mixed, 1)

                def step(t):
                    if (t + 1).exists(TILES):
                        flip_again(t + 1)
                    if t.exists(TILES):
                        mix(t)

                second_pass(pe, step)

            @block.scalar
            def _(act):
                act.wait_ge(w_in, 64)
                act.wait_ge(b_in, 16 * B_LOADS)
                for c in range(CHUNKS):
                    dest = mem.counts[c * CELL_CHUNK:(c + 1) * CELL_CHUNK].rearrange("(p s) -> p s", p=P)
                    act.dma_start(dest[:, 0:TILES * CHUNK].rearrange("p (r m) -> p r m", r=7),
                                  mem.zeros[:].rearrange("p (r m) -> p r m", r=1).to_broadcast([P, 7, 7 * CHUNK])).then_inc(mem.counts_zeroed, 16)
                dest = mem.counts[CHUNKS * CELL_CHUNK:(CHUNKS + 1) * CELL_CHUNK].rearrange("(p s j) -> p s j", p=P, j=CHUNK)
                act.dma_start(dest[:, 0:28, 0:P], mem.zeros[:].rearrange("p (s j) -> p s j", j=P)).then_inc(mem.counts_zeroed, 16)
                act.dma_start(dest[:, 28:TILES, 0:P], mem.zeros[:, 0:21 * P].rearrange("p (s j) -> p s j", j=P)).then_inc(mem.counts_zeroed, 16)
                act.dma_start(mem.counts[DUMMY:DUMMY + 2 * GROUP * P].rearrange("(p s) -> p s", p=P), mem.zeros[:, 0:2 * GROUP]).then_inc(mem.counts_zeroed, 16)

                def keep(u):
                    after(act, xs_ready, u + 1)
                    nc.scalar.copy(h[:, u.value(), :], xs[:, u.slot(4), :]).then_inc(act_h, 1)

                def flip_out(u):
                    after(act, xs_flipped, u + 1)
                    after(act, kv_ps, u + -1)
                    nc.scalar.copy(xT[:, u.slot(2), :], bank[3 + u.slot(2)][:, 0:D]).then_inc(xT_ready, 1)

                def square(u):
                    after(act, kv_ps, u + 1)
                    after(act, head_var, u + -1)
                    nc.scalar.activation(sq[:, u.slot(2), :], kv_bank[u.slot(4)][:, :], ACT.Square).then_inc(sq_ready, 1)

                def step(t):
                    if (t + 2).exists(TILES):
                        flip_out(t + 2)
                        keep(t + 2)
                    if (t + 1).exists(TILES):
                        square(t + 1)

                first_pass(act, step)
                act.wait_ge(act_h, TILES)
                act.wait_ge(m_ready, 1)

                def again(u):
                    after(act, fl2, u + -3)
                    nc.scalar.copy(xs[:, u.slot(4), :], h[:, u.value(), :]).then_inc(xs2, 1)

                def out(u):
                    after(act, fl2, u + 1)
                    after(act, mixed, u + -1)
                    nc.scalar.copy(xT[:, u.slot(2), :], bank[3 + u.slot(2)][:, 0:D]).then_inc(xt2, 1)

                def step(t):
                    if (t + 2).exists(TILES):
                        again(t + 2)
                    if (t + 1).exists(TILES):
                        out(t + 1)

                second_pass(act, step)

            @block.gpsimd
            def _(pool):
                nc.gpsimd.memset(kvn[:], 1.0).then_inc(zero_kv, 1)
                nc.gpsimd.memset(kvb[:], 0.0).then_inc(zero_kv, 1)
                nc.gpsimd.memset(ones_row[:], 1.0).then_inc(zero_kv, 1)
                pool.wait_ge(var_ready, 1)
                power(nc, mem, rstd[:], TILES).then_inc(rstd_ready, 1)

                def step(t):
                    if t.exists(TILES):
                        after(pool, head_var, t + 1)
                        power(nc, mem, hs[:, t.slot(4), :], 2 * HEADS).then_inc(head_rstd, 1)

                first_pass(pool, step)

            @block.vector
            def _(dve):
                step1 = Steps(dve, own)
                with dve.Fori(0, TILES) as n:
                    nc.vector.bn_stats(stats[:, n, :], xk[:, n, :]).then_inc(stats_done, 1)
                dve.wait_ge(stats_done, TILES)
                ln_rows(nc, dve, step1, stats, mean, rstd, tmp, var_ready, rstd_ready)
                for i in range(3):
                    dve.wait_ge(wT, i + 1)
                    dest = woT[:] if i == 2 else wkv[:, :, i * D:(i + 1) * D]
                    nc.vector.tensor_copy(dest, bank[i][:].rearrange("p (b c) -> p b c", b=HALVES)).then_inc(wTd, 1)
                dve.wait_ge(wTd, 3)
                heads = wkv[:].rearrange("p a (g d) -> p (a g) d", d=HEAD)
                means = w_mean[:].rearrange("p a g -> p (a g)")
                step1(nc.vector.tensor_reduce(means, heads, X_AXIS, ALU.add))
                step1(nc.vector.tensor_scalar(means, means, 1.0 / HEAD, None, ALU.mult))
                nc.vector.tensor_tensor(heads, heads, means.rearrange("p (g o) -> p g o", o=1).to_broadcast([P, HALVES * 2 * HEADS, HEAD]), ALU.subtract).then_inc(wTd, 1)
                dve.wait_ge(zero_kv, 2)
                own_step = StepCount(dve, own_tiles, 1, -3)

                def normalise(u):
                    t = u.value()
                    after(dve, xs_flipped, u + -3)
                    after(dve, act_h, u + -3)
                    nc.vector.tensor_scalar(xs[:, u.slot(4), :], xk[:, t, :], mean[:, bass.ds(t, 1)], rstd[:, bass.ds(t, 1)], ALU.subtract, ALU.mult).then_inc(xs_ready, 1)

                def scale(u):
                    after(dve, head_rstd, u + 1)
                    after(dve, kv_added, u + -1)
                    blocks = lambda ap: ap.rearrange("p (b h d) -> p b h d", b=2 * HALVES, d=HEAD)
                    factor = hs[:, u.slot(4), :].rearrange("p (b h o) -> p b h o", b=2 * HALVES, o=1).to_broadcast([P, 2 * HALVES, P // HEAD, HEAD])
                    nc.vector.tensor_tensor(kvn[:, u.slot(2), :, 0:P].rearrange("p b (h d) -> p b h d", d=HEAD),
                                            blocks(kv_bank[u.slot(4)][:, :]), factor, ALU.mult).then_inc(kvn_ready, 1)

                def step(t):
                    own_step.begin(t)
                    if (t + 3).exists(TILES):
                        normalise(t + 3)
                    v = hs[:, t.slot(4), :]
                    if t.exists(TILES):
                        after(dve, sq_ready, t + 1)
                        own_step.issue(nc.vector.tensor_reduce(v, sq[:, t.slot(2), :].rearrange("p (g d) -> p g d", d=HEAD), X_AXIS, ALU.add))
                    if (t + -1).exists(TILES):
                        scale(t + -1)
                    if t.exists(TILES):
                        dve.wait_ge(own_tiles, own_step.at + own_step.k)
                        nc.vector.tensor_scalar(v, v, 1.0 / HEAD, EPS, ALU.mult, ALU.add).then_inc(head_var, 1)
                    own_step.finish()

                first_pass(dve, step)
                dve.wait_ge(kv_added, TILES)
                dve.wait_ge(b_in, 16 * B_LOADS)
                step1(nc.vector.tensor_copy(sums[:], bank[7][:, 0:K_COL + HALVES]))
                nc.vector.tensor_copy(k_sum[:], sums[:, K_COL:K_COL + HALVES].rearrange("p (a o) -> p a o", o=1).to_broadcast([P, HALVES, P])).then_inc(k_sum_ready, 1)
                step1(nc.vector.tensor_scalar(v_part[:], v_col[:, 1:2].to_broadcast([P, HALVES]), float(N), None, ALU.mult))
                for a in range(HALVES):
                    last = nc.vector.scalar_tensor_tensor(out=v_part[:, a:a + 1], in0=sums[:, a * V + P:a * V + P + 1], scalar=v_col[:, 0:1], in1=v_part[:, a:a + 1], op0=ALU.mult, op1=ALU.add)
                step1(last)
                dve.wait_ge(k_sum_flipped, 1)
                blocks = [(slice(b * HEAD, (b + 1) * HEAD), a) for a in range(HALVES) for b in range(P // HEAD)]
                for r, a in blocks:
                    last = nc.vector.scalar_tensor_tensor(out=k_row[r, a, 0:HEAD], in0=bank[2][r, a * P + r.start:a * P + r.stop], scalar=v_col[r, 1:2], in1=k_gain[r, :], op0=ALU.mult, op1=ALU.mult)
                for r, a in blocks:
                    last = nc.vector.scalar_tensor_tensor(out=kvb[r, a, r], in0=sums[r, a * V + r.start:a * V + r.stop], scalar=v_col[r, 0:1], in1=k_gain[r, :], op0=ALU.mult, op1=ALU.mult)
                step1(last)
                for r, a in blocks:
                    last = nc.vector.scalar_tensor_tensor(out=kvb[r, a, r], in0=k_shift[r, :], scalar=v_part[r, a:a + 1], in1=kvb[r, a, r], op0=ALU.mult, op1=ALU.add)
                step1(last)
                for r, a in blocks:
                    last = nc.vector.tensor_tensor(kvb[r, a, r], kvb[r, a, r], k_row[r, a, 0:HEAD], ALU.add)
                step1(last)
                nc.vector.tensor_scalar(kvb[:], kvb[:], 1.0 / N, None, ALU.mult).then_inc(kvb_ready, 1)
                dve.wait_ge(tq_ps, 1)
                for a in range(HALVES):
                    last = nc.vector.tensor_copy(tq[:, a, :], bank[a][:, 0:D])
                last.then_inc(tq_ready, 1)
                dve.wait_ge(m_ps, 1)
                for a in range(HALVES):
                    last = nc.vector.tensor_copy(m_sb[:, a, :], bank[3 + a][:, 0:D])
                last.then_inc(m_ready, 1)

                def step(t):
                    if t.exists(TILES):
                        after(dve, mixed, t + 1)
                        x = xk[:, t.value(), :]
                        nc.vector.tensor_tensor(x, bank[5 + t.slot(2)][:, 0:D], x, ALU.add).then_inc(mix_read, 1)

                second_pass(dve, step)


def ln_rows(nc, dve, step, stats, mean, rstd, tmp, var_ready, rstd_ready, width=D):
    m_e, m_o, v_e, v_o = (stats[:, :, k] for k in (1, 4, 2, 5))
    step(nc.vector.tensor_tensor(mean[:], m_e, m_o, ALU.add))
    step(nc.vector.tensor_tensor(tmp[:], m_e, m_o, ALU.subtract))
    step(nc.vector.tensor_scalar(mean[:], mean[:], 0.5, None, ALU.mult))
    step(nc.vector.tensor_tensor(tmp[:], tmp[:], tmp[:], ALU.mult))
    step(nc.vector.tensor_tensor(rstd[:], v_e, v_o, ALU.add))
    step(nc.vector.tensor_scalar(tmp[:], tmp[:], 0.25, EPS, ALU.mult, ALU.add))
    nc.vector.scalar_tensor_tensor(out=rstd[:], in0=rstd[:], scalar=1.0 / width, in1=tmp[:], op0=ALU.mult, op1=ALU.add).then_inc(var_ready, 1)
    dve.wait_ge(rstd_ready, 1)


def power(nc, mem, ap, width):
    return nc.gpsimd.tensor_tensor(ap, ap, mem.minus_half[:].to_broadcast([P, width]), ALU.pow)


def scatter_stage(nc, mem):
    with ExitStack() as ctx:
        sb = lambda n, s, d: ctx.enter_context(nc.sbuf_tensor(n, s, d))
        sem = ctx.enter_context(stage_semaphores(nc))
        bank = mem.bank
        key_rows, key_bits = sb("key_rows", [P, GROUP * P], I32), sb("key_bits", [P, GROUP * P], BF16)
        masked = sb("key_masked", [P, GROUP * P], I32)
        dup_f, dup_in = sb("dup_mask_f", [P, GROUP * P], F32), sem("dup_mask_in")
        dup_mask = sb("dup_mask", [P, GROUP * P], BF16)
        equal = sb("equal", [P, 4, GROUP * P], BF16)
        value = sb("cell_value", [P, QUADS, GROUP], F32)
        earlier, is_dup = sb("earlier", [P, QUADS, GROUP], F32), sb("is_dup", [P, QUADS, GROUP], I32)
        cell = sb("cell_slot", [P, QUADS, GROUP], I32)
        lane, tile_no, bits_a, bits_b = (sb(n, [P, ETILES * P], F32 if n[:1] == "d" else I32) for n in ("dst_lane", "dst_tile", "bits_a", "bits_b"))
        iota = sb("iota_f", [P, P], F32)
        hot_lane, hot_tile = sb("hot_lane", [P, QUADS, GROUP, P], BF16), sb("hot_tile", [P, QUADS, GROUP, TILES], BF16)
        bias15 = sb("bias15", [P, 1], F32)
        keys_in, bits_ready, own, cleared = sem("keys_in"), sem("bits_ready"), sem("scatter_own"), sem("hot_cleared")
        dots, equals, dups, cells_set, retired, hots, hots_used = (
            sem(n) for n in ("dots", "equals", "dups", "cells_set", "groups_retired", "hots", "hots_used"))
        own_turns, own_turns_pool = sem("own_turns"), sem("own_turns_pool")
        scattered, deg_done, masked_done, xm_out = sem("scattered"), sem("deg_done"), sem("masked_done"), sem("xm_out")
        GQ = GROUP * QUADS
        pair = lambda k: mem.psum[:, 2 * (k % 2) * 512:(2 * (k % 2) + 2) * 512]
        deg_ps = bank[4][:, 0:TILES]

        with nc.Block() as block:
            @block.sync
            def _(sp):
                rows4 = mem.cells_dram[0:ITERS * GQ * P].rearrange("(n q m) -> n q m", q=QUADS, m=GROUP * P)
                sp.dma_start(dup_f[:], mem.dup_mask_dram).then_inc(dup_in, 16)
                sp.dma_start(rows(mem.xm_dram), mem.xk[:, 0:FULL, :]).then_inc(xm_out, 16)
                sp.dma_start(mem.xm_dram[FULL * P:N, :], mem.xk[0:TAIL, FULL, :]).then_inc(xm_out, 16)
                sp.dma_start(mem.h[0:1, 0, :], mem.mask_embed.rearrange("(o d) -> o d", o=1)).then_inc(xm_out, 16)
                slots = mem.slot_rows.rearrange("(p t) d -> p (t d)", p=P)
                whole = XT * D // (7 * CHUNK)
                sp.dma_start(slots[:, 0:whole * 7 * CHUNK].rearrange("p (r m) -> p r m", r=whole),
                             mem.zeros[:].rearrange("p (r m) -> p r m", r=1).to_broadcast([P, whole, 7 * CHUNK])).then_inc(xm_out, 16)
                sp.dma_start(slots[:, whole * 7 * CHUNK:], mem.zeros[:, 0:XT * D - whole * 7 * CHUNK]).then_inc(xm_out, 16)
                with sp.Fori(0, ITERS) as n:
                    sp.wait_ge(masked_done, n + CREDIT)
                    for q in range(QUADS):
                        sp.dma_start(key_rows[32 * q:32 * q + 32, :], rows4[n][q].partition_broadcast(32)).then_inc(keys_in, 16)
                sp.wait_ge(xm_out, 16 * 5)

            @block.gpsimd
            def _(pool):
                pool.wait_ge(mem.counts_zeroed, 16 * (CHUNKS + 3))
                with pool.Fori(0, ITERS) as n:
                    for q in range(QUADS):
                        pool.wait_ge(cells_set, QUADS * n + q + 1)
                        pool.sem_inc(own_turns_pool, 1)
                        for i in range(GROUP):
                            pool.indirect_dma_start(out=mem.counts_2d, out_offset=bass.IndirectOffsetOnAxis(ap=cell[:, q, i:i + 1], axis=0),
                                                    in_=value[:, q, i:i + 1], in_offset=None, compute_op=ALU.add).then_inc(scattered, 16)
                        pool.wait_ge(scattered, 16 * GROUP * (QUADS * n + q + 1))
                        pool.sem_inc(retired, 1)

            @block.tensor
            def _(pe):
                pe.sem_inc(dots, CREDIT)
                pe.sem_inc(hots_used, CREDIT)
                pe.wait_ge(cleared, 5)
                nc.tensor.matmul(deg_ps, hot_lane[:, 2, 0, :], hot_tile[:, 2, 0, :], start=True, stop=False, skip_group_check=True)

                def degrees(q):
                    for i in range(GROUP):
                        last = nc.tensor.matmul(deg_ps, hot_lane[:, q, i, :], hot_tile[:, q, i, :], start=False, stop=False, skip_group_check=True)
                    last.then_inc(hots_used, 1)

                with pe.Fori(0, ITERS) as n:
                    pe.wait_ge(bits_ready, n + 1)
                    for q in range(QUADS):
                        for i in range(GROUP):
                            k = GROUP * q + i
                            pe.wait_ge(equals, GQ * n + k + 1)
                            qs = slice(32 * q, 32 * q + 32)
                            for b in range(2):
                                last = nc.tensor.matmul(pair(k)[:, b * 512:(b + 1) * 512], key_bits[qs, i * P:(i + 1) * P],
                                                        key_bits[qs, b * 512:(b + 1) * 512], start=True, stop=True)
                            last.then_inc(dots, 1)
                        pe.wait_ge(hots, QUADS * n + q + 1)
                        degrees((q + 2) % QUADS)
                pe.wait_ge(hots, QUADS * ITERS + 1)
                degrees(2)
                pe.wait_ge(hots, QUADS * ITERS + 2)
                degrees(3)
                nc.tensor.matmul(deg_ps, hot_lane[:, 3, 0, :], mem.zero_bf[:, 0:TILES], start=False, stop=True, skip_group_check=True).then_inc(deg_done, 1)

            @block.scalar
            def _(act):
                act.sem_inc(equals, 2)
                act.wait_ge(cleared, 5)
                with act.Fori(0, ITERS) as n:
                    for q in range(QUADS):
                        act.wait_ge(retired, QUADS * n + q + 1)
                        for i in range(GROUP):
                            k = GROUP * q + i
                            act.wait_ge(dots, GQ * n + k + 1 + CREDIT)
                            act.wait_ge(dups, GQ * n + k + 1)
                            nc.scalar.activation(equal[:, k % 4, :], pair(k), ACT.Relu, bias=bias15[:], scale=2.0,
                                                 accum_out=value[:, q, i:i + 1]).then_inc(equals, 1)

            @block.vector
            def _(dve):
                step = Steps(dve, own)
                dve.sem_inc(dups, 4)
                dve.sem_inc(retired, 4)
                dve.sem_inc(masked_done, CREDIT)
                dve.sem_inc(hots, 2)
                nc.vector.memset(hot_lane[:, 2:4], 0.0).then_inc(cleared, 1)
                nc.vector.memset(hot_tile[:, 2:4], 0.0).then_inc(cleared, 1)
                nc.vector.memset(mem.zero_bf[:], 0.0).then_inc(cleared, 1)
                nc.vector.memset(bias15[:], -15.0).then_inc(cleared, 1)
                step(nc.vector.tensor_copy(iota[:], mem.iota))
                dve.wait_ge(dup_in, 16)
                nc.vector.tensor_copy(dup_mask[:], dup_f[:]).then_inc(cleared, 1)
                cc = mem.cell_col
                nc.vector.tensor_scalar(bits_b[:], cc[:], PART_BITS, 3, ALU.logical_shift_right, ALU.bitwise_and)
                step(nc.vector.tensor_scalar(bits_a[:], cc[:], PART_BITS + TILE_BITS + COL_BITS, 2, ALU.logical_shift_right, ALU.logical_shift_left))
                step(nc.vector.tensor_tensor(bits_a[:], bits_a[:], bits_b[:], ALU.bitwise_or))
                step(nc.vector.tensor_copy(tile_no[:], bits_a[:]))
                step(nc.vector.tensor_scalar(bits_b[:], cc[:], P - 1, None, ALU.bitwise_and))
                step(nc.vector.tensor_copy(lane[:], bits_b[:]))
                with dve.Fori(0, ITERS) as n:
                    step.loop(n, QUADS)
                    dve.wait_ge(keys_in, 64 * n + 64)
                    nc.vector.tensor_tensor(masked[:], key_rows[:], mem.bit_mask.to_broadcast([P, GROUP * P]), ALU.bitwise_and).then_inc(masked_done, 1)
                    dve.wait_ge(masked_done, n + 1 + CREDIT)
                    dve.wait_ge(dots, GQ * n + CREDIT)
                    nc.vector.tensor_scalar(key_bits[:], masked[:], 0.0, 0.5, ALU.not_equal, ALU.subtract).then_inc(bits_ready, 1)
                    for q in range(QUADS):
                        for i in range(GROUP):
                            k = GROUP * q + i
                            dve.wait_ge(equals, GQ * n + k + 3)
                            nc.vector.scalar_tensor_tensor(out=equal[:, k % 4, 0:(i + 1) * P], in0=equal[:, k % 4, 0:(i + 1) * P], scalar=1.0,
                                                           in1=dup_mask[:, (GROUP - 1 - i) * P:], op0=ALU.mult, op1=ALU.mult,
                                                           accum_out=earlier[:, q, i:i + 1]).then_inc(dups, 1)
                        cols = bass.ds(n * GQ + q * GROUP, GROUP)
                        dve.wait_ge(hots_used, QUADS * n + q + CREDIT)
                        flat = lambda t, m: t[:, cols].rearrange("p (g o) -> p g o", o=1).to_broadcast([P, GROUP, m])
                        row = lambda m: iota[:, 0:m].rearrange("p (o j) -> p o j", o=1).to_broadcast([P, GROUP, m])
                        nc.vector.tensor_tensor(hot_lane[:, q], flat(lane, P), row(P), ALU.is_equal)
                        nc.vector.tensor_tensor(hot_tile[:, q], flat(tile_no, TILES), row(TILES), ALU.is_equal).then_inc(hots, 1)
                        dve.wait_ge(dups, GQ * n + GROUP * q + GROUP + 4)
                        dve.wait_ge(retired, QUADS * n + q + 1)
                        nc.vector.tensor_copy(cell[:, q, :], cc[:, cols])
                        step(nc.vector.tensor_scalar(is_dup[:, q, :], earlier[:, q, :], 0.0, None, ALU.is_gt))
                        dve.sem_inc(own_turns, 1)
                        nc.vector.copy_predicated(cell[:, q, :], is_dup[:, q, :], mem.dummy).then_inc(cells_set, 1)
                step.end(QUADS, ITERS)
                dve.wait_ge(deg_done, 1)
                step(nc.vector.tensor_scalar(mem.rdeg[:], deg_ps, 1.0, None, ALU.max))
                step(nc.vector.reduce_max(mem.top[:, 0:1], mem.rdeg[:], X_AXIS))
                nc.vector.reciprocal(mem.rdeg[:], mem.rdeg[:])


def largest_degree(nc, mem):
    with ExitStack() as ctx:
        flipped, topped = (ctx.enter_context(nc.semaphore(n)) for n in ("top_flipped", "topped"))
        with nc.Block() as block:
            @block.tensor
            def _(pe):
                nc.tensor.transpose(mem.bank[0][0:1, 0:P], mem.top[:, 0:1], mem.ident).then_inc(flipped, 1)

            @block.vector
            def _(dve):
                dve.wait_ge(flipped, 1)
                nc.vector.reduce_max(mem.top[0:1, 1:2], mem.bank[0][0:1, 0:P], X_AXIS).then_inc(topped, 1)
                dve.wait_ge(topped, 1)
                nc.vector.tensor_copy(mem.top_int[0:1, 0:1], mem.top[0:1, 1:2])


def gnn_layer(nc, mem, layer, g):
    with ExitStack() as ctx:
        sb = lambda n, s, d: ctx.enter_context(nc.sbuf_tensor(f"{n}_{layer}", s, d))
        new_sem = ctx.enter_context(stage_semaphores(nc))
        sem = lambda n: new_sem(f"{n}_{layer}")
        bank, h, hi, lo = mem.bank, mem.h, mem.h_hi, mem.h_lo
        wl, wr = sb("wl", [P, HALVES, D], F32), sb("wr", [P, HALVES, D], F32)
        bn = sb("bn_rows", [P, 5, D], F32)
        agg, own_rows, hT = sb("agg", [P, HALVES, CHUNK], F32), sb("own_rows", [P, 2, D], F32), sb("hT", [P, 2, HALVES, P], F32)
        z1s = sb("z1", [P, 2, D], F32)
        landed = [sem(f"counts_in{k}") for k in range(SLOTS)]
        split, batch_done, agg_out, copied, flipped, hT_ready = (sem(n) for n in ("h_split", "batch_done", "agg_out", "rows_copied", "rows_flipped", "hT_ready"))
        own, z_ps, z_read, w_in, w_ready, hi_done, z_own = (sem(n) for n in ("bn_own", "z_ps", "z_read", "w_in", "w_ready", "hi_done", "z_own"))

        var_ready, rstd_ready = sem("bn_var_ready"), sem("bn_rstd_ready")
        with nc.Block() as block:
            @block.sync
            def _(sp):
                def load(n, b):
                    s0, m = batch_tiles(b)
                    k = b % SLOTS
                    if isinstance(n, int) and n == CHUNKS:
                        cells = mem.counts[CHUNKS * CELL_CHUNK:(CHUNKS + 1) * CELL_CHUNK].rearrange("(p s j) -> p s j", p=P, j=CHUNK)[:, s0:s0 + m, 0:P]
                        dest = mem.slot[k][:, 0:m * P].rearrange("p (s j) -> p s j", j=P)
                    else:
                        cells = mem.counts[0:CHUNKS * CELL_CHUNK].rearrange("(n p s) -> n p s", n=CHUNKS, p=P)[n][:, s0 * CHUNK:(s0 + m) * CHUNK]
                        dest = mem.slot[k][:, 0:m * CHUNK]
                    sp.dma_start(dest.bitcast(F32), cells).then_inc(landed[k], 16)

                for b in range(SLOTS):
                    load(0, b)
                sp.dma_start(wl[:], g["Wl"][layer].rearrange("(a p) d -> p a d", p=P)).then_inc(w_in, 16)
                sp.dma_start(wr[:], g["Wr"][layer].rearrange("(a p) d -> p a d", p=P)).then_inc(w_in, 16)
                for i, name in enumerate(("rvar", "gamma", "b", "rmean", "beta")):
                    sp.dma_start(bn[:, i, :], g[name][layer].partition_broadcast(P)).then_inc(w_in, 16)

                def chunk_loads(n, following):
                    for b in range(BATCHES):
                        nxt = (n, b + SLOTS) if b + SLOTS < BATCHES else (following, b + SLOTS - BATCHES)
                        if nxt[0] is None:
                            continue
                        sp.wait_ge(batch_done, BATCHES * n + b + 1)
                        load(*nxt)

                with sp.Fori(0, CHUNKS - 1) as n:
                    chunk_loads(n, n + 1)
                chunk_loads(CHUNKS - 1, CHUNKS)
                chunk_loads(CHUNKS, None)

            @block.tensor
            def _(pe):
                pe.sem_inc(z_ps, CREDIT)
                def products(b, width, ty):
                    s0, m = batch_tiles(b)
                    for i in range(m):
                        s = s0 + i
                        right = mem.slot[b % SLOTS][:, i * width:(i + 1) * width]
                        for a in range(HALVES):
                            for part, left in enumerate((hi, lo)):
                                l = left[:, s, a * P:(a + 1) * P]
                                last = nc.tensor.matmul(bank[a][:, 0:width], l if ty is F32R else l.bitcast(F32), right if ty is F32R else right.bitcast(F32),
                                                        start=(s == 0 and part == 0), stop=(s == TILES - 1 and part == 1))
                    last.then_inc(batch_done, 1)

                def flip(n, i, per=4):
                    pe.wait_ge(copied, 4 * n + i + 1)
                    for a in range(HALVES):
                        last = nc.tensor.transpose(bank[2 + i % 2][:, a * P:(a + 1) * P], own_rows[:, i % 2, a * P:(a + 1) * P], mem.ident)
                    last.then_inc(flipped, 1)

                def project(n, i):
                    out = bank[4 + i % 2]
                    pe.wait_ge(hT_ready, 4 * n + i + 1)
                    pe.wait_ge(z_read, 4 * n + i + 1)
                    for a in range(HALVES):
                        nc.tensor.matmul(out[:, 0:D], hT[:, i % 2, a, :], wr[:, a, :], start=(a == 0), stop=(a == HALVES - 1))
                    pe.wait_ge(agg_out, HALVES * n + HALVES + CREDIT)
                    for a in range(HALVES):
                        last = nc.tensor.matmul(out[:, D:2 * D], agg[:, a, i * P:(i + 1) * P], wl[:, a, :], start=(a == 0), stop=(a == HALVES - 1))
                    last.then_inc(z_ps, 1)

                def chunk(n, width, ty):
                    tiles = width // P
                    pe.wait_ge(agg_out, HALVES * n + CREDIT)
                    for b in range(BATCHES):
                        s0, m = batch_tiles(b)
                        pe.wait_ge(split, (s0 + m - 1) // 7 + 1)
                        pe.wait_ge(landed[b % SLOTS], 16 * (BATCHES // SLOTS) * n + 16 * (b // SLOTS + 1))
                        if b == BATCHES - 1:
                            for i in range(min(2, tiles)):
                                flip(n, i)
                        products(b, width, ty)
                    pe.wait_ge(w_ready, 1)
                    for i in range(tiles):
                        project(n, i)
                        if i + 2 < tiles:
                            flip(n, i + 2)

                def everything(ty):
                    with pe.Fori(0, CHUNKS) as n:
                        chunk(n, CHUNK, ty)
                    chunk(CHUNKS, P, ty)

                with pe.register(f"top_{layer}") as top:
                    pe.reg_load(top, mem.top_int[0:1, 0:1])
                    with pe.If_lt(top, EXACT):
                        everything(F32R)
                    with pe.Else():
                        everything(F32)

            @block.gpsimd
            def _(pool):
                pool.wait_ge(var_ready, 1)
                power(nc, mem, bn[:, 0, :], D).then_inc(rstd_ready, 1)

            @block.scalar
            def _(act):
                def copy_rows(n, i, t):
                    nc.scalar.copy(own_rows[:, i % 2, :], h[:, t, :]).then_inc(copied, 1)

                def take(n, i):
                    act.wait_ge(flipped, 4 * n + i + 1)
                    nc.scalar.copy(hT[:, i % 2, :, :].rearrange("p a b -> p (a b)"), bank[2 + i % 2][:, 0:D]).then_inc(hT_ready, 1)

                def sums(n, width):
                    act.wait_ge(batch_done, BATCHES * n + BATCHES)
                    nc.scalar.copy(agg[:, 1, 0:width], bank[1][:, 0:width]).then_inc(agg_out, 1)

                with act.Fori(0, CHUNKS) as n:
                    for i in range(2):
                        act.wait_ge(z_ps, 4 * n + CREDIT)
                        copy_rows(n, i, 4 * n + i)
                    for i in range(2):
                        take(n, i)
                    sums(n, CHUNK)
                    for i in range(2, 4):
                        copy_rows(n, i, 4 * n + i)
                    for i in range(2, 4):
                        act.wait_ge(z_ps, 4 * n + i - 1 + CREDIT)
                        take(n, i)
                act.wait_ge(z_ps, 4 * CHUNKS + CREDIT)
                copy_rows(CHUNKS, 0, FULL)
                take(CHUNKS, 0)
                sums(CHUNKS, P)

            @block.vector
            def _(dve):
                step = Steps(dve, own)
                dve.sem_inc(z_read, 2)
                dve.sem_inc(agg_out, CREDIT)
                for k in range(7):
                    part = slice(7 * k, 7 * k + 7)
                    nc.vector.tensor_copy(hi[:, part, :], h[:, part, :]).then_inc(hi_done, 1)
                    dve.wait_ge(hi_done, k + 1)
                    nc.vector.tensor_tensor(lo[:, part, :], h[:, part, :], hi[:, part, :].bitcast(F32), ALU.subtract).then_inc(split, 1)
                dve.wait_ge(w_in, 16 * 7)
                rvar, gamma, b, rmean, beta = (bn[:, i, :] for i in range(5))
                nc.vector.tensor_scalar(rvar, rvar, EPS, None, ALU.add).then_inc(var_ready, 1)
                dve.wait_ge(rstd_ready, 1)
                step(nc.vector.tensor_tensor(gamma, gamma, rvar, ALU.mult))
                step(nc.vector.tensor_tensor(b, b, rmean, ALU.subtract))
                step(nc.vector.tensor_tensor(b, b, gamma, ALU.mult))
                step(nc.vector.tensor_tensor(b, b, beta, ALU.add))
                for w in (wl, wr):
                    for a in range(HALVES):
                        last = nc.vector.tensor_tensor(w[:, a, :], w[:, a, :], gamma, ALU.mult)
                last.then_inc(w_ready, 1)

                def sums(n, width):
                    dve.wait_ge(batch_done, BATCHES * n + BATCHES)
                    nc.vector.tensor_copy(agg[:, 0, 0:width], bank[0][:, 0:width]).then_inc(agg_out, 1)

                def finish(n, i, t):
                    z, z1 = bank[4 + i % 2], z1s[:, i % 2, :]
                    dve.wait_ge(z_ps, 4 * n + i + 1 + CREDIT)
                    step(nc.vector.tensor_tensor(z1, z[:, 0:D], b, ALU.add))
                    nc.vector.scalar_tensor_tensor(out=z1, in0=z[:, D:2 * D], scalar=mem.rdeg[:, bass.ds(t, 1)], in1=z1,
                                                   op0=ALU.mult, op1=ALU.add).then_inc(z_read, 1)
                    dve.wait_ge(z_read, 4 * n + i + 3)
                    if layer < LAYERS - 1:
                        nc.vector.scalar_tensor_tensor(out=h[:, t, :], in0=z1, scalar=0.0, in1=h[:, t, :], op0=ALU.max, op1=ALU.add)
                    else:
                        nc.vector.tensor_tensor(h[:, t, :], z1, h[:, t, :], ALU.add)

                with dve.Fori(0, CHUNKS) as n:
                    step.loop(n, 4)
                    sums(n, CHUNK)
                    for i in range(4):
                        finish(n, i, 4 * n + i)
                step.end(4, CHUNKS)
                sums(CHUNKS, P)
                finish(CHUNKS, 0, FULL)


def router_stage(nc, mem, f):
    with ExitStack() as ctx:
        sb = lambda n, s, d: ctx.enter_context(nc.sbuf_tensor(n, s, d))
        sem = ctx.enter_context(stage_semaphores(nc))
        bank, h = mem.bank, mem.h
        xm, stats, tmp = sb("xm_rows", [P, TILES, D], F32), sb("ffn_stats", [P, TILES, 6], F32), sb("ffn_tmp", [P, TILES], F32)
        gate_w, gate_b = sb("gate_w", [P, HALVES, E], F32), sb("gate_b", [P, E], F32)
        xs, xT = sb("router_rows", [P, 2, D], F32), sb("router_xT", [P, 2, HALVES, P], F32)
        logits, score, onehot = (sb(n, [P, TILES, E], F32) for n in ("logits", "score", "onehot"))
        best = sb("best", [P, 3, TILES], F32)
        chosen = sb("chosen", [P, E, TILES, 2], BF16)
        tri, ones = sb("tri_bf", [P, P], BF16), sb("ones_bf", [P, P], BF16)
        rank = sb("rank_e", [P, E], F32)
        counts, counts_i, ends = sb("e_counts", [P, E], F32), sb("e_counts_i", [P, E], I32), sb("e_ends", [P, E], F32)
        room, w_e = xm[:].rearrange("p t d -> p (t d)"), E * 2 * TILES
        before, place, keep = (room[:, k * w_e:(k + 1) * w_e].rearrange("p (e m) -> p e m", e=E) for k in range(3))
        tile_e = room[0:1, 3 * w_e:3 * w_e + XT * E].rearrange("p (j e) -> p j e", e=E)
        one = sb("ones_e", [P, E], F32)
        slot_f, tile_f = sb("slot_f", [P, TILES, 2], F32), sb("tile_f", [1, XT], F32)
        loaded, gate_in, added, own, stats_done = (sem(n) for n in ("xm_in", "gate_in", "x2_done", "router_own", "ffn_stats_done"))
        var_ready, rstd_ready, xs_ready, flipped, xT_ready, logit_ps, logit_read = (
            sem(n) for n in ("ffn_var", "ffn_rstd", "router_xs", "router_flip", "router_xT_ready", "logit_ps", "logit_read"))
        cleared, chosen_ready, ranked, exp_in, exp_out = (sem(n) for n in ("router_cleared", "chosen_ready", "ranked", "exp_in", "exp_out"))
        parts = [(12 * k, 12) for k in range(4)] + [(FULL, 1)]

        with nc.Block() as block:
            @block.sync
            def _(sp):
                sp.wait_ge(cleared, 1)
                for k, (t, m) in enumerate(parts):
                    if t < FULL:
                        sp.dma_start(xm[:, t:t + m, :], rows(mem.xm_dram)[:, t:t + m, :]).then_inc(mem.part_in[k], 16)
                    else:
                        sp.dma_start(xm[0:TAIL, t, :], mem.xm_dram[FULL * P:N, :]).then_inc(mem.part_in[k], 16)
                sp.dma_start(gate_w[:], f["gate_w"].rearrange("(a p) e -> p a e", p=P)).then_inc(gate_in, 16)
                sp.dma_start(gate_b[:], f["gate_b"].partition_broadcast(P)).then_inc(gate_in, 16)
                for e in range(E):
                    sp.dma_start(mem.w1[:, e, :, :], f["w1"][e].rearrange("(a p) f -> p a f", p=P)).then_inc(mem.w1_in, 16)

            @block.tensor
            def _(pe):
                pe.sem_inc(flipped, CREDIT)
                pe.wait_ge(gate_in, 32)

                def tile(j, n):
                    pe.wait_ge(xs_ready, 2 * n + j + 1)
                    for a in range(HALVES):
                        last = nc.tensor.transpose(bank[j][:, a * P:(a + 1) * P], xs[:, j, a * P:(a + 1) * P], mem.ident)
                    last.then_inc(flipped, 1)
                    pe.wait_ge(xT_ready, 2 * n + j + 1)
                    pe.wait_ge(logit_read, 2 * n + CREDIT)
                    for a in range(HALVES):
                        last = nc.tensor.matmul(bank[2 + j][:, 0:E], xT[:, j, a, :], gate_w[:, a, :], start=(a == 0), stop=(a == HALVES - 1))
                    last.then_inc(logit_ps, 1)

                with pe.Fori(0, FULL // 2) as n:
                    for j in range(2):
                        tile(j, n)
                tile(0, FULL // 2)
                pe.wait_ge(chosen_ready, 1)
                flat = chosen[:].rearrange("p e t k -> p (e t k)")
                w = E // 4 * 2 * TILES
                for c in range(4):
                    nc.tensor.matmul(bank[c][:, 0:w], tri[:], flat[:, c * w:(c + 1) * w], start=True, stop=True)
                    last = nc.tensor.matmul(bank[4 + c][:, 0:w], ones[:], flat[:, c * w:(c + 1) * w], start=True, stop=True)
                last.then_inc(ranked, 1)

            @block.scalar
            def _(act):
                def take(j, n):
                    act.wait_ge(flipped, 2 * n + j + 1 + CREDIT)
                    nc.scalar.copy(xT[:, j, :, :].rearrange("p a b -> p (a b)"), bank[j][:, 0:D]).then_inc(xT_ready, 1)

                with act.Fori(0, FULL // 2) as n:
                    for j in range(2):
                        take(j, n)
                take(0, FULL // 2)
                act.wait_ge(exp_in, 1)
                nc.scalar.activation(mem.gates[:, 1, :], mem.gates[:, 1, :], ACT.Exp).then_inc(exp_out, 1)

            @block.gpsimd
            def _(pool):
                nc.gpsimd.memset(xm[:, FULL, :], 0.0).then_inc(cleared, 1)
                nc.gpsimd.iota(mem.rank_i[:], pattern=[[-1, E]], base=E, channel_multiplier=0).then_inc(cleared, 1)
                pool.wait_ge(var_ready, 1)
                power(nc, mem, mem.rstd[:], TILES).then_inc(rstd_ready, 1)

            @block.vector
            def _(dve):
                step = Steps(dve, own)
                dve.sem_inc(logit_read, CREDIT)
                for k, (t, m) in enumerate(parts):
                    dve.wait_ge(mem.part_in[k], 16)
                    nc.vector.tensor_tensor(h[:, t:t + m, :], h[:, t:t + m, :], xm[:, t:t + m, :], ALU.add).then_inc(added, 1)
                dve.wait_ge(added, len(parts))
                with dve.Fori(0, TILES) as n:
                    nc.vector.bn_stats(stats[:, n, :], h[:, n, :]).then_inc(stats_done, 1)
                dve.wait_ge(stats_done, TILES)
                ln_rows(nc, dve, step, stats, mem.mean, mem.rstd, tmp, var_ready, rstd_ready)

                def normalise(j, n, t):
                    dve.wait_ge(flipped, 2 * n + CREDIT)
                    nc.vector.tensor_scalar(xs[:, j, :], h[:, t, :], mem.mean[:, bass.ds(t, 1)], mem.rstd[:, bass.ds(t, 1)], ALU.subtract, ALU.mult).then_inc(xs_ready, 1)

                def read(j, n, t):
                    dve.wait_ge(logit_ps, 2 * n + j + 1)
                    nc.vector.tensor_tensor(logits[:, t, :], bank[2 + j][:, 0:E], gate_b[:], ALU.add).then_inc(logit_read, 1)

                dve.wait_ge(gate_in, 32)
                with dve.Fori(0, FULL // 2) as n:
                    for j in range(2):
                        normalise(j, n, 2 * n + j)
                    for j in range(2):
                        read(j, n, 2 * n + j)
                normalise(0, FULL // 2, FULL)
                read(0, FULL // 2, FULL)
                dve.wait_ge(logit_read, TILES + CREDIT)
                dve.wait_ge(cleared, 2)
                step(nc.vector.tensor_copy(rank[:], mem.rank_i[:]))
                wide = lambda v: v.rearrange("p (t o) -> p t o", o=1).to_broadcast([P, TILES, E])
                each = rank[:].rearrange("p (o e) -> p o e", o=1).to_broadcast([P, TILES, E])
                for k in range(2):
                    step(nc.vector.reduce_max(best[:, k, :], logits[:], X_AXIS))
                    step(nc.vector.tensor_tensor(score[:], logits[:], wide(best[:, k, :]), ALU.is_equal))
                    step(nc.vector.tensor_tensor(score[:], score[:], each, ALU.mult))
                    step(nc.vector.reduce_max(best[:, 2, :], score[:], X_AXIS))
                    step(nc.vector.tensor_tensor(onehot[:], score[:], wide(best[:, 2, :]), ALU.is_equal))
                    step(nc.vector.tensor_scalar(onehot[:, FULL, :], onehot[:, FULL, :], mem.valid, None, ALU.mult))
                    step(nc.vector.tensor_copy(chosen[:, :, :, k], onehot[:].rearrange("p t e -> p e t")))
                    if k == 0:
                        step(nc.vector.scalar_tensor_tensor(out=logits[:], in0=onehot[:], scalar=-3e38, in1=logits[:], op0=ALU.mult, op1=ALU.add))
                        step(nc.vector.tensor_copy(mem.weigh[:], onehot[:]))
                nc.vector.tensor_copy(tri[:], mem.tri)
                nc.vector.memset(ones[:], 1.0).then_inc(chosen_ready, 1)
                nc.vector.tensor_tensor(mem.gates[:, 1, :], best[:, 1, :], best[:, 0, :], ALU.subtract).then_inc(exp_in, 1)
                dve.wait_ge(exp_out, 1)
                step(nc.vector.tensor_scalar(mem.gates[:, 0, :], mem.gates[:, 1, :], 1.0, None, ALU.add))
                step(nc.vector.reciprocal(mem.gates[:, 0, :], mem.gates[:, 0, :]))
                step(nc.vector.tensor_tensor(mem.gates[:, 1, :], mem.gates[:, 0, :], mem.gates[:, 1, :], ALU.mult))
                step(nc.vector.tensor_tensor(mem.weigh[:], mem.weigh[:], wide(mem.gates[:, 0, :]), ALU.mult))
                step(nc.vector.tensor_tensor(onehot[:], onehot[:], wide(mem.gates[:, 1, :]), ALU.mult))
                step(nc.vector.tensor_tensor(mem.weigh[:], mem.weigh[:], onehot[:], ALU.add))
                step(nc.vector.memset(keep, 1.0))
                step(nc.vector.memset(keep[:, :, 0:1], 0.0))
                step(nc.vector.memset(one[:], 1.0))
                dve.wait_ge(ranked, 1)
                w = E // 4 * 2 * TILES
                per = lambda c: mem.bank[c][:, 0:w].rearrange("p (e m) -> p e m", e=E // 4)
                for c in range(4):
                    nc.vector.tensor_reduce(counts[:, 4 * c:4 * c + 4], per(4 + c), X_AXIS, ALU.add)
                    last = nc.vector.tensor_copy(before[:, 4 * c:4 * c + 4, 1:], per(4 + c)[:, :, 0:2 * TILES - 1])
                step(last)
                step(nc.vector.tensor_scalar(counts_i[:], counts[:], float(P - 1), None, ALU.add))
                step(nc.vector.tensor_scalar(counts_i[:], counts_i[:], 7, 7, ALU.logical_shift_right, ALU.logical_shift_left))
                step(nc.vector.tensor_copy(counts[:], counts_i[:]))
                step(nc.vector.tensor_tensor_scan(ends[:], one[:], counts[:], 0.0, ALU.mult, ALU.add))
                step(nc.vector.tensor_tensor(before[:, :, 0], ends[:], counts[:], ALU.subtract))
                flat = lambda t: t.rearrange("p e m -> p (e m)")
                step(nc.vector.tensor_tensor_scan(flat(place), flat(keep), flat(before), 0.0, ALU.mult, ALU.add))
                for c in range(4):
                    last = nc.vector.tensor_tensor(place[:, 4 * c:4 * c + 4, :], place[:, 4 * c:4 * c + 4, :], per(c), ALU.add)
                step(last)
                step(nc.vector.tensor_tensor(place, place, chosen[:].rearrange("p e t k -> p e (t k)"), ALU.mult))
                step(nc.vector.tensor_reduce(slot_f[:].rearrange("p t k -> p (t k)"), place.rearrange("p e m -> p m e"), X_AXIS, ALU.add))
                step(nc.vector.tensor_copy(mem.slots[:], slot_f[:]))
                step(nc.vector.tensor_scalar(tile_f[:], mem.iota[0:1, 0:XT], float(P), None, ALU.mult))
                first = tile_f[:].rearrange("p (j o) -> p j o", o=1).to_broadcast([1, XT, E])
                last_of = ends[0:1, :].rearrange("p (o e) -> p o e", o=1).to_broadcast([1, XT, E])
                step(nc.vector.tensor_tensor(tile_e, first, last_of, ALU.is_ge))
                step(nc.vector.tensor_reduce(tile_f[:], tile_e, X_AXIS, ALU.add))
                step(nc.vector.tensor_scalar(mem.tile_expert[:], tile_f[:], float(E - 1), None, ALU.min))


def dispatch_stage(nc, mem, f):
    with ExitStack() as ctx:
        sb = lambda n, s, d: ctx.enter_context(nc.sbuf_tensor(n, s, d))
        sem = ctx.enter_context(stage_semaphores(nc))
        xs, where = sb("dispatch_rows", [P, 4, D], F32), sb("dispatch_slot", [P, 4, 2], I32)
        ready, turn = sem("dispatch_ready"), sem("dispatch_turn")
        sent = [sem(f"dispatch_sent{j}") for j in range(4)]
        with nc.Block() as block:
            @block.sync
            def _(sp):
                for e in range(E):
                    sp.dma_start(mem.w2[:, e, :, :], f["w2"][e].rearrange("(a p) f -> p a f", p=P)).then_inc(mem.w2_in, 16)
                sp.dma_start(mem.b1_rows[:], f["b1"].rearrange("e (a p) -> (e a) p", p=P)).then_inc(mem.b1_in, 16)

            @block.vector
            def _(dve):
                def prepare(u):
                    j, t = u.slot(4), u.value()
                    after(dve, sent[j], u, times=32, over=4)
                    nc.vector.tensor_scalar(xs[:, j, :], mem.h[:, t, :], mem.mean[:, bass.ds(t, 1)], mem.rstd[:, bass.ds(t, 1)], ALU.subtract, ALU.mult)
                    nc.vector.tensor_copy(where[:, j, :], mem.slots[:, t, :]).then_inc(ready, 1)

                four_steps(dve, 0, FULL, 4, prepare)

            @block.gpsimd
            def _(pool):
                def send(u):
                    j = u.slot(4)
                    r = TAIL if u.n is None and u.c == FULL else P
                    after(pool, ready, u + 1)
                    pool.sem_inc(turn, 1)
                    for k in range(2):
                        pool.indirect_dma_start(out=mem.slot_rows, out_offset=bass.IndirectOffsetOnAxis(ap=where[0:r, j, k:k + 1], axis=0),
                                                in_=xs[0:r, j, :], in_offset=None).then_inc(sent[j], 16)

                four_steps(pool, 0, FULL, 4, send)
                for j in range(4):
                    pool.wait_ge(sent[j], 32 * len(range(j, TILES, 4)))


def expert_stage(nc, mem):
    with ExitStack() as ctx:
        sb = lambda n, s, d: ctx.enter_context(nc.sbuf_tensor(n, s, d))
        sem = ctx.enter_context(stage_semaphores(nc))
        bank = mem.bank
        FT = FF // P
        xs, xT = sb("slot_x", [P, 4, D], F32), sb("slot_xT", [P, 2, D], F32)
        hid, hT, y = sb("hidden", [P, 2, FF], F32), sb("hidden_T", [P, 2, FT, P], F32), sb("slot_y", [P, 2, D], F32)
        x_in = [sem(f"slot_in{j}") for j in range(4)]
        y_out = [sem(f"slot_out{j}") for j in range(2)]
        flipped, xT_ready, hid_ps, hid_ready, hid_flip_a, hid_flip_b, hT_ready, y_ps, y_ready = (
            sem(n) for n in ("slot_flipped", "slot_xT_ready", "hid_ps", "hid_ready", "hid_flip_a", "hid_flip_b", "hT_ready_e", "y_ps", "y_ready"))
        b1_flipped, b1_ready, hid_last = sem("b1_flipped"), sem("b1_ready"), sem("hT_dve")
        load_v = mem.slot_rows.rearrange("(t p) d -> t p d", p=P)
        store_v = mem.slot_out.rearrange("(t p) d -> t p d", p=P)
        PEEL = 6

        def run(eng, body):
            four_steps(eng, -2, XT, PEEL, body)

        def expert_of(eng, u):
            return eng.value_load(mem.tile_expert[0:1, bass.ds(u.value(), 1)], min_val=0, max_val=E - 1)

        with nc.Block() as block:
            @block.sync
            def _(sp):
                for j in range(4):
                    sp.dma_start(xs[:, j, :], load_v[j]).then_inc(x_in[j], 16)

                def step(t):
                    if (t + 6).exists(XT) and (t + 2).exists(XT):
                        after(sp, flipped, t + 3)
                        j = (t + 6).slot(4)
                        sp.dma_start(xs[:, j, :], load_v[(t + 6).value()]).then_inc(x_in[j], 16)
                    if (t + -1).exists(XT):
                        after(sp, y_ready, t)
                        j = (t + -1).slot(2)
                        sp.dma_start(store_v[(t + -1).value()], y[:, j, :]).then_inc(y_out[j], 16)

                four_steps(sp, -2, XT, PEEL + 2, step)
                sp.wait_ge(y_out[0], 16 * ((XT + 1) // 2))
                sp.wait_ge(y_out[1], 16 * (XT // 2))

            @block.tensor
            def _(pe):
                pe.wait_ge(mem.b1_in, 16)
                nc.tensor.transpose(bank[7][:, 0:E * FT], mem.b1_rows[:], mem.ident[0:E * FT, 0:E * FT]).then_inc(b1_flipped, 1)
                pe.wait_ge(mem.w1_in, 16 * E)
                pe.wait_ge(mem.w2_in, 16 * E)
                w1 = mem.w1[:].rearrange("p e a f -> p e (a f)")
                w2 = mem.w2[:].rearrange("p e a f -> p e (a f)")

                def rows_flip(u):
                    after(pe, x_in[u.slot(4)], u + 4, times=16, over=4)
                    after(pe, xT_ready, u)
                    for a in range(HALVES):
                        last = nc.tensor.transpose(bank[0][:, a * P:(a + 1) * P], xs[:, u.slot(4), a * P:(a + 1) * P], mem.ident)
                    last.then_inc(flipped, 1)

                def first_product(u):
                    e = expert_of(pe, u)
                    after(pe, xT_ready, u + 1)
                    after(pe, hid_ready, u)
                    for a in range(HALVES):
                        last = nc.tensor.matmul(bank[1][:, :], xT[:, u.slot(2), a * P:(a + 1) * P], w1[:, e, a * FF:(a + 1) * FF], start=(a == 0), stop=(a == HALVES - 1))
                    last.then_inc(hid_ps, 1)

                def hidden_flip(u):
                    after(pe, hid_ready, u + 1)
                    after(pe, hT_ready, u)
                    after(pe, hid_last, u)
                    for k in range(FT):
                        last = nc.tensor.transpose(bank[2 + k // 2][:, (k % 2) * P:(k % 2 + 1) * P], hid[:, u.slot(2), k * P:(k + 1) * P], mem.ident)
                        if k % 2:
                            last.then_inc((hid_flip_a, hid_flip_b)[k // 2], 1)

                def second_product(u):
                    e = expert_of(pe, u)
                    after(pe, hT_ready, u + 1)
                    after(pe, hid_last, u + 1)
                    after(pe, y_ready, u + -1)
                    for k in range(FT):
                        last = nc.tensor.matmul(bank[4 + u.slot(2)][:, 0:D], hT[:, u.slot(2), k, :], w2[:, e, k * D:(k + 1) * D], start=(k == 0), stop=(k == FT - 1))
                    last.then_inc(y_ps, 1)

                def step(t):
                    if (t + 2).exists(XT):
                        rows_flip(t + 2)
                    if (t + 1).exists(XT):
                        first_product(t + 1)
                    if t.exists(XT):
                        hidden_flip(t)
                    if (t + -1).exists(XT):
                        second_product(t + -1)

                run(pe, step)

            @block.scalar
            def _(act):
                act.wait_ge(b1_ready, 1)

                def rows_out(u):
                    after(act, flipped, u + 1)
                    after(act, hid_ps, u + -1)
                    nc.scalar.copy(xT[:, u.slot(2), :], bank[0][:, 0:D]).then_inc(xT_ready, 1)

                def hidden_out(u):
                    e = expert_of(act, u)
                    after(act, hid_flip_a, u + 1)
                    after(act, y_ps, u + -1)
                    for k in range(FT // 2):
                        last = nc.scalar.activation(hT[:, u.slot(2), k, :], bank[2][:, k * P:(k + 1) * P], ACT.Relu, bias=mem.b1T[:, bass.ds(e * FT + k, 1)])
                    last.then_inc(hT_ready, 1)

                def result_out(u):
                    after(act, y_ps, u + 1)
                    after(act, y_out[u.slot(2)], u, times=16, over=2)
                    nc.scalar.copy(y[:, u.slot(2), :], bank[4 + u.slot(2)][:, 0:D]).then_inc(y_ready, 1)

                def step(t):
                    if (t + 2).exists(XT):
                        rows_out(t + 2)
                    if t.exists(XT):
                        hidden_out(t)
                    if (t + -1).exists(XT):
                        result_out(t + -1)

                run(act, step)

            @block.vector
            def _(dve):
                dve.wait_ge(b1_flipped, 1)
                nc.vector.tensor_copy(mem.b1T[:], bank[7][:, 0:E * FT]).then_inc(b1_ready, 1)
                dve.wait_ge(b1_ready, 1)

                def hidden_keep(u):
                    after(dve, hid_ps, u + 1)
                    after(dve, hid_flip_b, u + -1)
                    nc.vector.tensor_copy(hid[:, u.slot(2), :], bank[1][:, :]).then_inc(hid_ready, 1)

                def hidden_out(u):
                    e = expert_of(dve, u)
                    after(dve, hid_flip_b, u + 1)
                    after(dve, y_ps, u + -1)
                    for k in range(FT // 2, FT):
                        last = nc.vector.tensor_scalar(hT[:, u.slot(2), k, :], bank[3][:, (k % 2) * P:(k % 2 + 1) * P], mem.b1T[:, bass.ds(e * FT + k, 1)], 0.0, ALU.add, ALU.max)
                    last.then_inc(hid_last, 1)

                def step(t):
                    if (t + 1).exists(XT):
                        hidden_keep(t + 1)
                    if t.exists(XT):
                        hidden_out(t)

                run(dve, step)


def combine_stage(nc, mem, f, out):
    with ExitStack() as ctx:
        sb = lambda n, s, d: ctx.enter_context(nc.sbuf_tensor(n, s, d))
        sem = ctx.enter_context(stage_semaphores(nc))
        bank, h = mem.bank, mem.h
        gamma, beta, b2 = sb("ffn_gamma", [P, D], F32), sb("ffn_beta", [P, D], F32), sb("ffn_b2", [E, D], F32)
        rows_in, where = sb("gathered", [P, 4, 2, D], F32), sb("gather_slot", [P, 4, 2], I32)
        wrow, wT = sb("weigh_rows", [P, 4, E], F32), sb("weigh_T", [E, 2, P], F32)
        acc, norm, res = (sb(n, [P, 4, D], F32) for n in ("acc", "acc_norm", "res"))
        st, mv, offset = sb("acc_stats", [P, 2, 6], F32), sb("acc_mv", [P, 2, 2], F32), sb("minus_mean_rstd", [P, TILES], F32)
        in_b, where_ready, turn, weigh_ready, w_flipped, wT_ready, bias_ps = (
            sem(n) for n in ("ffn_rows_in", "where_ready", "gather_turn", "weigh_ready", "w_flipped", "wT_ready_c", "bias_ps"))
        own, var_ready, rstd_ready, res_ready, rows_done, aggr_turn, offset_ready, acc_set = (
            sem(n) for n in ("combine_own", "acc_var", "acc_rstd", "res_ready", "rows_done", "aggr_turn", "offset_ready", "acc_set"))
        gathered = [sem(f"gathered{j}") for j in range(4)]
        stored = [sem(f"stored{j}") for j in range(4)]
        FIRST, PEEL = -3, 8

        def run(eng, body):
            four_steps(eng, FIRST, TILES, PEEL, body)

        with nc.Block() as block:
            @block.sync
            def _(sp):
                sp.dma_start(gamma[:], f["gamma"].partition_broadcast(P)).then_inc(in_b, 16)
                sp.dma_start(beta[:], f["beta"].partition_broadcast(P)).then_inc(in_b, 16)
                sp.dma_start(b2[:], f["b2"]).then_inc(in_b, 16)
                out_v = out[0:FULL * P, :].rearrange("(t p) d -> t p d", p=P)

                def step(t):
                    u = t + -1
                    if not u.exists(TILES):
                        return
                    after(sp, res_ready, u + 1)
                    if u.n is None and u.c == FULL:
                        sp.dma_start(out[FULL * P:N, :], res[0:TAIL, u.slot(4), :]).then_inc(stored[u.slot(4)], 16)
                    else:
                        sp.dma_start(out_v[u.value()], res[:, u.slot(4), :]).then_inc(stored[u.slot(4)], 16)

                run(sp, step)
                for j in range(4):
                    sp.wait_ge(stored[j], 16 * len(range(j, TILES, 4)))

            @block.gpsimd
            def _(pool):
                def gather(u):
                    j = u.slot(4)
                    r = TAIL if u.n is None and u.c == FULL else P
                    after(pool, where_ready, u + 1)
                    pool.sem_inc(turn, 1)
                    for k in range(2):
                        pool.indirect_dma_start(out=rows_in[0:r, j, k, :], out_offset=None, in_=mem.slot_out,
                                                in_offset=bass.IndirectOffsetOnAxis(ap=where[0:r, j, k:k + 1], axis=0)).then_inc(gathered[j], 16)

                def step(t):
                    if (t + 3).exists(TILES):
                        gather(t + 3)
                    if t.exists(TILES):
                        after(pool, var_ready, t + 1)
                        power(nc, mem, mv[:, t.slot(2), 1:2], 1).then_inc(rstd_ready, 1)

                run(pool, step)

            @block.tensor
            def _(pe):
                pe.wait_ge(in_b, 48)

                def flip(u):
                    after(pe, weigh_ready, u + 1)
                    after(pe, wT_ready, u + -1)
                    nc.tensor.transpose(bank[u.slot(2)][0:E, 0:P], wrow[:, u.slot(4), :], mem.ident).then_inc(w_flipped, 1)

                def bias(u):
                    after(pe, wT_ready, u + 1)
                    after(pe, rows_done, u + -1)
                    nc.tensor.matmul(bank[2 + u.slot(2)][:, 0:D], wT[:, u.slot(2), :], b2[:], start=True, stop=True).then_inc(bias_ps, 1)

                def step(t):
                    if (t + 2).exists(TILES):
                        flip(t + 2)
                    if (t + 1).exists(TILES):
                        bias(t + 1)

                run(pe, step)

            @block.scalar
            def _(act):
                act.wait_ge(offset_ready, 1)

                def step(t):
                    u = t + 2
                    if not u.exists(TILES):
                        return
                    after(act, res_ready, u + -3)
                    nc.scalar.activation(acc[:, u.slot(4), :], h[:, u.value(), :], ACT.Identity, scale=mem.rstd[:, bass.ds(u.value(), 1)],
                                         bias=offset[:, bass.ds(u.value(), 1)]).then_inc(acc_set, 1)
                    after(act, w_flipped, u + 1)
                    after(act, bias_ps, u + -1)
                    nc.scalar.copy(wT[:, u.slot(2), :], bank[u.slot(2)][0:E, 0:P]).then_inc(wT_ready, 1)

                run(act, step)

            @block.vector
            def _(dve):
                nc.vector.scalar_tensor_tensor(out=offset[:], in0=mem.mean[:], scalar=-1.0, in1=mem.rstd[:], op0=ALU.mult, op1=ALU.mult).then_inc(offset_ready, 1)
                own_step = StepCount(dve, own, 7, FIRST)
                dve.wait_ge(in_b, 48)

                def ask(u):
                    t = u.value()
                    after(dve, w_flipped, u + -3)
                    nc.vector.tensor_copy(wrow[:, u.slot(4), :], mem.weigh[:, t, :]).then_inc(weigh_ready, 1)
                    nc.vector.tensor_copy(where[:, u.slot(4), :], mem.slots[:, t, :]).then_inc(where_ready, 1)

                def step(t):
                    own_step.begin(t)
                    if (t + 3).exists(TILES):
                        ask(t + 3)
                    u, now, before = t + -1, t.exists(TILES), (t + -1).exists(TILES)
                    a, b, r = acc[:, t.slot(4), :], norm[:, u.slot(4), :], res[:, u.slot(4), :]
                    m, old = mv[:, t.slot(2), :], mv[:, u.slot(2), :]

                    def add(k):
                        return nc.vector.scalar_tensor_tensor(out=a, in0=rows_in[:, t.slot(4), k, :], scalar=mem.gates[:, k, bass.ds(t.value(), 1)],
                                                              in1=a, op0=ALU.mult, op1=ALU.add)

                    if now:
                        after(dve, acc_set, t + 1)
                        after(dve, gathered[t.slot(4)], t + 4, times=32, over=4)
                        own_step.issue(add(0))
                    if before:
                        after(dve, rstd_ready, u + 1)
                        own_step(nc.vector.tensor_scalar(b, acc[:, u.slot(4), :], old[:, 0:1], old[:, 1:2], ALU.subtract, ALU.mult))
                    if now:
                        if not before:
                            own_step.eng.wait_ge(own, own_step.at + own_step.k)
                        own_step.issue(add(1))
                    if before:
                        own_step(nc.vector.tensor_tensor(b, b, gamma[:], ALU.mult))
                    if now:
                        if not before:
                            own_step.eng.wait_ge(own, own_step.at + own_step.k)
                        after(dve, bias_ps, t + 1)
                        nc.vector.tensor_tensor(a, a, bank[2 + t.slot(2)][:, 0:D], ALU.add).then_inc(rows_done, 1)
                    if before:
                        own_step(nc.vector.tensor_tensor(b, b, beta[:], ALU.add))
                    if now:
                        after(dve, rows_done, t + 1)
                        own_step.issue(nc.vector.bn_stats(st[:, t.slot(2), :], a))
                    if before:
                        after(dve, stored[u.slot(4)], u, times=16, over=4)
                        nc.vector.tensor_tensor(r, b, h[:, u.value(), :], ALU.add).then_inc(res_ready, 1)
                    if now:
                        dve.wait_ge(own, own_step.at + own_step.k)
                        dve.sem_inc(aggr_turn, 1)
                        own_step(nc.vector.bn_aggr(m, st[:, t.slot(2), :]))
                        nc.vector.tensor_scalar(m[:, 1:2], m[:, 1:2], EPS, None, ALU.add).then_inc(var_ready, 1)
                    own_step.finish()

                run(dve, step)


class Memory:
    pass


def program(nc, a, out):
    mem = Memory()
    with ExitStack() as ctx:
        sb = lambda n, s, d: ctx.enter_context(nc.sbuf_tensor(n, s, d))
        mem.psum = ctx.enter_context(nc.psum_tensor("psum", [P, 8 * 512], F32))
        mem.bank = [mem.psum[:, k * 512:(k + 1) * 512] for k in range(8)]
        mem.h = sb("h", [P, TILES, D], F32)
        mem.cf = sb("const_f", [P, 3 * P + 1], F32)
        mem.ident, mem.iota, mem.tri = (mem.cf[:, k * P:(k + 1) * P] for k in range(3))
        mem.minus_half = sb("minus_half", [P, 1], F32)
        mem.valid = mem.cf[:, 3 * P:3 * P + 1]
        mem.rdeg, mem.top, mem.top_int = sb("rdeg", [P, TILES], F32), sb("top", [P, 2], F32), sb("top_int", [P, 1], I32)
        mem.x, mem.mask_embed, mem.cf_dram, mem.ci_dram = a["x"], a["L0_gnn_mask_embed"], a["const_f"][:, 0:3 * P + 1], a["const_i"]
        mem.counts_2d = nc.dram_tensor("counts", [CELLS, 1], F32).ap()
        mem.counts = mem.counts_2d.rearrange("n o -> (n o)")
        mem.cells_dram = nc.dram_tensor("cells", [ETILES * P * P], I32).ap()
        mem.slot_rows = nc.dram_tensor("slot_rows", [XT * P, D], F32).ap()
        mem.slot_out = nc.dram_tensor("slot_out", [XT * P, D], F32).ap()
        mem.xm_dram = nc.dram_tensor("x_mix", [N, D], F32).ap()
        mem.counts_zeroed = ctx.enter_context(nc.semaphore("counts_zeroed"))

        with ExitStack() as early:
            sbe = lambda n, s, d: early.enter_context(nc.sbuf_tensor(n, s, d))
            mem.xk = sbe("x_keep", [P, TILES, D], F32)
            mem.ci = sbe("const_i", [P, 1 + GROUP + 2 * P], I32)
            mem.bit_mask, mem.dummy = mem.ci[:, 0:1], mem.ci[:, 1:1 + GROUP]
            mem.pad_and, mem.pad_or = (mem.ci[:, 1 + GROUP + k * P:1 + GROUP + (k + 1) * P] for k in range(2))
            mem.zeros = sbe("zeros", [P, 7 * CHUNK], F32)
            mem.zero_bf = sbe("zero_bf", [P, P], BF16)
            mem.cell_col = sbe("cell_col", [P, ETILES * P], I32)
            mem.dup_mask_dram = a["const_f"][:, 3 * P + 1:]
            index_stage(nc, mem, a["src"], a["dst"])
            mix_stage(nc, mem, {k: a["L0_mix_" + k] for k in ("wq", "wk", "wv", "wo", "bo", "ln_k_g", "ln_k_b", "ln_v_g", "ln_v_b")})
            scatter_stage(nc, mem)
        largest_degree(nc, mem)
        with ExitStack() as mid:
            sbm = lambda n, s, d: mid.enter_context(nc.sbuf_tensor(n, s, d))
            mem.h_hi, mem.h_lo = (sbm(n, [P, TILES, D], F32R) for n in ("h_hi", "h_lo"))
            mem.slot = [sbm(f"counts_slot{k}", [P, 5 * CHUNK], F32R) for k in range(SLOTS)]
            for layer in range(LAYERS):
                gnn_layer(nc, mem, layer, {k: a["L0_gnn_" + k] for k in ("Wl", "Wr", "rvar", "gamma", "b", "rmean", "beta")})
        with ExitStack() as late:
            sbl = lambda n, s, d: late.enter_context(nc.sbuf_tensor(n, s, d))
            seml = lambda n: late.enter_context(nc.semaphore(n))
            mem.w1 = sbl("w1", [P, E, HALVES, FF], F32)
            mem.mean, mem.rstd = sbl("ffn_mean", [P, TILES], F32), sbl("ffn_rstd", [P, TILES], F32)
            mem.gates, mem.weigh, mem.slots = sbl("gates", [P, 2, TILES], F32), sbl("weigh", [P, TILES, E], F32), sbl("slots", [P, TILES, 2], I32)
            mem.tile_expert, mem.rank_i = sbl("tile_expert", [1, XT], I32), sbl("rank_i", [P, E], I32)
            mem.part_in = [seml(f"xm_in{k}") for k in range(5)]
            mem.w1_in, mem.w2_in, mem.b1_in = seml("w1_in"), seml("w2_in"), seml("b1_in")
            f = {k: a["L0_ffn_" + k] for k in ("gate_w", "gate_b", "w1", "b1", "w2", "b2", "gamma", "beta")}
            router_stage(nc, mem, f)
            with ExitStack() as experts:
                sbx = lambda n, s, d: experts.enter_context(nc.sbuf_tensor(n, s, d))
                mem.w2 = sbx("w2", [P, E, FF // P, D], F32)
                mem.b1_rows, mem.b1T = sbx("b1_rows", [E * FF // P, P], F32), sbx("b1T", [P, E * FF // P], F32)
                dispatch_stage(nc, mem, f)
                expert_stage(nc, mem)
            combine_stage(nc, mem, f, out)


INPUTS = ["x", "src", "dst"] + ["L0_gnn_" + k for k in ("mask_embed", "Wl", "Wr", "b", "gamma", "beta", "rmean", "rvar")] \
    + ["L0_mix_" + k for k in ("wq", "wk", "wv", "wo", "bo", "ln_k_g", "ln_k_b", "ln_v_g", "ln_v_b")] \
    + ["L0_ffn_" + k for k in ("gate_w", "gate_b", "w1", "b1", "w2", "b2", "gamma", "beta")]


def constants(np):
    p = np.arange(P)
    ident = np.eye(P, dtype=np.float32)
    iota = np.broadcast_to(p.astype(np.float32), (P, P))
    tri = (p[:, None] < p[None, :]).astype(np.float32)
    dup = np.concatenate([np.ones((P, (GROUP - 1) * P), np.float32), tri.T], axis=1)
    const_f = np.ascontiguousarray(np.concatenate([ident, iota, tri, (p < TAIL)[:, None], dup], axis=1), dtype=np.float32)
    bit = (np.uint32(1) << (p % 32).astype(np.uint32)).view(np.int32)[:, None]
    dummy = DUMMY + np.arange(GROUP)[None, :] * P + p[:, None]
    edge = (ETILES - 1) * P * P + np.arange(P * P).reshape(P, P)
    pad = edge >= EDGES
    pad_and = np.where(pad, 0, -1)
    pad_or = np.where(pad, (DUMMY + GROUP * P + (edge - EDGES) % (GROUP * P)) | TAG, 0)
    const_i = np.ascontiguousarray(np.concatenate([bit, dummy, pad_and, pad_or], axis=1).astype(np.int32))
    return {"const_f": const_f, "const_i": const_i}


def kernel(**inputs):
    import numpy as np
    import concourse.bacc as bacc
    from concourse.bass_utils import run_bass_kernel_spmd

    nc = bacc.Bacc("TRN2", target_bir_lowering=False, num_devices=1)
    arrays, a = {}, {}
    for name, value in list({k: inputs[k] for k in INPUTS}.items()) + list(constants(np).items()):
        value = np.ascontiguousarray(value)
        arrays[f"in_{name}"] = value
        a[name] = nc.dram_tensor(f"in_{name}", value.shape, mybir.dt.from_np(value.dtype), kind="ExternalInput").ap()
    out = nc.dram_tensor("out_rows", (N, D), F32, kind="ExternalOutput").ap()
    program(nc, a, out)
    return run_bass_kernel_spmd(nc, [arrays], core_ids=[0]).results[0]["out_rows"]
```

```python
from contextlib import ExitStack, contextmanager

import concourse.bass as bass
from concourse import mybir

F32, F32R, BF16 = mybir.dt.float32, mybir.dt.float32r, mybir.dt.bfloat16
I32 = mybir.dt.int32
ALU = mybir.AluOpType
ACT = mybir.ActivationFunctionType
X_AXIS = mybir.AxisListType.X

P = 128
N, D, EDGES, LAYERS = 6250, 256, 200000, 3
HALVES = D // P
TILES = -(-N // P)
FULL = TILES - 1
TAIL = N - FULL * P
EPS = 1e-5

CHUNK = 512
CHUNKS = N // CHUNK
PART_BITS, TILE_BITS, COL_BITS = 7, 6, 9
CELL_CHUNK = 1 << (PART_BITS + TILE_BITS + COL_BITS)
GROUP = 8
QUADS = 4
ECHUNKS = -(-EDGES // P)
ITERS = -(-ECHUNKS // (GROUP * QUADS))
ECOLS = ITERS * GROUP * QUADS
ETILES = -(-ECOLS // P)
DUMMY = (CHUNKS + 1) * CELL_CHUNK
DUMMY_PAD = DUMMY + QUADS * GROUP * P
CELLS = DUMMY_PAD + GROUP * P
LANDED = 16 * GROUP
START = 16
TAG = 0x20000000
EARLY_ZEROS = 2
CREDIT = 1
EXACT = 4096

BATCHES = 12
SLOTS = 4
HEADS, HEAD = 4, 64
E, FF = 16, 512
XT = (2 * N + E * (P - 1)) // P


def batch_tiles(b):
    return (4 * b, 4 if b < BATCHES - 1 else TILES - 4 * (BATCHES - 1))


@contextmanager
def stage_semaphores(nc):
    taken = []

    def sem(name):
        taken.append(nc.alloc_semaphore(name))
        return taken[-1]

    yield sem
    nc.clear_and_free_semaphores(taken)
    nc.all_engine_barrier()


class Steps:

    def __init__(self, eng, sem):
        self.eng, self.sem, self.base, self.k, self.at = eng, sem, 0, 0, 0

    def loop(self, n, per):
        self.base, self.at, self.k = self.base + self.k, n * per, 0

    def end(self, per, times):
        assert self.k == per, (self.k, per)
        self.base, self.at, self.k = self.base + per * times, 0, 0

    def __call__(self, ins):
        self.k += 1
        ins.then_inc(self.sem, 1)
        self.eng.wait_ge(self.sem, self.at + (self.base + self.k))


class Count:

    def __init__(self, n, c):
        self.n, self.c = n, c

    def __add__(self, k):
        return Count(self.n, self.c + k)

    def value(self, times=1, over=1):
        c = times * (self.c // over)
        return c if self.n is None else self.n * (4 // over * times) + c

    def slot(self, k):
        return self.c % k

    def exists(self, last):
        return self.n is not None or 0 <= self.c < last


def after(eng, sem, count, times=1, over=1):
    v = count.value(times, over)
    if count.n is not None or v > 0:
        eng.wait_ge(sem, v)


def four_steps(eng, first, last, peel, body):
    n_loop = (last - first + 1 - 2 * peel) // 4
    for t in range(first, first + peel):
        body(Count(None, t))
    with eng.Fori(0, n_loop) as n:
        for j in range(4):
            body(Count(n, first + peel + j))
    for t in range(first + peel + 4 * n_loop, last + 1):
        body(Count(None, t))


class StepCount:

    def __init__(self, eng, sem, per, first):
        self.eng, self.sem, self.per, self.first = eng, sem, per, first

    def begin(self, t):
        self.at, self.k = (t + -self.first).value(times=self.per), 0

    def issue(self, ins):
        self.k += 1
        ins.then_inc(self.sem, 1)

    def __call__(self, ins):
        self.issue(ins)
        self.eng.wait_ge(self.sem, self.at + self.k)

    def finish(self):
        if self.k < self.per:
            self.eng.sem_inc(self.sem, self.per - self.k)


def rows(ap):
    return ap[0:FULL * P, :].rearrange("(t p) w -> p t w", p=P)


def load_keys(sp, mem, keys, sem):
    for q in range(QUADS):
        sp.dma_start(mem.key_rows[32 * q:32 * q + 32, :], keys[q * GROUP * P:(q + 1) * GROUP * P].partition_broadcast(32)).then_inc(sem, 16)


def zero_chunk(act, mem, c):
    dest = mem.counts[c * CELL_CHUNK:(c + 1) * CELL_CHUNK].rearrange("(p s) -> p s", p=P)
    act.dma_start(dest[:, 0:TILES * CHUNK].rearrange("p (r m) -> p r m", r=7),
                  mem.zeros[:].rearrange("p (r m) -> p r m", r=1).to_broadcast([P, 7, 7 * CHUNK])).then_inc(mem.counts_zeroed, 16)


def index_stage(nc, mem, src, dst, rvar):
    with ExitStack() as ctx:
        sb = lambda n, s, d: ctx.enter_context(nc.sbuf_tensor(n, s, d))
        sem = ctx.enter_context(stage_semaphores(nc))
        s_sb, d_sb = sb("src_rows", [P, ETILES, P], I32), sb("dst_rows", [P, ETILES, P], I32)
        a2, a3 = sb("cell_tile", [P, ETILES, P], I32), sb("cell_chunk", [P, ETILES, P], I32)
        cleared, loaded, own, cells_ready = sem("edges_cleared"), sem("edges_loaded"), sem("index_own"), sem("cells_ready")
        stored, flipped, const_in = sem("cells_stored"), sem("cells_flipped"), sem("const_in")
        ends = sb("chunk_ends", [P, 2, ETILES], F32)
        per_tile = P // GROUP
        top, low = sb("group_top", [ETILES, per_tile], F32), sb("group_low", [ETILES, per_tile], F32)
        clash, clash_i = sb("group_clash", [ETILES, per_tile], F32), sb("group_clash_i", [ETILES, per_tile], I32)
        ends_ready, ends_flipped, clash_ready, clash_out, clash_in = (sem(n) for n in ("ends_ready", "ends_flipped", "clash_ready", "clash_out", "clash_in"))
        var = sb("bn_var", [P, LAYERS * HALVES], F32)
        var_in, var_ready, bn_rstd, early_out = sem("bn_var_in"), sem("bn_var_ready"), sem("bn_rstd_ready"), sem("bn_rstd_out")
        x_in, moved, zeros_set = sem("x_in"), sem("x_pad_set"), sem("zeros_set")
        full = EDGES // (P * P)
        rest = EDGES - full * P * P
        rrows, rcols = rest // P, rest % P
        with nc.Block() as block:
            @block.sync
            def _(sp):
                sp.dma_start(mem.cf[:], mem.cf_dram).then_inc(const_in, 16)
                sp.dma_start(mem.ci[:], mem.ci_dram).then_inc(const_in, 16)
                for layer in range(LAYERS):
                    for a in range(HALVES):
                        k = layer * HALVES + a
                        sp.dma_start(var[:, k:k + 1], rvar[layer, a * P:(a + 1) * P].rearrange("(p o) -> p o", o=1)).then_inc(var_in, 16)
                sp.dma_start(mem.dup_f[:], mem.dup_mask_dram).then_inc(const_in, 16)
                sp.wait_ge(cleared, 2)
                for t, a in ((s_sb, src), (d_sb, dst)):
                    sp.dma_start(t[:, 0:full, :], a[0:full * P * P].rearrange("(i q p) -> q i p", q=P, p=P)).then_inc(loaded, 16)
                    sp.dma_start(t[0:rrows, full, :], a[full * P * P:full * P * P + rrows * P].rearrange("(q p) -> q p", p=P)).then_inc(loaded, 16)
                    sp.dma_start(t[rrows:rrows + 1, full, 0:rcols], a[EDGES - rcols:EDGES].rearrange("(q p) -> q p", q=1)).then_inc(loaded, 16)
                sp.wait_ge(moved, 1)
                for k in range(4):
                    m = FULL // 4
                    sp.dma_start(mem.xk[:, k * m:(k + 1) * m, :], rows(mem.x)[:, k * m:(k + 1) * m, :]).then_inc(x_in, 16)
                sp.dma_start(mem.xk[0:TAIL, FULL, :], mem.x[FULL * P:N, :]).then_inc(x_in, 16)
                sp.wait_ge(cells_ready, 1)
                store = mem.cells_dram.rearrange("(i q p) -> q i p", q=P, p=P)
                sp.dma_start(store, s_sb[:]).then_inc(stored, 16)
                sp.wait_ge(clash_ready, 1)
                sp.dma_start(mem.waits_dram.rearrange("(i r) -> i r", r=per_tile), clash_i[:]).then_inc(clash_out, 16)
                sp.wait_ge(clash_out, 16)
                sp.dma_start(mem.landed_before[:], mem.waits_dram.rearrange("(o m) -> o m", o=1)).then_inc(clash_in, 16)
                sp.wait_ge(clash_in, 16)
                sp.wait_ge(stored, 16)
                load_keys(sp, mem, mem.cells_dram[0:QUADS * GROUP * P], stored)
                sp.wait_ge(bn_rstd, 1)
                for k in range(LAYERS * HALVES):
                    sp.dma_start(mem.bn_rstd_dram[k // HALVES, (k % HALVES) * P:(k % HALVES + 1) * P].rearrange("(p o) -> p o", o=1), var[:, k:k + 1]).then_inc(early_out, 16)
                sp.wait_ge(early_out, 16 * LAYERS * HALVES)
                sp.wait_ge(stored, 16 + 16 * QUADS)
                sp.wait_ge(const_in, 48)
                sp.wait_ge(x_in, 80)

            @block.scalar
            def _(act):
                act.wait_ge(zeros_set, 1)
                act.wait_ge(x_in, 80)
                for c in range(EARLY_ZEROS):
                    zero_chunk(act, mem, c)

            @block.gpsimd
            def _(pool):
                nc.gpsimd.memset(mem.zeros[:], 0.0).then_inc(zeros_set, 1)
                nc.gpsimd.memset(mem.minus_half[:], -0.5)
                nc.gpsimd.memset(mem.xk[:, FULL, :], 0.0).then_inc(moved, 1)
                pool.wait_ge(moved, 1)
                pool.wait_ge(var_ready, 1)
                power(nc, mem, var[:], LAYERS * HALVES).then_inc(bn_rstd, 1)

            @block.vector
            def _(dve):
                step = Steps(dve, own)
                nc.vector.memset(s_sb[:, full, :], 0).then_inc(cleared, 1)
                nc.vector.memset(d_sb[:, full, :], 0).then_inc(cleared, 1)
                dve.wait_ge(var_in, 16 * LAYERS * HALVES)
                nc.vector.tensor_scalar(var[:], var[:], EPS, None, ALU.add).then_inc(var_ready, 1)
                dve.wait_ge(const_in, 48)
                dve.wait_ge(loaded, 96)
                nc.vector.tensor_reduce(ends[:, 0, :], d_sb[:], X_AXIS, ALU.max)
                step(nc.vector.tensor_reduce(ends[:, 1, :], d_sb[:], X_AXIS, ALU.min))
                dve.sem_inc(ends_ready, 1)
                nc.vector.tensor_scalar(a2[:], s_sb[:], PART_BITS, COL_BITS, ALU.logical_shift_right, ALU.logical_shift_left)
                nc.vector.tensor_scalar(a3[:], d_sb[:], COL_BITS, PART_BITS + TILE_BITS + COL_BITS, ALU.logical_shift_right, ALU.logical_shift_left)
                nc.vector.tensor_scalar(d_sb[:], d_sb[:], CHUNK - 1, TAG, ALU.bitwise_and, ALU.bitwise_or)
                step(nc.vector.tensor_scalar(s_sb[:], s_sb[:], P - 1, TILE_BITS + COL_BITS, ALU.bitwise_and, ALU.logical_shift_left))
                step(nc.vector.tensor_tensor(a2[:], a2[:], a3[:], ALU.bitwise_or))
                step(nc.vector.tensor_tensor(a2[:], a2[:], d_sb[:], ALU.bitwise_or))
                step(nc.vector.tensor_tensor(s_sb[:], s_sb[:], a2[:], ALU.bitwise_or))
                step(nc.vector.tensor_tensor(s_sb[:, full, :], s_sb[:, full, :], mem.pad_and, ALU.bitwise_and))
                nc.vector.tensor_tensor(s_sb[:, full, :], s_sb[:, full, :], mem.pad_or, ALU.bitwise_or).then_inc(cells_ready, 1)
                for i in range(ETILES):
                    if i % 4 == 0:
                        dve.wait_ge(flipped, i // 4 + 1)
                    nc.vector.tensor_scalar(mem.cell_col[:, i * P:(i + 1) * P], mem.bank[i // 4][:, (i % 4) * P:(i % 4 + 1) * P].bitcast(I32),
                                            TAG, None, ALU.bitwise_xor)

                dve.wait_ge(ends_flipped, 1)
                chunks = lambda k: mem.bank[5][0:ETILES, k * P:(k + 1) * P].rearrange("i (r g) -> i r g", g=GROUP)
                nc.vector.memset(clash[:], 1.0)
                nc.vector.tensor_reduce(top[:], chunks(0), X_AXIS, ALU.max)
                step(nc.vector.tensor_reduce(low[:], chunks(1)[:, :, 1:], X_AXIS, ALU.min))
                step(nc.vector.tensor_tensor(clash[:, 1:], top[:, 0:per_tile - 1], low[:, 1:], ALU.is_ge))
                nc.vector.tensor_scalar(clash_i[:], clash[:], float(LANDED), float(START), ALU.mult, ALU.add).then_inc(clash_ready, 1)

            @block.tensor
            def _(pe):
                pe.wait_ge(ends_ready, 1)
                for k in range(2):
                    last = nc.tensor.transpose(mem.bank[5][0:ETILES, k * P:(k + 1) * P], ends[:, k, :], mem.ident)
                last.then_inc(ends_flipped, 1)
                pe.wait_ge(cells_ready, 1)
                for i in range(ETILES):
                    last = nc.tensor.transpose(mem.bank[i // 4][:, (i % 4) * P:(i % 4 + 1) * P], s_sb[:, i, :].bitcast(F32), mem.ident)
                    if i % 4 == 3 or i == ETILES - 1:
                        last.then_inc(flipped, 1)


def mix_stage(nc, mem, w):
    with ExitStack() as ctx:
        sb = lambda n, s, d: ctx.enter_context(nc.sbuf_tensor(n, s, d))
        sem = ctx.enter_context(stage_semaphores(nc))
        bank, h, xk, ident = mem.bank, mem.h, mem.xk, mem.ident
        raw = [sb(f"raw_{n}", [P, HALVES, D], F32) for n in ("wk", "wv", "wo")]
        wq = sb("wq_sb", [P, HALVES, D], F32)
        wkv, woT = sb("wkv", [P, HALVES, 2 * D], F32), sb("woT", [P, HALVES, D], F32)
        w_mean = sb("w_mean", [P, HALVES, 2 * HEADS], F32)
        k_gain, k_shift = sb("k_gain", [P, HEAD], F32), sb("k_shift", [P, HEAD], F32)
        v_col = sb("v_gain_shift", [P, 2], F32)
        bo_row, ones_row = sb("bo_row", [1, D], F32), sb("ones_row", [1, P], F32)
        stats = sb("ln_stats", [P, TILES, 6], F32)
        mean, rstd, tmp = sb("ln_mean", [P, TILES], F32), sb("ln_rstd", [P, TILES], F32), sb("ln_tmp", [P, TILES], F32)
        xs, xT = sb("xs", [P, 4, D], F32), sb("xT", [P, 2, D], F32)
        sq, kvn = sb("sq", [P, 2, 2 * D], F32), sb("kvn", [P, 2, 2 * HALVES, P + 1], F32)
        hs = sb("head_var_rstd", [P, 4, 2 * HEADS], F32)
        V, K_COL = 200, 400
        sums, k_sum, k_row = sb("kv_sums", [P, K_COL + HALVES], F32), sb("k_sum_wide", [P, HALVES, P], F32), sb("k_part", [P, HALVES, P], F32)
        v_part = sb("v_part", [P, HALVES], F32)
        kvb, tq, m_sb = sb("kv_blocks", [P, HALVES, P], F32), sb("kv_wo", [P, HALVES, D], F32), sb("mix_w", [P, HALVES, D], F32)
        w_in, b_in, own, wT, wTd = sem("mixw_in"), sem("mixb_in"), sem("mix_own"), sem("mixw_T"), sem("mixw_Td")
        xs_ready, xs_flipped, xT_ready, kv_ps, sq_ready, own_tiles = (sem(n) for n in ("xs_ready", "xs_flipped", "xT_ready", "kv_ps", "sq_ready", "own_tiles"))
        kvn_ready, kv_added, zero_kv, k_sum_ready, k_sum_flipped = (sem(n) for n in ("kvn_ready", "kv_added", "zero_kv", "k_sum_ready", "k_sum_flipped"))
        kvb_ready, tq_ps, tq_ready, m_ps, m_ready, act_h = (sem(n) for n in ("kvb_ready", "tq_ps", "tq_ready", "m_ps", "m_ready", "act_h"))
        stats_done = sem("stats_done")
        var_ready, rstd_ready, head_var, head_rstd = (sem(n) for n in ("var_ready", "rstd_ready", "head_var", "head_rstd"))
        mixed, mix_read, xs2, fl2, xt2 = (sem(n) for n in ("mixed", "mix_read", "xs_again", "xs_flipped_again", "xT_again"))
        kv_bank = [bank[k] for k in (0, 1, 5, 6)]
        B_LOADS = 7

        def first_pass(eng, body):
            four_steps(eng, -3, TILES + 1, 6, body)

        def second_pass(eng, body):
            four_steps(eng, -2, TILES - 1, 4, body)

        with nc.Block() as block:
            @block.sync
            def _(sp):
                for t, n in zip(raw + [wq], ("wk", "wv", "wo", "wq")):
                    sp.dma_start(t[:], w[n].rearrange("(a p) d -> p a d", p=P)).then_inc(w_in, 16)
                sp.dma_start(k_gain[:], w["ln_k_g"].partition_broadcast(P)).then_inc(b_in, 16)
                sp.dma_start(k_shift[:], w["ln_k_b"].partition_broadcast(P)).then_inc(b_in, 16)
                for b in range(P // HEAD):
                    for k, n in enumerate(("ln_v_g", "ln_v_b")):
                        sp.dma_start(v_col[b * HEAD:(b + 1) * HEAD, k:k + 1], w[n].rearrange("(p o) -> p o", o=1)).then_inc(b_in, 16)
                sp.dma_start(bo_row[:], w["bo"].rearrange("(o d) -> o d", o=1)).then_inc(b_in, 16)
                sp.wait_ge(b_in, 16 * B_LOADS)

            @block.tensor
            def _(pe):
                pe.wait_ge(w_in, 64)
                for i, t in enumerate(raw):
                    for a in range(HALVES):
                        for b in range(HALVES):
                            last = nc.tensor.transpose(bank[i][:, (b * HALVES + a) * P:(b * HALVES + a + 1) * P], t[:, a, b * P:(b + 1) * P], ident)
                    last.then_inc(wT, 1)
                nc.tensor.matmul(bank[7][:, 0:K_COL + HALVES], mem.zeros[:, 0:P], mem.zeros[:, 0:K_COL + HALVES], start=True, stop=False, skip_group_check=True)
                pe.wait_ge(wTd, 4)

                def flip(u):
                    after(pe, xs_ready, u + 1)
                    after(pe, xT_ready, u + -1)
                    for a in range(HALVES):
                        last = nc.tensor.transpose(bank[3 + u.slot(2)][:, a * P:(a + 1) * P], xs[:, u.slot(4), a * P:(a + 1) * P], ident)
                    last.then_inc(xs_flipped, 1)

                def product(u):
                    after(pe, xT_ready, u + 1)
                    after(pe, kvn_ready, u + -3)
                    for a in range(HALVES):
                        last = nc.tensor.matmul(kv_bank[u.slot(4)][:, :], xT[:, u.slot(2), a * P:(a + 1) * P], wkv[:, a, :], start=(a == 0), stop=(a == HALVES - 1))
                    last.then_inc(kv_ps, 1)

                def add(u):
                    tail = u.n is None and u.c == FULL
                    r, j = TAIL if tail else P, u.slot(2)
                    after(pe, kvn_ready, u + 1)
                    for a in range(HALVES):
                        nc.tensor.matmul(bank[7][:, a * V:a * V + P + 1], kvn[0:r, j, HALVES + a, 0:P], kvn[0:r, j, a, :],
                                         start=False, stop=tail, skip_group_check=True)
                        last = nc.tensor.matmul(bank[7][:, K_COL + a:K_COL + a + 1], kvn[0:r, j, a, 0:P], kvn[0:r, j, a, P:P + 1],
                                                start=False, stop=tail, skip_group_check=True)
                    last.then_inc(kv_added, 1)

                pe.wait_ge(zero_kv, 3)

                def step(t):
                    if (t + 2).exists(TILES):
                        flip(t + 2)
                    if (t + 1).exists(TILES):
                        product(t + 1)
                    if (t + -2).exists(TILES):
                        add(t + -2)

                first_pass(pe, step)
                pe.wait_ge(k_sum_ready, 1)
                for a in range(HALVES):
                    last = nc.tensor.matmul(bank[2][:, a * P:(a + 1) * P], k_sum[:, a, :], ident, start=True, stop=True)
                last.then_inc(k_sum_flipped, 1)
                pe.wait_ge(kvb_ready, 1)
                for a in range(HALVES):
                    last = nc.tensor.matmul(bank[a][:, 0:D], kvb[:, a, :], woT[:, a, :], start=True, stop=True)
                last.then_inc(tq_ps, 1)
                pe.wait_ge(tq_ready, 1)
                for i in range(HALVES):
                    for a in range(HALVES):
                        last = nc.tensor.matmul(bank[3 + i][:, 0:D], wq[:, a, i * P:(i + 1) * P], tq[:, a, :], start=(a == 0), stop=(a == HALVES - 1))
                last.then_inc(m_ps, 1)
                pe.wait_ge(m_ready, 1)

                def flip_again(u):
                    after(pe, xs2, u + 1)
                    after(pe, xt2, u + -1)
                    for a in range(HALVES):
                        last = nc.tensor.transpose(bank[3 + u.slot(2)][:, a * P:(a + 1) * P], xs[:, u.slot(4), a * P:(a + 1) * P], ident)
                    last.then_inc(fl2, 1)

                def mix(u):
                    after(pe, xt2, u + 1)
                    after(pe, mix_read, u + -1)
                    to = bank[5 + u.slot(2)][:, 0:D]
                    nc.tensor.matmul(to, ones_row[:], bo_row[:], start=True, stop=False)
                    for a in range(HALVES):
                        last = nc.tensor.matmul(to, xT[:, u.slot(2), a * P:(a + 1) * P], m_sb[:, a, :], start=False, stop=(a == HALVES - 1))
                    last.then_inc(mixed, 1)

                def step(t):
                    if (t + 1).exists(TILES):
                        flip_again(t + 1)
                    if t.exists(TILES):
                        mix(t)

                second_pass(pe, step)

            @block.scalar
            def _(act):
                act.wait_ge(w_in, 64)
                act.wait_ge(b_in, 16 * B_LOADS)
                for c in range(EARLY_ZEROS, CHUNKS):
                    zero_chunk(act, mem, c)
                dest = mem.counts[CHUNKS * CELL_CHUNK:(CHUNKS + 1) * CELL_CHUNK].rearrange("(p s j) -> p s j", p=P, j=CHUNK)
                act.dma_start(dest[:, 0:28, 0:P], mem.zeros[:].rearrange("p (s j) -> p s j", j=P)).then_inc(mem.counts_zeroed, 16)
                act.dma_start(dest[:, 28:TILES, 0:P], mem.zeros[:, 0:21 * P].rearrange("p (s j) -> p s j", j=P)).then_inc(mem.counts_zeroed, 16)
                act.dma_start(mem.counts[DUMMY:CELLS].rearrange("(p s) -> p s", p=P), mem.zeros[:, 0:(CELLS - DUMMY) // P]).then_inc(mem.counts_zeroed, 16)

                def keep(u):
                    after(act, xs_ready, u + 1)
                    nc.scalar.copy(h[:, u.value(), :], xs[:, u.slot(4), :]).then_inc(act_h, 1)

                def flip_out(u):
                    after(act, xs_flipped, u + 1)
                    after(act, kv_ps, u + -1)
                    nc.scalar.copy(xT[:, u.slot(2), :], bank[3 + u.slot(2)][:, 0:D]).then_inc(xT_ready, 1)

                def square(u):
                    after(act, kv_ps, u + 1)
                    after(act, head_var, u + -1)
                    nc.scalar.activation(sq[:, u.slot(2), :], kv_bank[u.slot(4)][:, :], ACT.Square).then_inc(sq_ready, 1)

                def step(t):
                    if (t + 2).exists(TILES):
                        flip_out(t + 2)
                        keep(t + 2)
                    if (t + 1).exists(TILES):
                        square(t + 1)

                first_pass(act, step)
                act.wait_ge(act_h, TILES)
                act.wait_ge(m_ready, 1)

                def again(u):
                    after(act, fl2, u + -3)
                    nc.scalar.copy(xs[:, u.slot(4), :], h[:, u.value(), :]).then_inc(xs2, 1)

                def out(u):
                    after(act, fl2, u + 1)
                    after(act, mixed, u + -1)
                    nc.scalar.copy(xT[:, u.slot(2), :], bank[3 + u.slot(2)][:, 0:D]).then_inc(xt2, 1)

                def step(t):
                    if (t + 2).exists(TILES):
                        again(t + 2)
                    if (t + 1).exists(TILES):
                        out(t + 1)

                second_pass(act, step)

            @block.gpsimd
            def _(pool):
                nc.gpsimd.memset(kvn[:], 1.0).then_inc(zero_kv, 1)
                nc.gpsimd.memset(kvb[:], 0.0).then_inc(zero_kv, 1)
                nc.gpsimd.memset(ones_row[:], 1.0).then_inc(zero_kv, 1)
                pool.wait_ge(var_ready, 1)
                power(nc, mem, rstd[:], TILES).then_inc(rstd_ready, 1)

                def step(t):
                    if t.exists(TILES):
                        after(pool, head_var, t + 1)
                        power(nc, mem, hs[:, t.slot(4), :], 2 * HEADS).then_inc(head_rstd, 1)

                first_pass(pool, step)

            @block.vector
            def _(dve):
                step1 = Steps(dve, own)
                with dve.Fori(0, 7) as n:
                    for j in range(TILES // 7):
                        nc.vector.bn_stats(stats[:, n * (TILES // 7) + j, :], xk[:, n * (TILES // 7) + j, :]).then_inc(stats_done, 1)
                dve.wait_ge(stats_done, TILES)
                ln_rows(nc, dve, step1, stats, mean, rstd, tmp, var_ready, rstd_ready)
                for i in range(3):
                    dve.wait_ge(wT, i + 1)
                    dest = woT[:] if i == 2 else wkv[:, :, i * D:(i + 1) * D]
                    nc.vector.tensor_copy(dest, bank[i][:].rearrange("p (b c) -> p b c", b=HALVES)).then_inc(wTd, 1)
                dve.wait_ge(wTd, 3)
                heads = wkv[:].rearrange("p a (g d) -> p (a g) d", d=HEAD)
                means = w_mean[:].rearrange("p a g -> p (a g)")
                step1(nc.vector.tensor_reduce(means, heads, X_AXIS, ALU.add))
                step1(nc.vector.tensor_scalar(means, means, 1.0 / HEAD, None, ALU.mult))
                nc.vector.tensor_tensor(heads, heads, means.rearrange("p (g o) -> p g o", o=1).to_broadcast([P, HALVES * 2 * HEADS, HEAD]), ALU.subtract).then_inc(wTd, 1)
                dve.wait_ge(zero_kv, 2)
                own_step = StepCount(dve, own_tiles, 1, -3)

                def normalise(u):
                    t = u.value()
                    after(dve, xs_flipped, u + -3)
                    after(dve, act_h, u + -3)
                    nc.vector.tensor_scalar(xs[:, u.slot(4), :], xk[:, t, :], mean[:, bass.ds(t, 1)], rstd[:, bass.ds(t, 1)], ALU.subtract, ALU.mult).then_inc(xs_ready, 1)

                def scale(u):
                    after(dve, head_rstd, u + 1)
                    after(dve, kv_added, u + -1)
                    blocks = lambda ap: ap.rearrange("p (b h d) -> p b h d", b=2 * HALVES, d=HEAD)
                    factor = hs[:, u.slot(4), :].rearrange("p (b h o) -> p b h o", b=2 * HALVES, o=1).to_broadcast([P, 2 * HALVES, P // HEAD, HEAD])
                    nc.vector.tensor_tensor(kvn[:, u.slot(2), :, 0:P].rearrange("p b (h d) -> p b h d", d=HEAD),
                                            blocks(kv_bank[u.slot(4)][:, :]), factor, ALU.mult).then_inc(kvn_ready, 1)

                def step(t):
                    own_step.begin(t)
                    if (t + 3).exists(TILES):
                        normalise(t + 3)
                    v = hs[:, t.slot(4), :]
                    if t.exists(TILES):
                        after(dve, sq_ready, t + 1)
                        own_step.issue(nc.vector.tensor_reduce(v, sq[:, t.slot(2), :].rearrange("p (g d) -> p g d", d=HEAD), X_AXIS, ALU.add))
                    if (t + -1).exists(TILES):
                        scale(t + -1)
                    if t.exists(TILES):
                        dve.wait_ge(own_tiles, own_step.at + own_step.k)
                        nc.vector.tensor_scalar(v, v, 1.0 / HEAD, EPS, ALU.mult, ALU.add).then_inc(head_var, 1)
                    own_step.finish()

                first_pass(dve, step)
                dve.wait_ge(kv_added, TILES)
                dve.wait_ge(b_in, 16 * B_LOADS)
                step1(nc.vector.tensor_copy(sums[:], bank[7][:, 0:K_COL + HALVES]))
                nc.vector.tensor_copy(k_sum[:], sums[:, K_COL:K_COL + HALVES].rearrange("p (a o) -> p a o", o=1).to_broadcast([P, HALVES, P])).then_inc(k_sum_ready, 1)
                step1(nc.vector.tensor_scalar(v_part[:], v_col[:, 1:2].to_broadcast([P, HALVES]), float(N), None, ALU.mult))
                for a in range(HALVES):
                    last = nc.vector.scalar_tensor_tensor(out=v_part[:, a:a + 1], in0=sums[:, a * V + P:a * V + P + 1], scalar=v_col[:, 0:1], in1=v_part[:, a:a + 1], op0=ALU.mult, op1=ALU.add)
                step1(last)
                dve.wait_ge(k_sum_flipped, 1)
                blocks = [(slice(b * HEAD, (b + 1) * HEAD), a) for a in range(HALVES) for b in range(P // HEAD)]
                for r, a in blocks:
                    last = nc.vector.scalar_tensor_tensor(out=k_row[r, a, 0:HEAD], in0=bank[2][r, a * P + r.start:a * P + r.stop], scalar=v_col[r, 1:2], in1=k_gain[r, :], op0=ALU.mult, op1=ALU.mult)
                for r, a in blocks:
                    last = nc.vector.scalar_tensor_tensor(out=kvb[r, a, r], in0=sums[r, a * V + r.start:a * V + r.stop], scalar=v_col[r, 0:1], in1=k_gain[r, :], op0=ALU.mult, op1=ALU.mult)
                step1(last)
                for r, a in blocks:
                    last = nc.vector.scalar_tensor_tensor(out=kvb[r, a, r], in0=k_shift[r, :], scalar=v_part[r, a:a + 1], in1=kvb[r, a, r], op0=ALU.mult, op1=ALU.add)
                step1(last)
                for r, a in blocks:
                    last = nc.vector.tensor_tensor(kvb[r, a, r], kvb[r, a, r], k_row[r, a, 0:HEAD], ALU.add)
                step1(last)
                nc.vector.tensor_scalar(kvb[:], kvb[:], 1.0 / N, None, ALU.mult).then_inc(kvb_ready, 1)
                dve.wait_ge(tq_ps, 1)
                for a in range(HALVES):
                    last = nc.vector.tensor_copy(tq[:, a, :], bank[a][:, 0:D])
                last.then_inc(tq_ready, 1)
                dve.wait_ge(m_ps, 1)
                for a in range(HALVES):
                    last = nc.vector.tensor_copy(m_sb[:, a, :], bank[3 + a][:, 0:D])
                last.then_inc(m_ready, 1)

                def step(t):
                    if t.exists(TILES):
                        after(dve, mixed, t + 1)
                        x = xk[:, t.value(), :]
                        nc.vector.tensor_tensor(x, bank[5 + t.slot(2)][:, 0:D], x, ALU.add).then_inc(mix_read, 1)

                second_pass(dve, step)


def ln_rows(nc, dve, step, stats, mean, rstd, tmp, var_ready, rstd_ready, width=D):
    m_e, m_o, v_e, v_o = (stats[:, :, k] for k in (1, 4, 2, 5))
    step(nc.vector.tensor_tensor(mean[:], m_e, m_o, ALU.add))
    step(nc.vector.tensor_tensor(tmp[:], m_e, m_o, ALU.subtract))
    step(nc.vector.tensor_scalar(mean[:], mean[:], 0.5, None, ALU.mult))
    step(nc.vector.tensor_tensor(tmp[:], tmp[:], tmp[:], ALU.mult))
    step(nc.vector.tensor_tensor(rstd[:], v_e, v_o, ALU.add))
    step(nc.vector.tensor_scalar(tmp[:], tmp[:], 0.25, EPS, ALU.mult, ALU.add))
    nc.vector.scalar_tensor_tensor(out=rstd[:], in0=rstd[:], scalar=1.0 / width, in1=tmp[:], op0=ALU.mult, op1=ALU.add).then_inc(var_ready, 1)
    dve.wait_ge(rstd_ready, 1)


def power(nc, mem, ap, width):
    return nc.gpsimd.tensor_tensor(ap, ap, mem.minus_half[:].to_broadcast([P, width]), ALU.pow)


def scatter_stage(nc, mem):
    with ExitStack() as ctx:
        sb = lambda n, s, d: ctx.enter_context(nc.sbuf_tensor(n, s, d))
        sem = ctx.enter_context(stage_semaphores(nc))
        bank = mem.bank
        key_rows, key_bits = mem.key_rows, sb("key_bits", [P, GROUP * P], BF16)
        masked = sb("key_masked", [P, GROUP * P], I32)
        dup_mask = sb("dup_mask", [P, GROUP * P], BF16)
        equal = sb("equal", [P, 4, GROUP * P], BF16)
        value = sb("cell_value", [P, QUADS, GROUP], F32)
        earlier, is_dup = sb("earlier", [P, QUADS, GROUP], F32), sb("is_dup", [P, QUADS, GROUP], I32)
        cell = sb("cell_slot", [P, QUADS, GROUP], I32)
        lane, tile_no, bits_a, bits_b = (sb(n, [P, ETILES * P], F32 if n[:1] == "d" else I32) for n in ("dst_lane", "dst_tile", "bits_a", "bits_b"))
        iota = sb("iota_f", [P, P], F32)
        hot_lane, hot_tile = sb("hot_lane", [P, QUADS, GROUP, P], BF16), sb("hot_tile", [P, QUADS, GROUP, TILES], BF16)
        bias15 = sb("bias15", [P, 1], F32)
        keys_in, bits_ready, own, cleared = sem("keys_in"), sem("bits_ready"), sem("scatter_own"), sem("hot_cleared")
        dots, equals, dups, cells_set, retired, hots, hots_used = (
            sem(n) for n in ("dots", "equals", "dups", "cells_set", "groups_retired", "hots", "hots_used"))
        own_turns, own_turns_pool = sem("own_turns"), sem("own_turns_pool")
        deg_done, masked_done, xm_out = sem("deg_done"), sem("masked_done"), sem("xm_out")
        scattered = [sem(f"scattered{q}") for q in range(QUADS)]
        GQ = GROUP * QUADS
        pair = lambda k: mem.psum[:, 2 * (k % 3) * 512:(2 * (k % 3) + 2) * 512]
        pair_before = {k: k - 3 if k >= 3 else max(c for c in range(GQ) if c % 3 == k) - GQ for k in range(GQ)}
        deg_ps = bank[6][:, 0:TILES]

        with nc.Block() as block:
            @block.sync
            def _(sp):
                key_cells = mem.cells_dram[GQ * P:(ITERS + 1) * GQ * P].rearrange("(n m) -> n m", m=GQ * P)
                slots = mem.slot_rows.rearrange("(p t) d -> p (t d)", p=P)
                piece, m = 7 * CHUNK, FULL // 4
                stores = [(rows(mem.xm_dram)[:, k * m:(k + 1) * m, :], mem.xk[:, k * m:(k + 1) * m, :]) for k in range(4)]
                stores += [(mem.xm_dram[FULL * P:N, :], mem.xk[0:TAIL, FULL, :]), (mem.h[0:1, 0, :], mem.mask_embed.rearrange("(o d) -> o d", o=1))]
                stores += [(slots[:, k:min(k + piece, XT * D)], mem.zeros[:, 0:min(piece, XT * D - k)]) for k in range(0, XT * D, piece)]

                def next_keys(n):
                    sp.wait_ge(masked_done, n + 1 + CREDIT)
                    load_keys(sp, mem, key_cells[n], keys_in)

                for n, (to, what) in enumerate(stores):
                    next_keys(n)
                    sp.dma_start(to, what).then_inc(xm_out, 16)
                with sp.Fori(len(stores), ITERS) as n:
                    next_keys(n)
                sp.wait_ge(xm_out, 16 * len(stores))

            @block.gpsimd
            def _(pool):
                starts = list(range(QUADS)) + [QUADS - 1] * GROUP
                for k, q in enumerate(starts):
                    pool.dma_start(mem.starts_dram[k:k + 1], mem.zeros[0:1, k:k + 1]).then_inc(scattered[q], 16)
                pool.wait_ge(mem.counts_zeroed, 16 * (CHUNKS + 3))

                def add(index, amount, landed):
                    pool.indirect_dma_start(out=mem.counts_2d, out_offset=bass.IndirectOffsetOnAxis(ap=index, axis=0),
                                            in_=amount, in_offset=None, compute_op=ALU.add).then_inc(landed, 16)

                for q in range(QUADS):
                    pool.wait_ge(scattered[q], START + (LANDED if q == QUADS - 1 else 0))
                with pool.Fori(0, ITERS) as n:
                    for q in range(QUADS):
                        before = scattered[(q - 1) % QUADS]
                        pool.wait_ge(cells_set, QUADS * n + q + 1)
                        landed = pool.value_load(mem.landed_before[0:1, bass.ds(QUADS * n + q, 1)], min_val=START, max_val=START + LANDED)
                        pool.wait_ge(before, LANDED * n + landed)
                        pool.sem_inc(own_turns_pool, 1)
                        for i in range(1, GROUP):
                            add(cell[:, q, i:i + 1], value[:, q, i:i + 1], scattered[q])
                        pool.wait_ge(before, LANDED * n + (START + LANDED))
                        pool.sem_inc(retired, 1)
                        add(cell[:, q, 0:1], value[:, q, 0:1], scattered[q])
                pool.wait_ge(scattered[QUADS - 1], START + LANDED * (ITERS + 1))

            @block.tensor
            def _(pe):
                pe.sem_inc(dots, CREDIT)
                pe.sem_inc(hots_used, CREDIT)
                pe.wait_ge(cleared, 5)
                nc.tensor.matmul(deg_ps, hot_lane[:, 2, 0, :], hot_tile[:, 2, 0, :], start=True, stop=False, skip_group_check=True)

                def degrees(q):
                    for i in range(GROUP):
                        last = nc.tensor.matmul(deg_ps, hot_lane[:, q, i, :], hot_tile[:, q, i, :], start=False, stop=False, skip_group_check=True)
                    last.then_inc(hots_used, 1)

                with pe.Fori(0, ITERS) as n:
                    pe.wait_ge(bits_ready, n + 1)
                    for q in range(QUADS):
                        for i in range(GROUP):
                            k = GROUP * q + i
                            pe.wait_ge(equals, GQ * n + max(pair_before[k] + 1 + 2, 1))
                            qs = slice(32 * q, 32 * q + 32)
                            for b in range(2):
                                last = nc.tensor.matmul(pair(k)[:, b * 512:(b + 1) * 512], key_bits[qs, i * P:(i + 1) * P],
                                                        key_bits[qs, b * 512:(b + 1) * 512], start=True, stop=True)
                            last.then_inc(dots, 1)
                        pe.wait_ge(hots, QUADS * n + q + 1)
                        degrees((q + 2) % QUADS)
                pe.wait_ge(hots, QUADS * ITERS + 1)
                degrees(2)
                pe.wait_ge(hots, QUADS * ITERS + 2)
                degrees(3)
                nc.tensor.matmul(deg_ps, hot_lane[:, 3, 0, :], mem.zero_bf[:, 0:TILES], start=False, stop=True, skip_group_check=True).then_inc(deg_done, 1)

            @block.scalar
            def _(act):
                act.sem_inc(equals, 2)
                act.wait_ge(cleared, 5)
                with act.Fori(0, ITERS) as n:
                    for q in range(QUADS):
                        act.wait_ge(retired, QUADS * n + q + 1)
                        for i in range(GROUP):
                            k = GROUP * q + i
                            act.wait_ge(dots, GQ * n + k + 1 + CREDIT)
                            act.wait_ge(dups, GQ * n + k + 1)
                            nc.scalar.activation(equal[:, k % 4, :], pair(k), ACT.Relu, bias=bias15[:], scale=2.0,
                                                 accum_out=value[:, q, i:i + 1]).then_inc(equals, 1)

            @block.vector
            def _(dve):
                step = Steps(dve, own)
                dve.sem_inc(dups, 4)
                dve.sem_inc(retired, 3)
                dve.sem_inc(masked_done, CREDIT)
                dve.sem_inc(hots, 2)
                nc.vector.memset(hot_lane[:, 2:4], 0.0).then_inc(cleared, 1)
                nc.vector.memset(hot_tile[:, 2:4], 0.0).then_inc(cleared, 1)
                nc.vector.memset(mem.zero_bf[:], 0.0).then_inc(cleared, 1)
                nc.vector.memset(bias15[:], -15.0).then_inc(cleared, 1)
                step(nc.vector.tensor_copy(iota[:], mem.iota))
                nc.vector.tensor_copy(dup_mask[:], mem.dup_f[:]).then_inc(cleared, 1)
                cc = mem.cell_col
                nc.vector.tensor_scalar(bits_b[:], cc[:], PART_BITS, 3, ALU.logical_shift_right, ALU.bitwise_and)
                step(nc.vector.tensor_scalar(bits_a[:], cc[:], PART_BITS + TILE_BITS + COL_BITS, 2, ALU.logical_shift_right, ALU.logical_shift_left))
                step(nc.vector.tensor_tensor(bits_a[:], bits_a[:], bits_b[:], ALU.bitwise_or))
                step(nc.vector.tensor_copy(tile_no[:], bits_a[:]))
                step(nc.vector.tensor_scalar(bits_b[:], cc[:], P - 1, None, ALU.bitwise_and))
                step(nc.vector.tensor_copy(lane[:], bits_b[:]))

                def mask_bits():
                    nc.vector.tensor_tensor(masked[:], key_rows[:], mem.bit_mask.to_broadcast([P, GROUP * P]), ALU.bitwise_and).then_inc(masked_done, 1)

                def signs(n):
                    dve.wait_ge(masked_done, n + 1 + CREDIT)
                    nc.vector.tensor_scalar(key_bits[:], masked[:], 0.0, 0.5, ALU.not_equal, ALU.subtract).then_inc(bits_ready, 1)

                mask_bits()
                signs(0)
                with dve.Fori(0, ITERS) as n:
                    step.loop(n, QUADS)
                    for q in range(QUADS):
                        for i in range(GROUP):
                            k = GROUP * q + i
                            if k == GQ - 3:
                                dve.wait_ge(dots, GQ * n + (GQ + CREDIT))
                                signs(n + 1)
                            dve.wait_ge(equals, GQ * n + k + 3)
                            nc.vector.scalar_tensor_tensor(out=equal[:, k % 4, 0:(i + 1) * P], in0=equal[:, k % 4, 0:(i + 1) * P], scalar=1.0,
                                                           in1=dup_mask[:, (GROUP - 1 - i) * P:], op0=ALU.mult, op1=ALU.mult,
                                                           accum_out=earlier[:, q, i:i + 1]).then_inc(dups, 1)
                        cols = bass.ds(n * GQ + q * GROUP, GROUP)
                        dve.wait_ge(hots_used, QUADS * n + q + CREDIT)
                        flat = lambda t, m: t[:, cols].rearrange("p (g o) -> p g o", o=1).to_broadcast([P, GROUP, m])
                        row = lambda m: iota[:, 0:m].rearrange("p (o j) -> p o j", o=1).to_broadcast([P, GROUP, m])
                        nc.vector.tensor_tensor(hot_lane[:, q], flat(lane, P), row(P), ALU.is_equal)
                        nc.vector.tensor_tensor(hot_tile[:, q], flat(tile_no, TILES), row(TILES), ALU.is_equal).then_inc(hots, 1)
                        if q == 1:
                            dve.wait_ge(bits_ready, n + 1)
                            dve.wait_ge(keys_in, 64 * n + 64)
                            mask_bits()
                        dve.wait_ge(dups, GQ * n + GROUP * q + GROUP + 4)
                        dve.wait_ge(retired, QUADS * n + q + 1)
                        nc.vector.tensor_copy(cell[:, q, :], cc[:, cols])
                        step(nc.vector.tensor_scalar(is_dup[:, q, :], earlier[:, q, :], 0.0, None, ALU.is_gt))
                        dve.sem_inc(own_turns, 1)
                        nc.vector.copy_predicated(cell[:, q, :], is_dup[:, q, :], mem.dummy[:, q * GROUP:(q + 1) * GROUP]).then_inc(cells_set, 1)
                step.end(QUADS, ITERS)
                dve.wait_ge(deg_done, 1)
                step(nc.vector.tensor_scalar(mem.rdeg[:], deg_ps, 1.0, None, ALU.max))
                step(nc.vector.reduce_max(mem.top[:, 0:1], mem.rdeg[:], X_AXIS))
                nc.vector.reciprocal(mem.rdeg[:], mem.rdeg[:])


def largest_degree(nc, mem):
    with ExitStack() as ctx:
        flipped, topped = (ctx.enter_context(nc.semaphore(n)) for n in ("top_flipped", "topped"))
        with nc.Block() as block:
            @block.tensor
            def _(pe):
                nc.tensor.transpose(mem.bank[0][0:1, 0:P], mem.top[:, 0:1], mem.ident).then_inc(flipped, 1)

            @block.vector
            def _(dve):
                dve.wait_ge(flipped, 1)
                nc.vector.reduce_max(mem.top[0:1, 1:2], mem.bank[0][0:1, 0:P], X_AXIS).then_inc(topped, 1)
                dve.wait_ge(topped, 1)
                nc.vector.tensor_copy(mem.top_int[0:1, 0:1], mem.top[0:1, 1:2])


def gnn_layer(nc, mem, layer, g):
    with ExitStack() as ctx:
        sb = lambda n, s, d: ctx.enter_context(nc.sbuf_tensor(f"{n}_{layer}", s, d))
        new_sem = ctx.enter_context(stage_semaphores(nc))
        sem = lambda n: new_sem(f"{n}_{layer}")
        bank, h, hi, lo = mem.bank, mem.h, mem.h_hi, mem.h_lo
        wl, wr = sb("wl", [P, HALVES, D], F32), sb("wr", [P, HALVES, D], F32)
        bn = sb("bn_rows", [P, 5, D], F32)
        agg, own_rows, hT = sb("agg", [P, HALVES, CHUNK], F32), sb("own_rows", [P, 2, D], F32), sb("hT", [P, 2, HALVES, P], F32)
        z1s = sb("z1", [P, 2, D], F32)
        landed = [sem(f"counts_in{k}") for k in range(SLOTS)]
        split, batch_done, agg_out, copied, flipped, hT_ready = (sem(n) for n in ("h_split", "batch_done", "agg_out", "rows_copied", "rows_flipped", "hT_ready"))
        own, z_ps, z_read, w_in, w_ready, hi_done, z_own = (sem(n) for n in ("bn_own", "z_ps", "z_read", "w_in", "w_ready", "hi_done", "z_own"))

        with nc.Block() as block:
            @block.sync
            def _(sp):
                def load(n, b):
                    s0, m = batch_tiles(b)
                    k = b % SLOTS
                    if isinstance(n, int) and n == CHUNKS:
                        cells = mem.counts[CHUNKS * CELL_CHUNK:(CHUNKS + 1) * CELL_CHUNK].rearrange("(p s j) -> p s j", p=P, j=CHUNK)[:, s0:s0 + m, 0:P]
                        dest = mem.slot[k][:, 0:m * P].rearrange("p (s j) -> p s j", j=P)
                    else:
                        cells = mem.counts[0:CHUNKS * CELL_CHUNK].rearrange("(n p s) -> n p s", n=CHUNKS, p=P)[n][:, s0 * CHUNK:(s0 + m) * CHUNK]
                        dest = mem.slot[k][:, 0:m * CHUNK]
                    sp.dma_start(dest.bitcast(F32), cells).then_inc(landed[k], 16)

                for b in range(SLOTS):
                    load(0, b)
                sp.dma_start(wl[:], g["Wl"][layer].rearrange("(a p) d -> p a d", p=P)).then_inc(w_in, 16)
                sp.dma_start(wr[:], g["Wr"][layer].rearrange("(a p) d -> p a d", p=P)).then_inc(w_in, 16)
                for i, row in enumerate([mem.bn_rstd_dram[layer]] + [g[name][layer] for name in ("gamma", "b", "rmean", "beta")]):
                    sp.dma_start(bn[:, i, :], row.partition_broadcast(P)).then_inc(w_in, 16)

                def chunk_loads(n, following):
                    for b in range(BATCHES):
                        nxt = (n, b + SLOTS) if b + SLOTS < BATCHES else (following, b + SLOTS - BATCHES)
                        if nxt[0] is None:
                            continue
                        sp.wait_ge(batch_done, BATCHES * n + b + 1)
                        load(*nxt)

                with sp.Fori(0, CHUNKS - 1) as n:
                    chunk_loads(n, n + 1)
                chunk_loads(CHUNKS - 1, CHUNKS)
                chunk_loads(CHUNKS, None)

            @block.tensor
            def _(pe):
                pe.sem_inc(z_ps, CREDIT)
                def products(b, width, ty):
                    s0, m = batch_tiles(b)
                    for i in range(m):
                        s = s0 + i
                        right = mem.slot[b % SLOTS][:, i * width:(i + 1) * width]
                        for a in range(HALVES):
                            for part, left in enumerate((hi, lo)):
                                l = left[:, s, a * P:(a + 1) * P]
                                last = nc.tensor.matmul(bank[a][:, 0:width], l if ty is F32R else l.bitcast(F32), right if ty is F32R else right.bitcast(F32),
                                                        start=(s == 0 and part == 0), stop=(s == TILES - 1 and part == 1))
                    last.then_inc(batch_done, 1)

                def flip(n, i, per=4):
                    pe.wait_ge(copied, 4 * n + i + 1)
                    for a in range(HALVES):
                        last = nc.tensor.transpose(bank[2 + i % 2][:, a * P:(a + 1) * P], own_rows[:, i % 2, a * P:(a + 1) * P], mem.ident)
                    last.then_inc(flipped, 1)

                def project(n, i):
                    out = bank[4 + i % 2]
                    pe.wait_ge(hT_ready, 4 * n + i + 1)
                    pe.wait_ge(z_read, 4 * n + i + 1)
                    for a in range(HALVES):
                        nc.tensor.matmul(out[:, 0:D], hT[:, i % 2, a, :], wr[:, a, :], start=(a == 0), stop=(a == HALVES - 1))
                    pe.wait_ge(agg_out, HALVES * n + HALVES + CREDIT)
                    for a in range(HALVES):
                        last = nc.tensor.matmul(out[:, D:2 * D], agg[:, a, i * P:(i + 1) * P], wl[:, a, :], start=(a == 0), stop=(a == HALVES - 1))
                    last.then_inc(z_ps, 1)

                def chunk(n, width, ty):
                    tiles = width // P
                    pe.wait_ge(agg_out, HALVES * n + CREDIT)
                    for b in range(BATCHES):
                        s0, m = batch_tiles(b)
                        pe.wait_ge(split, (s0 + m - 1) // 7 + 1)
                        pe.wait_ge(landed[b % SLOTS], 16 * (BATCHES // SLOTS) * n + 16 * (b // SLOTS + 1))
                        if b == BATCHES - 1:
                            for i in range(min(2, tiles)):
                                flip(n, i)
                        products(b, width, ty)
                    pe.wait_ge(w_ready, 1)
                    for i in range(tiles):
                        project(n, i)
                        if i + 2 < tiles:
                            flip(n, i + 2)

                def everything(ty):
                    with pe.Fori(0, CHUNKS) as n:
                        chunk(n, CHUNK, ty)
                    chunk(CHUNKS, P, ty)

                with pe.register(f"top_{layer}") as top:
                    pe.reg_load(top, mem.top_int[0:1, 0:1])
                    with pe.If_lt(top, EXACT):
                        everything(F32R)
                    with pe.Else():
                        everything(F32)

            @block.scalar
            def _(act):
                def copy_rows(n, i, t):
                    nc.scalar.copy(own_rows[:, i % 2, :], h[:, t, :]).then_inc(copied, 1)

                def take(n, i):
                    act.wait_ge(flipped, 4 * n + i + 1)
                    nc.scalar.copy(hT[:, i % 2, :, :].rearrange("p a b -> p (a b)"), bank[2 + i % 2][:, 0:D]).then_inc(hT_ready, 1)

                def sums(n, width):
                    act.wait_ge(batch_done, BATCHES * n + BATCHES)
                    nc.scalar.copy(agg[:, 1, 0:width], bank[1][:, 0:width]).then_inc(agg_out, 1)

                with act.Fori(0, CHUNKS) as n:
                    for i in range(2):
                        act.wait_ge(z_ps, 4 * n + CREDIT)
                        copy_rows(n, i, 4 * n + i)
                    for i in range(2):
                        take(n, i)
                    sums(n, CHUNK)
                    for i in range(2, 4):
                        copy_rows(n, i, 4 * n + i)
                    for i in range(2, 4):
                        act.wait_ge(z_ps, 4 * n + i - 1 + CREDIT)
                        take(n, i)
                act.wait_ge(z_ps, 4 * CHUNKS + CREDIT)
                copy_rows(CHUNKS, 0, FULL)
                take(CHUNKS, 0)
                sums(CHUNKS, P)

            @block.vector
            def _(dve):
                step = Steps(dve, own)
                dve.sem_inc(z_read, 2)
                dve.sem_inc(agg_out, CREDIT)
                rstd, gamma, b, rmean, beta = (bn[:, i, :] for i in range(5))

                def fold():
                    dve.wait_ge(w_in, 16 * 7)
                    step(nc.vector.tensor_tensor(gamma, gamma, rstd, ALU.mult))
                    step(nc.vector.tensor_tensor(b, b, rmean, ALU.subtract))
                    step(nc.vector.tensor_tensor(b, b, gamma, ALU.mult))
                    step(nc.vector.tensor_tensor(b, b, beta, ALU.add))
                    for w in (wl, wr):
                        for a in range(HALVES):
                            last = nc.vector.tensor_tensor(w[:, a, :], w[:, a, :], gamma, ALU.mult)
                    last.then_inc(w_ready, 1)

                for k in range(7):
                    part = slice(7 * k, 7 * k + 7)
                    nc.vector.tensor_copy(hi[:, part, :], h[:, part, :]).then_inc(hi_done, 1)
                    dve.wait_ge(hi_done, k + 1)
                    nc.vector.tensor_tensor(lo[:, part, :], h[:, part, :], hi[:, part, :].bitcast(F32), ALU.subtract).then_inc(split, 1)
                    if k == 5:
                        fold()

                def sums(n, width):
                    dve.wait_ge(batch_done, BATCHES * n + BATCHES)
                    nc.vector.tensor_copy(agg[:, 0, 0:width], bank[0][:, 0:width]).then_inc(agg_out, 1)

                def finish(n, i, t):
                    z, z1 = bank[4 + i % 2], z1s[:, i % 2, :]
                    dve.wait_ge(z_ps, 4 * n + i + 1 + CREDIT)
                    step(nc.vector.tensor_tensor(z1, z[:, 0:D], b, ALU.add))
                    nc.vector.scalar_tensor_tensor(out=z1, in0=z[:, D:2 * D], scalar=mem.rdeg[:, bass.ds(t, 1)], in1=z1,
                                                   op0=ALU.mult, op1=ALU.add).then_inc(z_read, 1)
                    dve.wait_ge(z_read, 4 * n + i + 3)
                    if layer < LAYERS - 1:
                        nc.vector.scalar_tensor_tensor(out=h[:, t, :], in0=z1, scalar=0.0, in1=h[:, t, :], op0=ALU.max, op1=ALU.add)
                    else:
                        nc.vector.tensor_tensor(h[:, t, :], z1, h[:, t, :], ALU.add)

                with dve.Fori(0, CHUNKS) as n:
                    step.loop(n, 4)
                    sums(n, CHUNK)
                    for i in range(4):
                        finish(n, i, 4 * n + i)
                step.end(4, CHUNKS)
                sums(CHUNKS, P)
                finish(CHUNKS, 0, FULL)


def router_stage(nc, mem, f):
    with ExitStack() as ctx:
        sb = lambda n, s, d: ctx.enter_context(nc.sbuf_tensor(n, s, d))
        sem = ctx.enter_context(stage_semaphores(nc))
        bank, h = mem.bank, mem.h
        xm, stats, tmp = sb("xm_rows", [P, TILES, D], F32), sb("ffn_stats", [P, TILES, 6], F32), sb("ffn_tmp", [P, TILES], F32)
        gate_w, gate_b = sb("gate_w", [P, HALVES, E], F32), sb("gate_b", [P, E], F32)
        xs, xT = sb("router_rows", [P, 4, D], F32), sb("router_xT", [P, 2, D], F32)
        logits, score, onehot = (sb(n, [P, TILES, E], F32) for n in ("logits", "score", "onehot"))
        best = sb("best", [P, 3, TILES], F32)
        chosen = sb("chosen", [P, E, TILES, 2], BF16)
        tri, ones = sb("tri_bf", [P, P], BF16), sb("ones_bf", [P, P], BF16)
        rank = sb("rank_e", [P, E], F32)
        counts, counts_i, ends = sb("e_counts", [P, E], F32), sb("e_counts_i", [P, E], I32), sb("e_ends", [P, E], F32)
        room, w_e = xm[:].rearrange("p t d -> p (t d)"), E * 2 * TILES
        before, place, keep = (room[:, k * w_e:(k + 1) * w_e].rearrange("p (e m) -> p e m", e=E) for k in range(3))
        tile_e = room[0:1, 3 * w_e:3 * w_e + XT * E].rearrange("p (j e) -> p j e", e=E)
        one = sb("ones_e", [P, E], F32)
        slot_f, tile_f = sb("slot_f", [P, TILES, 2], F32), sb("tile_f", [1, XT], F32)
        gate_in, added, own, stats_done = (sem(n) for n in ("gate_in", "x2_done", "router_own", "ffn_stats_done"))
        var_ready, rstd_ready, xs_ready, flipped, xT_ready, logit_ps, logit_read = (
            sem(n) for n in ("ffn_var", "ffn_rstd", "router_xs", "router_flip", "router_xT_ready", "logit_ps", "logit_read"))
        cleared, chosen_ready, ranked, exp_in, exp_out = (sem(n) for n in ("router_cleared", "chosen_ready", "ranked", "exp_in", "exp_out"))

        def tiles(eng, body):
            four_steps(eng, -2, TILES, 4, body)

        parts = [(12 * k, 12) for k in range(4)] + [(FULL, 1)]

        with nc.Block() as block:
            @block.sync
            def _(sp):
                sp.wait_ge(cleared, 1)
                for k, (t, m) in enumerate(parts):
                    if t < FULL:
                        sp.dma_start(xm[:, t:t + m, :], rows(mem.xm_dram)[:, t:t + m, :]).then_inc(mem.part_in[k], 16)
                    else:
                        sp.dma_start(xm[0:TAIL, t, :], mem.xm_dram[FULL * P:N, :]).then_inc(mem.part_in[k], 16)
                sp.dma_start(gate_w[:], f["gate_w"].rearrange("(a p) e -> p a e", p=P)).then_inc(gate_in, 16)
                sp.dma_start(gate_b[:], f["gate_b"].partition_broadcast(P)).then_inc(gate_in, 16)
                for e in range(E):
                    sp.dma_start(mem.w1[:, e, :, :], f["w1"][e].rearrange("(a p) f -> p a f", p=P)).then_inc(mem.w1_in, 16)

            @block.tensor
            def _(pe):
                pe.wait_ge(gate_in, 32)

                def flip(u):
                    after(pe, xs_ready, u + 1)
                    after(pe, xT_ready, u + -1)
                    for a in range(HALVES):
                        last = nc.tensor.transpose(bank[u.slot(2)][:, a * P:(a + 1) * P], xs[:, u.slot(4), a * P:(a + 1) * P], mem.ident)
                    last.then_inc(flipped, 1)

                def product(u):
                    after(pe, xT_ready, u + 1)
                    after(pe, logit_read, u + -1)
                    for a in range(HALVES):
                        last = nc.tensor.matmul(bank[2 + u.slot(2)][:, 0:E], xT[:, u.slot(2), a * P:(a + 1) * P], gate_w[:, a, :], start=(a == 0), stop=(a == HALVES - 1))
                    last.then_inc(logit_ps, 1)

                def step(t):
                    if (t + 1).exists(TILES):
                        flip(t + 1)
                    if t.exists(TILES):
                        product(t)

                tiles(pe, step)
                pe.wait_ge(chosen_ready, 1)
                flat = chosen[:].rearrange("p e t k -> p (e t k)")
                w = E // 4 * 2 * TILES
                for c in range(4):
                    nc.tensor.matmul(bank[c][:, 0:w], tri[:], flat[:, c * w:(c + 1) * w], start=True, stop=True)
                    last = nc.tensor.matmul(bank[4 + c][:, 0:w], ones[:], flat[:, c * w:(c + 1) * w], start=True, stop=True)
                last.then_inc(ranked, 1)

            @block.scalar
            def _(act):
                def step(t):
                    u = t + 1
                    if u.exists(TILES):
                        after(act, flipped, u + 1)
                        after(act, logit_ps, u + -1)
                        nc.scalar.copy(xT[:, u.slot(2), :], bank[u.slot(2)][:, 0:D]).then_inc(xT_ready, 1)

                tiles(act, step)
                act.wait_ge(exp_in, 1)
                nc.scalar.activation(mem.gates[:, 1, :], mem.gates[:, 1, :], ACT.Exp).then_inc(exp_out, 1)

            @block.gpsimd
            def _(pool):
                nc.gpsimd.memset(xm[:, FULL, :], 0.0).then_inc(cleared, 1)
                nc.gpsimd.iota(mem.rank_i[:], pattern=[[-1, E]], base=E, channel_multiplier=0).then_inc(cleared, 1)
                pool.wait_ge(var_ready, 1)
                power(nc, mem, mem.rstd[:], TILES).then_inc(rstd_ready, 1)

            @block.vector
            def _(dve):
                step = Steps(dve, own)
                for k, (t, m) in enumerate(parts):
                    dve.wait_ge(mem.part_in[k], 16)
                    nc.vector.tensor_tensor(h[:, t:t + m, :], h[:, t:t + m, :], xm[:, t:t + m, :], ALU.add).then_inc(added, 1)
                dve.wait_ge(added, len(parts))
                with dve.Fori(0, 7) as n:
                    for j in range(TILES // 7):
                        nc.vector.bn_stats(stats[:, n * (TILES // 7) + j, :], h[:, n * (TILES // 7) + j, :]).then_inc(stats_done, 1)
                dve.wait_ge(stats_done, TILES)
                ln_rows(nc, dve, step, stats, mem.mean, mem.rstd, tmp, var_ready, rstd_ready)

                def route_step(t):
                    u, last = t + 2, t + -1
                    if u.exists(TILES):
                        after(dve, flipped, u + -3)
                        at = bass.ds(u.value(), 1)
                        nc.vector.tensor_scalar(xs[:, u.slot(4), :], h[:, u.value(), :], mem.mean[:, at], mem.rstd[:, at], ALU.subtract, ALU.mult).then_inc(xs_ready, 1)
                    if last.exists(TILES):
                        after(dve, logit_ps, last + 1)
                        nc.vector.tensor_tensor(logits[:, last.value(), :], bank[2 + last.slot(2)][:, 0:E], gate_b[:], ALU.add).then_inc(logit_read, 1)

                tiles(dve, route_step)
                dve.wait_ge(logit_read, TILES)
                dve.wait_ge(cleared, 2)
                step(nc.vector.tensor_copy(rank[:], mem.rank_i[:]))
                wide = lambda v: v.rearrange("p (t o) -> p t o", o=1).to_broadcast([P, TILES, E])
                each = rank[:].rearrange("p (o e) -> p o e", o=1).to_broadcast([P, TILES, E])
                for k in range(2):
                    step(nc.vector.reduce_max(best[:, k, :], logits[:], X_AXIS))
                    step(nc.vector.tensor_tensor(score[:], logits[:], wide(best[:, k, :]), ALU.is_equal))
                    step(nc.vector.tensor_tensor(score[:], score[:], each, ALU.mult))
                    step(nc.vector.reduce_max(best[:, 2, :], score[:], X_AXIS))
                    step(nc.vector.tensor_tensor(onehot[:], score[:], wide(best[:, 2, :]), ALU.is_equal))
                    step(nc.vector.tensor_scalar(onehot[:, FULL, :], onehot[:, FULL, :], mem.valid, None, ALU.mult))
                    step(nc.vector.tensor_copy(chosen[:, :, :, k], onehot[:].rearrange("p t e -> p e t")))
                    if k == 0:
                        step(nc.vector.scalar_tensor_tensor(out=logits[:], in0=onehot[:], scalar=-3e38, in1=logits[:], op0=ALU.mult, op1=ALU.add))
                        step(nc.vector.tensor_copy(mem.weigh[:], onehot[:]))
                nc.vector.tensor_copy(tri[:], mem.tri)
                nc.vector.memset(ones[:], 1.0).then_inc(chosen_ready, 1)
                nc.vector.tensor_tensor(mem.gates[:, 1, :], best[:, 1, :], best[:, 0, :], ALU.subtract).then_inc(exp_in, 1)
                dve.wait_ge(exp_out, 1)
                step(nc.vector.tensor_scalar(mem.gates[:, 0, :], mem.gates[:, 1, :], 1.0, None, ALU.add))
                step(nc.vector.reciprocal(mem.gates[:, 0, :], mem.gates[:, 0, :]))
                step(nc.vector.tensor_tensor(mem.gates[:, 1, :], mem.gates[:, 0, :], mem.gates[:, 1, :], ALU.mult))
                step(nc.vector.tensor_tensor(mem.weigh[:], mem.weigh[:], wide(mem.gates[:, 0, :]), ALU.mult))
                step(nc.vector.tensor_tensor(onehot[:], onehot[:], wide(mem.gates[:, 1, :]), ALU.mult))
                step(nc.vector.tensor_tensor(mem.weigh[:], mem.weigh[:], onehot[:], ALU.add))
                step(nc.vector.memset(keep, 1.0))
                step(nc.vector.memset(keep[:, :, 0:1], 0.0))
                step(nc.vector.memset(one[:], 1.0))
                dve.wait_ge(ranked, 1)
                w = E // 4 * 2 * TILES
                per = lambda c: mem.bank[c][:, 0:w].rearrange("p (e m) -> p e m", e=E // 4)
                for c in range(4):
                    nc.vector.tensor_reduce(counts[:, 4 * c:4 * c + 4], per(4 + c), X_AXIS, ALU.add)
                    last = nc.vector.tensor_copy(before[:, 4 * c:4 * c + 4, 1:], per(4 + c)[:, :, 0:2 * TILES - 1])
                step(last)
                step(nc.vector.tensor_scalar(counts_i[:], counts[:], float(P - 1), None, ALU.add))
                step(nc.vector.tensor_scalar(counts_i[:], counts_i[:], 7, 7, ALU.logical_shift_right, ALU.logical_shift_left))
                step(nc.vector.tensor_copy(counts[:], counts_i[:]))
                step(nc.vector.tensor_tensor_scan(ends[:], one[:], counts[:], 0.0, ALU.mult, ALU.add))
                step(nc.vector.tensor_tensor(before[:, :, 0], ends[:], counts[:], ALU.subtract))
                flat = lambda t: t.rearrange("p e m -> p (e m)")
                step(nc.vector.tensor_tensor_scan(flat(place), flat(keep), flat(before), 0.0, ALU.mult, ALU.add))
                for c in range(4):
                    last = nc.vector.tensor_tensor(place[:, 4 * c:4 * c + 4, :], place[:, 4 * c:4 * c + 4, :], per(c), ALU.add)
                step(last)
                step(nc.vector.tensor_tensor(place, place, chosen[:].rearrange("p e t k -> p e (t k)"), ALU.mult))
                step(nc.vector.tensor_reduce(slot_f[:].rearrange("p t k -> p (t k)"), place.rearrange("p e m -> p m e"), X_AXIS, ALU.add))
                step(nc.vector.tensor_copy(mem.slots[:], slot_f[:]))
                step(nc.vector.tensor_scalar(tile_f[:], mem.iota[0:1, 0:XT], float(P), None, ALU.mult))
                first = tile_f[:].rearrange("p (j o) -> p j o", o=1).to_broadcast([1, XT, E])
                last_of = ends[0:1, :].rearrange("p (o e) -> p o e", o=1).to_broadcast([1, XT, E])
                step(nc.vector.tensor_tensor(tile_e, first, last_of, ALU.is_ge))
                step(nc.vector.tensor_reduce(tile_f[:], tile_e, X_AXIS, ALU.add))
                step(nc.vector.tensor_scalar(mem.tile_expert[:], tile_f[:], float(E - 1), None, ALU.min))


def dispatch_stage(nc, mem, f):
    with ExitStack() as ctx:
        sb = lambda n, s, d: ctx.enter_context(nc.sbuf_tensor(n, s, d))
        sem = ctx.enter_context(stage_semaphores(nc))
        xs, where = sb("dispatch_rows", [P, 4, D], F32), sb("dispatch_slot", [P, 4, 2], I32)
        ready, turn = sem("dispatch_ready"), sem("dispatch_turn")
        sent = [sem(f"dispatch_sent{j}") for j in range(4)]
        with nc.Block() as block:
            @block.sync
            def _(sp):
                for e in range(E):
                    sp.dma_start(mem.w2[:, e, :, :], f["w2"][e].rearrange("(a p) f -> p a f", p=P)).then_inc(mem.w2_in, 16)
                sp.dma_start(mem.b1_rows[:], f["b1"].rearrange("e (a p) -> (e a) p", p=P)).then_inc(mem.b1_in, 16)

            @block.vector
            def _(dve):
                def prepare(u):
                    j, t = u.slot(4), u.value()
                    after(dve, sent[j], u, times=32, over=4)
                    nc.vector.tensor_scalar(xs[:, j, :], mem.h[:, t, :], mem.mean[:, bass.ds(t, 1)], mem.rstd[:, bass.ds(t, 1)], ALU.subtract, ALU.mult)
                    nc.vector.tensor_copy(where[:, j, :], mem.slots[:, t, :]).then_inc(ready, 1)

                four_steps(dve, 0, FULL, 4, prepare)

            @block.gpsimd
            def _(pool):
                def send(u):
                    j = u.slot(4)
                    r = TAIL if u.n is None and u.c == FULL else P
                    after(pool, ready, u + 1)
                    pool.sem_inc(turn, 1)
                    for k in range(2):
                        pool.indirect_dma_start(out=mem.slot_rows, out_offset=bass.IndirectOffsetOnAxis(ap=where[0:r, j, k:k + 1], axis=0),
                                                in_=xs[0:r, j, :], in_offset=None).then_inc(sent[j], 16)

                four_steps(pool, 0, FULL, 4, send)
                for j in range(4):
                    pool.wait_ge(sent[j], 32 * len(range(j, TILES, 4)))


def expert_stage(nc, mem):
    with ExitStack() as ctx:
        sb = lambda n, s, d: ctx.enter_context(nc.sbuf_tensor(n, s, d))
        sem = ctx.enter_context(stage_semaphores(nc))
        bank = mem.bank
        FT = FF // P
        xs, xT = sb("slot_x", [P, 4, D], F32), sb("slot_xT", [P, 2, D], F32)
        hid, hT, y = sb("hidden", [P, 2, FF], F32), sb("hidden_T", [P, 2, FT, P], F32), sb("slot_y", [P, 2, D], F32)
        x_in = [sem(f"slot_in{j}") for j in range(4)]
        y_out = [sem(f"slot_out{j}") for j in range(2)]
        flipped, xT_ready, hid_ps, hid_ready, hid_flip_a, hid_flip_b, hT_ready, y_ps, y_ready = (
            sem(n) for n in ("slot_flipped", "slot_xT_ready", "hid_ps", "hid_ready", "hid_flip_a", "hid_flip_b", "hT_ready_e", "y_ps", "y_ready"))
        b1_flipped, b1_ready, hid_last = sem("b1_flipped"), sem("b1_ready"), sem("hT_dve")
        load_v = mem.slot_rows.rearrange("(t p) d -> t p d", p=P)
        store_v = mem.slot_out.rearrange("(t p) d -> t p d", p=P)
        PEEL = 6

        def run(eng, body):
            four_steps(eng, -2, XT, PEEL, body)

        def expert_of(eng, u):
            return eng.value_load(mem.tile_expert[0:1, bass.ds(u.value(), 1)], min_val=0, max_val=E - 1)

        with nc.Block() as block:
            @block.sync
            def _(sp):
                for j in range(4):
                    sp.dma_start(xs[:, j, :], load_v[j]).then_inc(x_in[j], 16)

                def step(t):
                    if (t + 6).exists(XT) and (t + 2).exists(XT):
                        after(sp, flipped, t + 3)
                        j = (t + 6).slot(4)
                        sp.dma_start(xs[:, j, :], load_v[(t + 6).value()]).then_inc(x_in[j], 16)
                    if (t + -1).exists(XT):
                        after(sp, y_ready, t)
                        j = (t + -1).slot(2)
                        sp.dma_start(store_v[(t + -1).value()], y[:, j, :]).then_inc(y_out[j], 16)

                four_steps(sp, -2, XT, PEEL + 2, step)
                sp.wait_ge(y_out[0], 16 * ((XT + 1) // 2))
                sp.wait_ge(y_out[1], 16 * (XT // 2))

            @block.tensor
            def _(pe):
                pe.wait_ge(mem.b1_in, 16)
                nc.tensor.transpose(bank[7][:, 0:E * FT], mem.b1_rows[:], mem.ident[0:E * FT, 0:E * FT]).then_inc(b1_flipped, 1)
                pe.wait_ge(mem.w1_in, 16 * E)
                pe.wait_ge(mem.w2_in, 16 * E)
                w1 = mem.w1[:].rearrange("p e a f -> p e (a f)")
                w2 = mem.w2[:].rearrange("p e a f -> p e (a f)")

                def rows_flip(u):
                    after(pe, x_in[u.slot(4)], u + 4, times=16, over=4)
                    after(pe, xT_ready, u)
                    for a in range(HALVES):
                        last = nc.tensor.transpose(bank[0][:, a * P:(a + 1) * P], xs[:, u.slot(4), a * P:(a + 1) * P], mem.ident)
                    last.then_inc(flipped, 1)

                def first_product(u):
                    e = expert_of(pe, u)
                    after(pe, xT_ready, u + 1)
                    after(pe, hid_ready, u)
                    for a in range(HALVES):
                        last = nc.tensor.matmul(bank[1][:, :], xT[:, u.slot(2), a * P:(a + 1) * P], w1[:, e, a * FF:(a + 1) * FF], start=(a == 0), stop=(a == HALVES - 1))
                    last.then_inc(hid_ps, 1)

                def hidden_flip(u):
                    after(pe, hid_ready, u + 1)
                    after(pe, hT_ready, u)
                    after(pe, hid_last, u)
                    for k in range(FT):
                        last = nc.tensor.transpose(bank[2 + k // 2][:, (k % 2) * P:(k % 2 + 1) * P], hid[:, u.slot(2), k * P:(k + 1) * P], mem.ident)
                        if k % 2:
                            last.then_inc((hid_flip_a, hid_flip_b)[k // 2], 1)

                def second_product(u):
                    e = expert_of(pe, u)
                    after(pe, hT_ready, u + 1)
                    after(pe, hid_last, u + 1)
                    after(pe, y_ready, u + -1)
                    for k in range(FT):
                        last = nc.tensor.matmul(bank[4 + u.slot(2)][:, 0:D], hT[:, u.slot(2), k, :], w2[:, e, k * D:(k + 1) * D], start=(k == 0), stop=(k == FT - 1))
                    last.then_inc(y_ps, 1)

                def step(t):
                    if (t + 2).exists(XT):
                        rows_flip(t + 2)
                    if (t + 1).exists(XT):
                        first_product(t + 1)
                    if t.exists(XT):
                        hidden_flip(t)
                    if (t + -1).exists(XT):
                        second_product(t + -1)

                run(pe, step)

            @block.scalar
            def _(act):
                act.wait_ge(b1_ready, 1)

                def rows_out(u):
                    after(act, flipped, u + 1)
                    after(act, hid_ps, u + -1)
                    nc.scalar.copy(xT[:, u.slot(2), :], bank[0][:, 0:D]).then_inc(xT_ready, 1)

                def hidden_out(u):
                    e = expert_of(act, u)
                    after(act, hid_flip_a, u + 1)
                    after(act, y_ps, u + -1)
                    for k in range(FT // 2):
                        last = nc.scalar.activation(hT[:, u.slot(2), k, :], bank[2][:, k * P:(k + 1) * P], ACT.Relu, bias=mem.b1T[:, bass.ds(e * FT + k, 1)])
                    last.then_inc(hT_ready, 1)

                def result_out(u):
                    after(act, y_ps, u + 1)
                    after(act, y_out[u.slot(2)], u, times=16, over=2)
                    nc.scalar.copy(y[:, u.slot(2), :], bank[4 + u.slot(2)][:, 0:D]).then_inc(y_ready, 1)

                def step(t):
                    if (t + 2).exists(XT):
                        rows_out(t + 2)
                    if t.exists(XT):
                        hidden_out(t)
                    if (t + -1).exists(XT):
                        result_out(t + -1)

                run(act, step)

            @block.vector
            def _(dve):
                dve.wait_ge(b1_flipped, 1)
                nc.vector.tensor_copy(mem.b1T[:], bank[7][:, 0:E * FT]).then_inc(b1_ready, 1)
                dve.wait_ge(b1_ready, 1)

                def hidden_keep(u):
                    after(dve, hid_ps, u + 1)
                    after(dve, hid_flip_b, u + -1)
                    nc.vector.tensor_copy(hid[:, u.slot(2), :], bank[1][:, :]).then_inc(hid_ready, 1)

                def hidden_out(u):
                    e = expert_of(dve, u)
                    after(dve, hid_flip_b, u + 1)
                    after(dve, y_ps, u + -1)
                    for k in range(FT // 2, FT):
                        last = nc.vector.tensor_scalar(hT[:, u.slot(2), k, :], bank[3][:, (k % 2) * P:(k % 2 + 1) * P], mem.b1T[:, bass.ds(e * FT + k, 1)], 0.0, ALU.add, ALU.max)
                    last.then_inc(hid_last, 1)

                def step(t):
                    if (t + 1).exists(XT):
                        hidden_keep(t + 1)
                    if t.exists(XT):
                        hidden_out(t)

                run(dve, step)


def combine_stage(nc, mem, f, out):
    with ExitStack() as ctx:
        sb = lambda n, s, d: ctx.enter_context(nc.sbuf_tensor(n, s, d))
        sem = ctx.enter_context(stage_semaphores(nc))
        bank, h = mem.bank, mem.h
        gamma, beta, b2 = sb("ffn_gamma", [P, D], F32), sb("ffn_beta", [P, D], F32), sb("ffn_b2", [E, D], F32)
        rows_in, where = sb("gathered", [P, 4, 2, D], F32), sb("gather_slot", [P, 4, 2], I32)
        wrow, wT = sb("weigh_rows", [P, 4, E], F32), sb("weigh_T", [E, 2, P], F32)
        acc, norm, res = (sb(n, [P, 4, D], F32) for n in ("acc", "acc_norm", "res"))
        st, mv, offset = sb("acc_stats", [P, 2, 6], F32), sb("acc_mv", [P, 2, 2], F32), sb("minus_mean_rstd", [P, TILES], F32)
        in_b, where_ready, turn, weigh_ready, w_flipped, wT_ready, bias_ps = (
            sem(n) for n in ("ffn_rows_in", "where_ready", "gather_turn", "weigh_ready", "w_flipped", "wT_ready_c", "bias_ps"))
        own, var_ready, rstd_ready, res_ready, rows_done, aggr_turn, offset_ready, acc_set, scaled = (
            sem(n) for n in ("combine_own", "acc_var", "acc_rstd", "res_ready", "rows_done", "aggr_turn", "offset_ready", "acc_set", "out_scaled"))
        gathered = [sem(f"gathered{j}") for j in range(4)]
        stored = [sem(f"stored{j}") for j in range(4)]
        FIRST, PEEL = -3, 8

        def run(eng, body):
            four_steps(eng, FIRST, TILES + 1, PEEL, body)

        with nc.Block() as block:
            @block.sync
            def _(sp):
                sp.dma_start(gamma[:], f["gamma"].partition_broadcast(P)).then_inc(in_b, 16)
                sp.dma_start(beta[:], f["beta"].partition_broadcast(P)).then_inc(in_b, 16)
                sp.dma_start(b2[:], f["b2"]).then_inc(in_b, 16)
                out_v = out[0:FULL * P, :].rearrange("(t p) d -> t p d", p=P)

                def step(t):
                    u = t + -2
                    if not u.exists(TILES):
                        return
                    after(sp, res_ready, u + 1)
                    if u.n is None and u.c == FULL:
                        sp.dma_start(out[FULL * P:N, :], res[0:TAIL, u.slot(4), :]).then_inc(stored[u.slot(4)], 16)
                    else:
                        sp.dma_start(out_v[u.value()], res[:, u.slot(4), :]).then_inc(stored[u.slot(4)], 16)

                run(sp, step)
                for j in range(4):
                    sp.wait_ge(stored[j], 16 * len(range(j, TILES, 4)))

            @block.gpsimd
            def _(pool):
                def gather(u):
                    j = u.slot(4)
                    r = TAIL if u.n is None and u.c == FULL else P
                    after(pool, where_ready, u + 1)
                    pool.sem_inc(turn, 1)
                    for k in range(2):
                        pool.indirect_dma_start(out=rows_in[0:r, j, k, :], out_offset=None, in_=mem.slot_out,
                                                in_offset=bass.IndirectOffsetOnAxis(ap=where[0:r, j, k:k + 1], axis=0)).then_inc(gathered[j], 16)

                def step(t):
                    if (t + 3).exists(TILES):
                        gather(t + 3)
                    if t.exists(TILES):
                        after(pool, var_ready, t + 1)
                        power(nc, mem, mv[:, t.slot(2), 1:2], 1).then_inc(rstd_ready, 1)
                    u = t + -2
                    if u.exists(TILES):
                        after(pool, scaled, u + 1)
                        after(pool, stored[u.slot(4)], u, times=16, over=4)
                        nc.gpsimd.tensor_tensor(res[:, u.slot(4), :], norm[:, u.slot(4), :], h[:, u.value(), :], ALU.add).then_inc(res_ready, 1)

                run(pool, step)

            @block.tensor
            def _(pe):
                pe.wait_ge(in_b, 48)

                def flip(u):
                    after(pe, weigh_ready, u + 1)
                    after(pe, wT_ready, u + -1)
                    nc.tensor.transpose(bank[u.slot(2)][0:E, 0:P], wrow[:, u.slot(4), :], mem.ident).then_inc(w_flipped, 1)

                def bias(u):
                    after(pe, wT_ready, u + 1)
                    after(pe, rows_done, u + -1)
                    nc.tensor.matmul(bank[2 + u.slot(2)][:, 0:D], wT[:, u.slot(2), :], b2[:], start=True, stop=True).then_inc(bias_ps, 1)

                def step(t):
                    if (t + 2).exists(TILES):
                        flip(t + 2)
                    if (t + 1).exists(TILES):
                        bias(t + 1)

                run(pe, step)

            @block.scalar
            def _(act):
                act.wait_ge(offset_ready, 1)

                def step(t):
                    u = t + 2
                    if not u.exists(TILES):
                        return
                    after(act, res_ready, u + -3)
                    nc.scalar.activation(acc[:, u.slot(4), :], h[:, u.value(), :], ACT.Identity, scale=mem.rstd[:, bass.ds(u.value(), 1)],
                                         bias=offset[:, bass.ds(u.value(), 1)]).then_inc(acc_set, 1)
                    after(act, w_flipped, u + 1)
                    after(act, bias_ps, u + -1)
                    nc.scalar.copy(wT[:, u.slot(2), :], bank[u.slot(2)][0:E, 0:P]).then_inc(wT_ready, 1)

                run(act, step)

            @block.vector
            def _(dve):
                nc.vector.scalar_tensor_tensor(out=offset[:], in0=mem.mean[:], scalar=-1.0, in1=mem.rstd[:], op0=ALU.mult, op1=ALU.mult).then_inc(offset_ready, 1)
                own_step = StepCount(dve, own, 6, FIRST)
                dve.wait_ge(in_b, 48)

                def ask(u):
                    t = u.value()
                    after(dve, w_flipped, u + -3)
                    nc.vector.tensor_copy(wrow[:, u.slot(4), :], mem.weigh[:, t, :]).then_inc(weigh_ready, 1)
                    nc.vector.tensor_copy(where[:, u.slot(4), :], mem.slots[:, t, :]).then_inc(where_ready, 1)

                def step(t):
                    own_step.begin(t)
                    if (t + 3).exists(TILES):
                        ask(t + 3)
                    u, now, before = t + -1, t.exists(TILES), (t + -1).exists(TILES)
                    a, b = acc[:, t.slot(4), :], norm[:, u.slot(4), :]
                    m, old = mv[:, t.slot(2), :], mv[:, u.slot(2), :]

                    def add(k):
                        return nc.vector.scalar_tensor_tensor(out=a, in0=rows_in[:, t.slot(4), k, :], scalar=mem.gates[:, k, bass.ds(t.value(), 1)],
                                                              in1=a, op0=ALU.mult, op1=ALU.add)

                    if now:
                        after(dve, acc_set, t + 1)
                        after(dve, gathered[t.slot(4)], t + 4, times=32, over=4)
                        own_step.issue(add(0))
                    if before:
                        after(dve, rstd_ready, u + 1)
                        after(dve, res_ready, u + -3)
                        own_step(nc.vector.tensor_scalar(b, acc[:, u.slot(4), :], old[:, 0:1], old[:, 1:2], ALU.subtract, ALU.mult))
                    if now:
                        if not before:
                            own_step.eng.wait_ge(own, own_step.at + own_step.k)
                        own_step.issue(add(1))
                    if before:
                        own_step(nc.vector.tensor_tensor(b, b, gamma[:], ALU.mult))
                    if now:
                        if not before:
                            own_step.eng.wait_ge(own, own_step.at + own_step.k)
                        after(dve, bias_ps, t + 1)
                        nc.vector.tensor_tensor(a, a, bank[2 + t.slot(2)][:, 0:D], ALU.add).then_inc(rows_done, 1)
                    if before:
                        nc.vector.tensor_tensor(b, b, beta[:], ALU.add).then_inc(scaled, 1)
                    if now:
                        after(dve, rows_done, t + 1)
                        own_step.issue(nc.vector.bn_stats(st[:, t.slot(2), :], a))
                    if now:
                        dve.wait_ge(own, own_step.at + own_step.k)
                        dve.sem_inc(aggr_turn, 1)
                        own_step(nc.vector.bn_aggr(m, st[:, t.slot(2), :]))
                        nc.vector.tensor_scalar(m[:, 1:2], m[:, 1:2], EPS, None, ALU.add).then_inc(var_ready, 1)
                    own_step.finish()

                run(dve, step)


class Memory:
    pass


def program(nc, a, out):
    mem = Memory()
    with ExitStack() as ctx:
        sb = lambda n, s, d: ctx.enter_context(nc.sbuf_tensor(n, s, d))
        mem.psum = ctx.enter_context(nc.psum_tensor("psum", [P, 8 * 512], F32))
        mem.bank = [mem.psum[:, k * 512:(k + 1) * 512] for k in range(8)]
        mem.h = sb("h", [P, TILES, D], F32)
        mem.cf = sb("const_f", [P, 3 * P + 1], F32)
        mem.ident, mem.iota, mem.tri = (mem.cf[:, k * P:(k + 1) * P] for k in range(3))
        mem.minus_half = sb("minus_half", [P, 1], F32)
        mem.valid = mem.cf[:, 3 * P:3 * P + 1]
        mem.rdeg, mem.top, mem.top_int = sb("rdeg", [P, TILES], F32), sb("top", [P, 2], F32), sb("top_int", [P, 1], I32)
        mem.x, mem.mask_embed, mem.cf_dram, mem.ci_dram = a["x"], a["L0_gnn_mask_embed"], a["const_f"][:, 0:3 * P + 1], a["const_i"]
        mem.counts_2d = nc.dram_tensor("counts", [CELLS, 1], F32).ap()
        mem.counts = mem.counts_2d.rearrange("n o -> (n o)")
        mem.cells_dram = nc.dram_tensor("cells", [ETILES * P * P], I32).ap()
        mem.waits_dram = nc.dram_tensor("landed_before_rows", [ETILES * P // GROUP], I32).ap()
        mem.bn_rstd_dram = nc.dram_tensor("bn_rstd", [LAYERS, D], F32).ap()
        mem.starts_dram = nc.dram_tensor("starts", [QUADS + GROUP], F32).ap()
        mem.slot_rows = nc.dram_tensor("slot_rows", [XT * P, D], F32).ap()
        mem.slot_out = nc.dram_tensor("slot_out", [XT * P, D], F32).ap()
        mem.xm_dram = nc.dram_tensor("x_mix", [N, D], F32).ap()
        mem.counts_zeroed = ctx.enter_context(nc.semaphore("counts_zeroed"))

        with ExitStack() as early:
            sbe = lambda n, s, d: early.enter_context(nc.sbuf_tensor(n, s, d))
            mem.xk = sbe("x_keep", [P, TILES, D], F32)
            mem.ci = sbe("const_i", [P, 1 + QUADS * GROUP + 2 * P], I32)
            mem.bit_mask, mem.dummy = mem.ci[:, 0:1], mem.ci[:, 1:1 + QUADS * GROUP]
            mem.pad_and, mem.pad_or = (mem.ci[:, 1 + QUADS * GROUP + k * P:1 + QUADS * GROUP + (k + 1) * P] for k in range(2))
            mem.landed_before = sbe("landed_before", [1, ETILES * P // GROUP], I32)
            mem.zeros = sbe("zeros", [P, 7 * CHUNK], F32)
            mem.zero_bf = sbe("zero_bf", [P, P], BF16)
            mem.dup_f = sbe("dup_mask_f", [P, GROUP * P], F32)
            mem.key_rows = sbe("key_rows", [P, GROUP * P], I32)
            mem.cell_col = sbe("cell_col", [P, ETILES * P], I32)
            mem.dup_mask_dram = a["const_f"][:, 3 * P + 1:]
            index_stage(nc, mem, a["src"], a["dst"], a["L0_gnn_rvar"])
            mix_stage(nc, mem, {k: a["L0_mix_" + k] for k in ("wq", "wk", "wv", "wo", "bo", "ln_k_g", "ln_k_b", "ln_v_g", "ln_v_b")})
            scatter_stage(nc, mem)
        largest_degree(nc, mem)
        with ExitStack() as mid:
            sbm = lambda n, s, d: mid.enter_context(nc.sbuf_tensor(n, s, d))
            mem.h_hi, mem.h_lo = (sbm(n, [P, TILES, D], F32R) for n in ("h_hi", "h_lo"))
            mem.slot = [sbm(f"counts_slot{k}", [P, 5 * CHUNK], F32R) for k in range(SLOTS)]
            for layer in range(LAYERS):
                gnn_layer(nc, mem, layer, {k: a["L0_gnn_" + k] for k in ("Wl", "Wr", "gamma", "b", "rmean", "beta")})
        with ExitStack() as late:
            sbl = lambda n, s, d: late.enter_context(nc.sbuf_tensor(n, s, d))
            seml = lambda n: late.enter_context(nc.semaphore(n))
            mem.w1 = sbl("w1", [P, E, HALVES, FF], F32)
            mem.mean, mem.rstd = sbl("ffn_mean", [P, TILES], F32), sbl("ffn_rstd", [P, TILES], F32)
            mem.gates, mem.weigh, mem.slots = sbl("gates", [P, 2, TILES], F32), sbl("weigh", [P, TILES, E], F32), sbl("slots", [P, TILES, 2], I32)
            mem.tile_expert, mem.rank_i = sbl("tile_expert", [1, XT], I32), sbl("rank_i", [P, E], I32)
            mem.part_in = [seml(f"xm_in{k}") for k in range(5)]
            mem.w1_in, mem.w2_in, mem.b1_in = seml("w1_in"), seml("w2_in"), seml("b1_in")
            f = {k: a["L0_ffn_" + k] for k in ("gate_w", "gate_b", "w1", "b1", "w2", "b2", "gamma", "beta")}
            router_stage(nc, mem, f)
            with ExitStack() as experts:
                sbx = lambda n, s, d: experts.enter_context(nc.sbuf_tensor(n, s, d))
                mem.w2 = sbx("w2", [P, E, FF // P, D], F32)
                mem.b1_rows, mem.b1T = sbx("b1_rows", [E * FF // P, P], F32), sbx("b1T", [P, E * FF // P], F32)
                dispatch_stage(nc, mem, f)
                expert_stage(nc, mem)
            combine_stage(nc, mem, f, out)


INPUTS = ["x", "src", "dst"] + ["L0_gnn_" + k for k in ("mask_embed", "Wl", "Wr", "b", "gamma", "beta", "rmean", "rvar")] \
    + ["L0_mix_" + k for k in ("wq", "wk", "wv", "wo", "bo", "ln_k_g", "ln_k_b", "ln_v_g", "ln_v_b")] \
    + ["L0_ffn_" + k for k in ("gate_w", "gate_b", "w1", "b1", "w2", "b2", "gamma", "beta")]


def constants(np):
    p = np.arange(P)
    ident = np.eye(P, dtype=np.float32)
    iota = np.broadcast_to(p.astype(np.float32), (P, P))
    tri = (p[:, None] < p[None, :]).astype(np.float32)
    dup = np.concatenate([np.ones((P, (GROUP - 1) * P), np.float32), tri.T], axis=1)
    const_f = np.ascontiguousarray(np.concatenate([ident, iota, tri, (p < TAIL)[:, None], dup], axis=1), dtype=np.float32)
    bit = (np.uint32(1) << (p % 32).astype(np.uint32)).view(np.int32)[:, None]
    dummy = DUMMY + np.arange(QUADS * GROUP)[None, :] * P + p[:, None]
    edge = (ETILES - 1) * P * P + np.arange(P * P).reshape(P, P)
    pad = edge >= EDGES
    pad_and = np.where(pad, 0, -1)
    pad_or = np.where(pad, (DUMMY_PAD + (edge - EDGES) % (GROUP * P)) | TAG, 0)
    const_i = np.ascontiguousarray(np.concatenate([bit, dummy, pad_and, pad_or], axis=1).astype(np.int32))
    return {"const_f": const_f, "const_i": const_i}


def kernel(**inputs):
    import numpy as np
    import concourse.bacc as bacc
    from concourse.bass_utils import run_bass_kernel_spmd

    nc = bacc.Bacc("TRN2", target_bir_lowering=False, num_devices=1)
    arrays, a = {}, {}
    for name, value in list({k: inputs[k] for k in INPUTS}.items()) + list(constants(np).items()):
        value = np.ascontiguousarray(value)
        arrays[f"in_{name}"] = value
        a[name] = nc.dram_tensor(f"in_{name}", value.shape, mybir.dt.from_np(value.dtype), kind="ExternalInput").ap()
    out = nc.dram_tensor("out_rows", (N, D), F32, kind="ExternalOutput").ap()
    program(nc, a, out)
    return run_bass_kernel_spmd(nc, [arrays], core_ids=[0]).results[0]["out_rows"]
```
